# Optimizing a Trainium2 kernel written in Bass

```python
import numpy as np
import jax
import jax.numpy as jnp

def _softmax(x, axis=-1):
    return jax.nn.softmax(x, axis=axis)

def _gelu(x):
    return jax.nn.gelu(x, approximate=True)

def _silu(x):
    return jax.nn.silu(x)

def _sigmoid(x):
    return jax.nn.sigmoid(x)

def _layernorm(x, axis=-1, eps=1e-05):
    m = jnp.mean(x, axis=axis, keepdims=True)
    v = jnp.var(x, axis=axis, keepdims=True)
    return (x - m) / jnp.sqrt(v + eps)

def _scatter_add(tgt, idx, src, axis=0):
    return tgt.at[idx].add(src)

def _segment_sum(src, seg, n):
    return jax.ops.segment_sum(src, seg, n)
kernel_name = 'mk_hybrid_d1_jaxref_r8_470991'

def setup_inputs(seed: int=0):
    np.random.seed(seed)
    _w = jnp.asarray

    def _L0_attn_a_setup():
        import jax, jax.numpy as jnp
        import numpy as np
        B, S, DM = (2, 256, 256)
        H, KVH, HD = (16, 4, 128)
        REP = H // KVH
        ROPE_BASE = 10000.0
        EPS = 1e-06

        def _rope_tables(seq_len, dim):
            inv_freq = 1.0 / ROPE_BASE ** (jnp.arange(0, dim, 2, dtype=jnp.float32) / dim)
            t = jnp.arange(seq_len, dtype=jnp.float32)
            freqs = jnp.outer(t, inv_freq)
            emb = jnp.concatenate([freqs, freqs], -1)
            return (jnp.cos(emb), jnp.sin(emb))

        def _rotate_half(x):
            d = x.shape[-1] // 2
            return jnp.concatenate([-x[..., d:], x[..., :d]], axis=-1)
        key = jax.random.key(seed)
        k0, k1, k2, k3, k4 = jax.random.split(key, 5)
        w = lambda k, o, i: jax.random.normal(k, (o, i), jnp.float32) * (1.0 / np.sqrt(i))
        return {'x': jax.random.normal(k0, (B, S, DM), jnp.float32), 'Wq': w(k1, H * HD, DM), 'Wk': w(k2, KVH * HD, DM), 'Wv': w(k3, KVH * HD, DM), 'Wo': w(k4, DM, H * HD)}
    _L0_attn_a_in = _L0_attn_a_setup()

    def _L0_attn_b_setup():
        import jax, jax.numpy as jnp
        import numpy as np
        import math
        FRAME_SIZE = 72
        GAMMA = 0.5
        NUM_HEADS = 32

        def rotate_half(x):
            x1, x2 = jnp.split(x, 2, axis=-1)
            return jnp.concatenate([-x2, x1], axis=-1)

        def apply_rope(x, freqs):
            return x * jnp.cos(freqs) + rotate_half(x) * jnp.sin(freqs)

        def rope_freqs(length, dim):
            theta = 10000.0 ** (-jnp.arange(0, dim, 2, dtype=jnp.float32) / dim)
            f = jnp.arange(length, dtype=jnp.float32)[:, None] * theta[None, :]
            return jnp.concatenate([f, f], axis=-1)
        key = jax.random.key(seed)
        ks = jax.random.split(key, 9)
        B, T, C = (2, 256, 256)
        s = 0.02
        return {'hidden_states': jax.random.normal(ks[0], (B, T, C), jnp.float32), 'Wq': jax.random.normal(ks[1], (C, C), jnp.float32) * s, 'bq': jnp.zeros((C,), jnp.float32), 'Wk': jax.random.normal(ks[2], (C, C), jnp.float32) * s, 'bk': jnp.zeros((C,), jnp.float32), 'Wv': jax.random.normal(ks[3], (C, C), jnp.float32) * s, 'bv': jnp.zeros((C,), jnp.float32), 'Wo': jax.random.normal(ks[4], (C, C), jnp.float32) * s, 'bo': jnp.zeros((C,), jnp.float32)}
    _L0_attn_b_in = _L0_attn_b_setup()

    def _L0_ffn_setup():
        import jax, jax.numpy as jnp
        import numpy as np
        B, S, H, I, E, F, K, R, TOPK = (1, 128, 256, 176, 64, 8, 8, 8, 6)
        ISH = 2 * I

        def _fused_linear(x, W, qa, qb, scale, w):
            out = x @ W.T
            a = jnp.einsum('th,krh->tkr', x, qa)
            b = jnp.einsum('tkr,khr->tkh', a, qb)
            mix = jnp.einsum('tkh,tk->th', b, w)
            return out + scale[None, :] * mix

        def _moe_forward(hidden_states, gate_weight, inv_mapping, mask_up_W, gate_W, gate_qa, gate_qb, gate_scale, up_W, up_qa, up_qb, up_scale, down_W, down_qa, down_qb, down_scale, sh_gate_W, sh_up_W, sh_down_W):
            b, s, h = hidden_states.shape
            x = hidden_states.reshape(-1, h)
            T = x.shape[0]
            scores = jax.nn.softmax(x @ gate_weight.T, axis=-1)
            topk_w, topk_idx = jax.lax.top_k(scores, TOPK)
            w_dense = jnp.zeros((T, E), x.dtype).at[jnp.arange(T)[:, None], topk_idx].add(topk_w)
            flat = w_dense[:, inv_mapping]
            scalar = flat.sum(-1)
            soft = jax.nn.softmax(jnp.where(flat == 0, -1000000000.0, flat), axis=-1)

            def expert(muW, gW, gqa, gqb, gs, uW, uqa, uqb, us, dW, dqa, dqb, ds, w):
                xe = x + w @ muW.T
                gate = jax.nn.silu(_fused_linear(xe, gW, gqa, gqb, gs, w))
                up = _fused_linear(xe, uW, uqa, uqb, us, w)
                return _fused_linear(gate * up, dW, dqa, dqb, ds, w)
            outs = jax.vmap(expert, in_axes=(0,) * 13 + (1,))(mask_up_W, gate_W, gate_qa, gate_qb, gate_scale, up_W, up_qa, up_qb, up_scale, down_W, down_qa, down_qb, down_scale, soft)
            y = jnp.einsum('fth,tf->th', outs, scalar).reshape(b, s, h)
            sh = jax.nn.silu(hidden_states @ sh_gate_W.T) * (hidden_states @ sh_up_W.T) @ sh_down_W.T
            return y + sh
        key = jax.random.key(seed)
        ks = jax.random.split(key, 20)
        g = lambda k, shape, s=0.02: jax.random.normal(k, shape, jnp.float32) * s
        return {'hidden_states': jax.random.normal(ks[0], (B, S, H), jnp.float32), 'gate_weight': g(ks[1], (E, H)), 'inv_mapping': jnp.arange(E, dtype=jnp.int32).reshape(F, K), 'mask_up_W': g(ks[2], (F, H, K)), 'gate_W': g(ks[3], (F, I, H)), 'gate_qa': g(ks[4], (F, K, R, H)), 'gate_qb': g(ks[5], (F, K, I, R)), 'gate_scale': jnp.full((F, I), 0.1, jnp.float32), 'up_W': g(ks[6], (F, I, H)), 'up_qa': g(ks[7], (F, K, R, H)), 'up_qb': g(ks[8], (F, K, I, R)), 'up_scale': jnp.full((F, I), 0.1, jnp.float32), 'down_W': g(ks[9], (F, H, I)), 'down_qa': g(ks[10], (F, K, R, I)), 'down_qb': g(ks[11], (F, K, H, R)), 'down_scale': jnp.full((F, H), 0.1, jnp.float32), 'sh_gate_W': g(ks[12], (ISH, H)), 'sh_up_W': g(ks[13], (ISH, H)), 'sh_down_W': g(ks[14], (H, ISH))}
    _L0_ffn_in = _L0_ffn_setup()
    _d = {'L0_attn_a_x': _L0_attn_a_in['x'], 'L0_attn_a_Wq': _L0_attn_a_in['Wq'], 'L0_attn_a_Wk': _L0_attn_a_in['Wk'], 'L0_attn_a_Wv': _L0_attn_a_in['Wv'], 'L0_attn_a_Wo': _L0_attn_a_in['Wo'], 'L0_attn_b_Wq': _L0_attn_b_in['Wq'], 'L0_attn_b_bq': _L0_attn_b_in['bq'], 'L0_attn_b_Wk': _L0_attn_b_in['Wk'], 'L0_attn_b_bk': _L0_attn_b_in['bk'], 'L0_attn_b_Wv': _L0_attn_b_in['Wv'], 'L0_attn_b_bv': _L0_attn_b_in['bv'], 'L0_attn_b_Wo': _L0_attn_b_in['Wo'], 'L0_attn_b_bo': _L0_attn_b_in['bo'], 'L0_ffn_gate_weight': _L0_ffn_in['gate_weight'], 'L0_ffn_inv_mapping': _L0_ffn_in['inv_mapping'], 'L0_ffn_mask_up_W': _L0_ffn_in['mask_up_W'], 'L0_ffn_gate_W': _L0_ffn_in['gate_W'], 'L0_ffn_gate_qa': _L0_ffn_in['gate_qa'], 'L0_ffn_gate_qb': _L0_ffn_in['gate_qb'], 'L0_ffn_gate_scale': _L0_ffn_in['gate_scale'], 'L0_ffn_up_W': _L0_ffn_in['up_W'], 'L0_ffn_up_qa': _L0_ffn_in['up_qa'], 'L0_ffn_up_qb': _L0_ffn_in['up_qb'], 'L0_ffn_up_scale': _L0_ffn_in['up_scale'], 'L0_ffn_down_W': _L0_ffn_in['down_W'], 'L0_ffn_down_qa': _L0_ffn_in['down_qa'], 'L0_ffn_down_qb': _L0_ffn_in['down_qb'], 'L0_ffn_down_scale': _L0_ffn_in['down_scale'], 'L0_ffn_sh_gate_W': _L0_ffn_in['sh_gate_W'], 'L0_ffn_sh_up_W': _L0_ffn_in['sh_up_W'], 'L0_ffn_sh_down_W': _L0_ffn_in['sh_down_W']}
    _x0 = _d['L0_attn_a_x']
    _d['L0_attn_a_x'] = jax.random.normal(jax.random.fold_in(jax.random.key(seed), 1), (4, 512, 256), dtype=_x0.dtype)
    del _x0
    return _d

def reference(L0_attn_a_x, L0_attn_a_Wq, L0_attn_a_Wk, L0_attn_a_Wv, L0_attn_a_Wo, L0_attn_b_Wq, L0_attn_b_bq, L0_attn_b_Wk, L0_attn_b_bk, L0_attn_b_Wv, L0_attn_b_bv, L0_attn_b_Wo, L0_attn_b_bo, L0_ffn_gate_weight, L0_ffn_inv_mapping, L0_ffn_mask_up_W, L0_ffn_gate_W, L0_ffn_gate_qa, L0_ffn_gate_qb, L0_ffn_gate_scale, L0_ffn_up_W, L0_ffn_up_qa, L0_ffn_up_qb, L0_ffn_up_scale, L0_ffn_down_W, L0_ffn_down_qa, L0_ffn_down_qb, L0_ffn_down_scale, L0_ffn_sh_gate_W, L0_ffn_sh_up_W, L0_ffn_sh_down_W):

    def _L0_attn_a_ref(x, Wq, Wk, Wv, Wo):
        import jax, jax.numpy as jnp
        import numpy as np
        B, S, DM = (2, 256, 256)
        H, KVH, HD = (16, 4, 128)
        REP = H // KVH
        ROPE_BASE = 10000.0
        EPS = 1e-06

        def _rope_tables(seq_len, dim):
            inv_freq = 1.0 / ROPE_BASE ** (jnp.arange(0, dim, 2, dtype=jnp.float32) / dim)
            t = jnp.arange(seq_len, dtype=jnp.float32)
            freqs = jnp.outer(t, inv_freq)
            emb = jnp.concatenate([freqs, freqs], -1)
            return (jnp.cos(emb), jnp.sin(emb))

        def _rotate_half(x):
            d = x.shape[-1] // 2
            return jnp.concatenate([-x[..., d:], x[..., :d]], axis=-1)
        bsz, seq_len, _ = x.shape
        q = (x @ Wq.T).reshape(bsz, seq_len, H, HD).transpose(0, 2, 1, 3)
        k = (x @ Wk.T).reshape(bsz, seq_len, KVH, HD).transpose(0, 2, 1, 3)
        v = (x @ Wv.T).reshape(bsz, seq_len, KVH, HD).transpose(0, 2, 1, 3)
        cos, sin = _rope_tables(seq_len, HD)
        cos, sin = (cos[None, None], sin[None, None])
        q = q * cos + _rotate_half(q) * sin
        k = k * cos + _rotate_half(k) * sin
        k = jnp.repeat(k, REP, axis=1)
        v = jnp.repeat(v, REP, axis=1)
        qf = jax.nn.elu(q) + 1.0
        kf = jax.nn.elu(k) + 1.0
        qf_t = qf.transpose(2, 0, 1, 3)
        kf_t = kf.transpose(2, 0, 1, 3)
        v_t = v.transpose(2, 0, 1, 3)

        def step(carry, inp):
            state, z = carry
            q_s, k_s, v_s = inp
            state = state + k_s[..., :, None] * v_s[..., None, :]
            z = z + k_s
            num = jnp.einsum('bhe,bhed->bhd', q_s, state)
            den = jnp.einsum('bhe,bhe->bh', q_s, z)[..., None] + EPS
            return ((state, z), num / den)
        init = (jnp.zeros((bsz, H, HD, HD), x.dtype), jnp.zeros((bsz, H, HD), x.dtype))
        _, out = jax.lax.scan(step, init, (qf_t, kf_t, v_t))
        out = out.transpose(1, 0, 2, 3).reshape(bsz, seq_len, H * HD)
        return out @ Wo.T

    def _L0_attn_b_ref(hidden_states, Wq, bq, Wk, bk, Wv, bv, Wo, bo):
        import jax, jax.numpy as jnp
        import numpy as np
        import math
        FRAME_SIZE = 72
        GAMMA = 0.5
        NUM_HEADS = 32

        def rotate_half(x):
            x1, x2 = jnp.split(x, 2, axis=-1)
            return jnp.concatenate([-x2, x1], axis=-1)

        def apply_rope(x, freqs):
            return x * jnp.cos(freqs) + rotate_half(x) * jnp.sin(freqs)

        def rope_freqs(length, dim):
            theta = 10000.0 ** (-jnp.arange(0, dim, 2, dtype=jnp.float32) / dim)
            f = jnp.arange(length, dtype=jnp.float32)[:, None] * theta[None, :]
            return jnp.concatenate([f, f], axis=-1)
        B, T, C = hidden_states.shape
        H = NUM_HEADS
        dh = C // H

        def split_heads(x):
            return x.reshape(B, T, H, dh).transpose(0, 2, 1, 3)
        q = split_heads(hidden_states @ Wq.T + bq)
        k = split_heads(hidden_states @ Wk.T + bk)
        v = split_heads(hidden_states @ Wv.T + bv)
        freqs_abs = rope_freqs(T, dh)[None, None]
        q = apply_rope(q, freqs_abs)
        k = apply_rope(k, freqs_abs)
        temporal_ids = jnp.floor((jnp.arange(T) // FRAME_SIZE).astype(jnp.float32) * GAMMA).astype(jnp.int32)
        n_temp = int(math.floor((T - 1) // FRAME_SIZE * GAMMA)) + 1
        freqs_temp = rope_freqs(n_temp, dh)[temporal_ids][None, None]
        q = apply_rope(q, freqs_temp)
        k = apply_rope(k, freqs_temp)
        scores = jnp.einsum('bhqd,bhkd->bhqk', q, k) / math.sqrt(dh)
        causal = jnp.tril(jnp.ones((T, T), dtype=bool))
        scores = jnp.where(causal[None, None], scores, -jnp.inf)
        weights = jax.nn.softmax(scores, axis=-1)
        out = jnp.einsum('bhqk,bhkd->bhqd', weights, v)
        out = out.transpose(0, 2, 1, 3).reshape(B, T, H * dh)
        return out @ Wo.T + bo

    def _L0_ffn_ref(hidden_states, gate_weight, inv_mapping, mask_up_W, gate_W, gate_qa, gate_qb, gate_scale, up_W, up_qa, up_qb, up_scale, down_W, down_qa, down_qb, down_scale, sh_gate_W, sh_up_W, sh_down_W):
        import jax, jax.numpy as jnp
        import numpy as np
        B, S, H, I, E, F, K, R, TOPK = (1, 128, 256, 176, 64, 8, 8, 8, 6)
        ISH = 2 * I

        def _fused_linear(x, W, qa, qb, scale, w):
            out = x @ W.T
            a = jnp.einsum('th,krh->tkr', x, qa)
            b = jnp.einsum('tkr,khr->tkh', a, qb)
            mix = jnp.einsum('tkh,tk->th', b, w)
            return out + scale[None, :] * mix

        def _moe_forward(hidden_states, gate_weight, inv_mapping, mask_up_W, gate_W, gate_qa, gate_qb, gate_scale, up_W, up_qa, up_qb, up_scale, down_W, down_qa, down_qb, down_scale, sh_gate_W, sh_up_W, sh_down_W):
            b, s, h = hidden_states.shape
            x = hidden_states.reshape(-1, h)
            T = x.shape[0]
            scores = jax.nn.softmax(x @ gate_weight.T, axis=-1)
            topk_w, topk_idx = jax.lax.top_k(scores, TOPK)
            w_dense = jnp.zeros((T, E), x.dtype).at[jnp.arange(T)[:, None], topk_idx].add(topk_w)
            flat = w_dense[:, inv_mapping]
            scalar = flat.sum(-1)
            soft = jax.nn.softmax(jnp.where(flat == 0, -1000000000.0, flat), axis=-1)

            def expert(muW, gW, gqa, gqb, gs, uW, uqa, uqb, us, dW, dqa, dqb, ds, w):
                xe = x + w @ muW.T
                gate = jax.nn.silu(_fused_linear(xe, gW, gqa, gqb, gs, w))
                up = _fused_linear(xe, uW, uqa, uqb, us, w)
                return _fused_linear(gate * up, dW, dqa, dqb, ds, w)
            outs = jax.vmap(expert, in_axes=(0,) * 13 + (1,))(mask_up_W, gate_W, gate_qa, gate_qb, gate_scale, up_W, up_qa, up_qb, up_scale, down_W, down_qa, down_qb, down_scale, soft)
            y = jnp.einsum('fth,tf->th', outs, scalar).reshape(b, s, h)
            sh = jax.nn.silu(hidden_states @ sh_gate_W.T) * (hidden_states @ sh_up_W.T) @ sh_down_W.T
            return y + sh
        return _moe_forward(hidden_states, gate_weight, inv_mapping, mask_up_W, gate_W, gate_qa, gate_qb, gate_scale, up_W, up_qa, up_qb, up_scale, down_W, down_qa, down_qb, down_scale, sh_gate_W, sh_up_W, sh_down_W)
    x = L0_attn_a_x
    x = x + _L0_attn_a_ref(_layernorm(x, axis=-1), L0_attn_a_Wq, L0_attn_a_Wk, L0_attn_a_Wv, L0_attn_a_Wo)
    x = x + _L0_ffn_ref(_layernorm(x, axis=-1), L0_ffn_gate_weight, L0_ffn_inv_mapping, L0_ffn_mask_up_W, L0_ffn_gate_W, L0_ffn_gate_qa, L0_ffn_gate_qb, L0_ffn_gate_scale, L0_ffn_up_W, L0_ffn_up_qa, L0_ffn_up_qb, L0_ffn_up_scale, L0_ffn_down_W, L0_ffn_down_qa, L0_ffn_down_qb, L0_ffn_down_scale, L0_ffn_sh_gate_W, L0_ffn_sh_up_W, L0_ffn_sh_down_W)
    x = x + _L0_attn_b_ref(_layernorm(x, axis=-1), L0_attn_b_Wq, L0_attn_b_bq, L0_attn_b_Wk, L0_attn_b_bk, L0_attn_b_Wv, L0_attn_b_bv, L0_attn_b_Wo, L0_attn_b_bo)
    x = x + _L0_ffn_ref(_layernorm(x, axis=-1), L0_ffn_gate_weight, L0_ffn_inv_mapping, L0_ffn_mask_up_W, L0_ffn_gate_W, L0_ffn_gate_qa, L0_ffn_gate_qb, L0_ffn_gate_scale, L0_ffn_up_W, L0_ffn_up_qa, L0_ffn_up_qb, L0_ffn_up_scale, L0_ffn_down_W, L0_ffn_down_qa, L0_ffn_down_qb, L0_ffn_down_scale, L0_ffn_sh_gate_W, L0_ffn_sh_up_W, L0_ffn_sh_down_W)
    return x

_drawn_inputs = setup_inputs


def setup_inputs(seed=0):
    import zlib

    import numpy as np

    out = dict(_drawn_inputs(seed))
    spreads = {'L0_attn_b_bq': (0.0, 0.8),
     'L0_attn_b_bk': (0.0, 0.8),
     'L0_attn_b_bv': (0.0, 0.442),
     'L0_attn_b_bo': (0.0, 0.1),
     'L0_ffn_gate_scale': (0.10000000149011612, 0.6),
     'L0_ffn_up_scale': (0.10000000149011612, 0.6),
     'L0_ffn_down_scale': (0.10000000149011612, 0.6)}
    factors = {'L0_attn_a_Wq': 8.0,
     'L0_attn_a_Wk': 7.262,
     'L0_attn_b_Wq': 8.0,
     'L0_attn_b_Wk': 8.0,
     'L0_attn_b_Wv': 3.323,
     'L0_ffn_gate_weight': 8.0,
     'L0_ffn_mask_up_W': 8.0,
     'L0_ffn_gate_W': 8.0,
     'L0_ffn_gate_qa': 8.0,
     'L0_ffn_gate_qb': 8.0,
     'L0_ffn_up_W': 8.0,
     'L0_ffn_up_qa': 8.0,
     'L0_ffn_up_qb': 8.0,
     'L0_ffn_down_W': 8.0,
     'L0_ffn_down_qa': 8.0,
     'L0_ffn_down_qb': 8.0,
     'L0_ffn_sh_gate_W': 4.828,
     'L0_ffn_sh_up_W': 4.85,
     'L0_ffn_sh_down_W': 4.98}
    for name, (base, spread) in spreads.items():
        noise = np.random.default_rng([zlib.crc32(name.encode()), seed]).standard_normal(out[name].shape)
        drawn = base * np.exp(spread * noise) if base else spread * noise
        out[name] = jnp.asarray(drawn.astype(out[name].dtype))
    for name, factor in factors.items():
        out[name] = (out[name] * factor).astype(out[name].dtype)
    return out
```

```python
from contextlib import ExitStack

import concourse.bass as bass
from concourse import mybir

F32 = mybir.dt.float32
F32R = mybir.dt.float32r
BF16 = mybir.dt.bfloat16
I32 = mybir.dt.int32
ALU = mybir.AluOpType
ACT = mybir.ActivationFunctionType
AX = mybir.AxisListType.X
ds = bass.ds

P = 128
D = 256
KD = D // P
NB = 4
BT = 4
S = BT * P
LN_EPS = 1e-5

AH, AG, HD = 16, 4, 128
REP = AH // AG
A_EPS = 1e-6
BH, BD = 32, 8
HG = 4
NHG = BH // HG
NEG = -1e30
EX, EK, ER, EI = 8, 8, 8, 176
NE = EX * EK
KR = EK * ER
TOPK = 6
HJ = EI // 2
W1N = 2 * EI + 2 * KR
W2N = D + KR
SH = 2 * EI
SHC = [(0, 128), (128, 128), (256, SH - 256)]

LN_STEPS = ["stats", "aggregate", "var_eps", "std", "rstd", "normalised", "xT_psum", "xT"]
ROUTER_STEPS = ["logits", "row_max", "shifted", "exp", "exp_sum", "exp_rec", "probs", "top8", "top6",
                "others", "w_dense", "w_denseT_psum", "w_denseT", "flat_psum", "flat", "scalar", "penalty",
                "masked", "group_max", "group_shifted", "group_exp", "group_sum", "group_rec", "soft",
                "softT_psum", "softT"]


class Steps:

    def __init__(self, names):
        self.names = names

    def after(self, name, rounds=0):
        return rounds * len(self.names) + self.names.index(name) + 1


class Chip:
    pass


def resident(nc, ctx, c, dram):
    def sb(name, shape, dt=F32):
        return ctx.enter_context(nc.sbuf_tensor(name, shape, dt))

    c.dram = dram
    c.x = sb("x_resident", [P, NB * BT, D])
    c.xT = sb("xT", [P, KD, S])
    c.ident = sb("ident", [P, P])
    c.w1 = sb("w1", [P, KD, EX * W1N])
    c.w2 = sb("w2", [HJ, 2, EX * W2N])
    c.qb = sb("qb_gate_up", [KR + EK, EX * 2 * EI])
    c.qbd = sb("qb_down", [P, EX // 2, D])
    c.ma = sb("mask_up_low_rank", [NE, EX * 2 * KR])
    c.shgu = sb("shared_gate_up", [P, KD, 2 * SH])
    c.shd = sb("shared_down", [P, 3, D])
    c.wrt = sb("router_w", [P, KD, NE])
    c.onehot = sb("onehot", [NE, NE])
    c.xn = sb("x_normalised", [P, BT, D])
    c.ln_stats = sb("ln_stats", [P, BT, 6])
    c.ln_mv = sb("ln_mean_var", [P, BT, 2])
    c.ln_ve = sb("ln_var_eps", [P, BT])
    c.ln_std = sb("ln_std", [P, BT])
    c.ln_rstd = sb("ln_rstd", [P, BT])
    c.x_loaded = ctx.enter_context(nc.semaphore("x_loaded"))
    c.a_loaded = ctx.enter_context(nc.semaphore("first_loaded"))
    c.waits_met = ctx.enter_context(nc.semaphore("waits_met"))
    c.f_loaded = ctx.enter_context(nc.semaphore("f_loaded"))


def load_x(c, sp):
    xv = c.dram["x"].rearrange("(n p) d -> p n d", p=P)
    sp.dma_start(c.x[:, 0:BT, :], xv[:, 0:BT, :]).then_inc(c.x_loaded, 16)
    sp.dma_start(c.ident[:, :], c.dram["ident"]).then_inc(c.x_loaded, 16)


def load_rest_of_x(c, sp):
    xv = c.dram["x"].rearrange("(n p) d -> p n d", p=P)
    sp.dma_start(c.x[:, BT:, :], xv[:, BT:, :]).then_inc(c.a_loaded, 16)


def load_expert_weights(c, sp):
    sp.dma_start(c.w1[:, :, :], c.dram["w1"].rearrange("(k p) n -> p k n", p=P)).then_inc(c.f_loaded, 16)
    sp.dma_start(c.w2[:, :, :], c.dram["w2"].rearrange("(j p) n -> p j n", p=HJ)).then_inc(c.f_loaded, 16)
    sp.dma_start(c.qb[0:KR, :], c.dram["qb"]).then_inc(c.f_loaded, 16)
    sp.dma_start(c.qbd[:, :, :], c.dram["qbd"].rearrange("(q p) n -> p q n", p=P)).then_inc(c.f_loaded, 16)
    sp.dma_start(c.shgu[:, :, :], c.dram["shgu"].rearrange("(k p) n -> p k n", p=P)).then_inc(c.f_loaded, 16)
    for j, (lo, n) in enumerate(SHC):
        sp.dma_start(c.shd[0:n, j, :], c.dram["shd"][lo:lo + n, :]).then_inc(c.f_loaded, 16)
    sp.dma_start(c.wrt[:, :, :], c.dram["wrt"].rearrange("(k p) n -> p k n", p=P)).then_inc(c.f_loaded, 16)
    sp.wait_ge(c.f_loaded, 16 * 9)


def apart(engine, c):
    engine.sem_inc(c.waits_met, 1)



LN = Steps(LN_STEPS)


def ln_vector(nc, c, dve, sem, blk, rounds, t=LN):
    for i in range(BT):
        last = nc.vector.bn_stats(c.ln_stats[:, i, :], c.x[:, ds(blk * BT + i, 1), :].rearrange("p a d -> p (a d)"))
    last.then_inc(sem, 1)
    dve.wait_ge(sem, t.after("stats", rounds))
    apart(dve, c)
    for i in range(BT):
        last = nc.vector.bn_aggr(c.ln_mv[:, i, :], c.ln_stats[:, i, :])
    last.then_inc(sem, 1)
    dve.wait_ge(sem, t.after("aggregate", rounds))
    nc.vector.tensor_scalar(c.ln_ve[:, :], c.ln_mv[:, :, 1], LN_EPS, None, ALU.add).then_inc(sem, 1)
    dve.wait_ge(sem, t.after("std", rounds))
    nc.vector.reciprocal(c.ln_rstd[:, :], c.ln_std[:, :]).then_inc(sem, 1)
    dve.wait_ge(sem, t.after("rstd", rounds))
    for i in range(BT):
        last = nc.vector.tensor_scalar(c.xn[:, i, :], c.x[:, ds(blk * BT + i, 1), :].rearrange("p a d -> p (a d)"),
                                       c.ln_mv[:, i, 0:1], c.ln_rstd[:, i:i + 1], ALU.subtract, ALU.mult)
    last.then_inc(sem, 1)


def ln_scalar(nc, c, act, sem, rounds, banks, t=LN):
    act.wait_ge(sem, t.after("var_eps", rounds))
    nc.scalar.activation(c.ln_std[:, :], c.ln_ve[:, :], ACT.Sqrt).then_inc(sem, 1)
    act.wait_ge(sem, t.after("xT_psum", rounds))
    for k in range(KD):
        last = nc.scalar.activation(c.xT[:, k, :], banks[k][:, :], ACT.Copy)
    last.then_inc(sem, 1)


def ln_tensor(nc, c, pe, sem, rounds, banks, t=LN):
    pe.wait_ge(sem, t.after("normalised", rounds))
    for k in range(KD):
        for i in range(BT):
            last = nc.tensor.transpose(banks[k][:, i * P:(i + 1) * P], c.xn[:, i, k * P:(k + 1) * P], c.ident[:, :])
    last.then_inc(sem, 1)



def linear_attention(nc, c):
    ITEMS = REP + 2
    SLOTS = [[0, 1], [2], [3, 4], [5]]
    with ExitStack() as ctx:
        def sb(name, shape, dt=F32):
            return ctx.enter_context(nc.sbuf_tensor("a_" + name, shape, dt))

        def psum(name):
            return ctx.enter_context(nc.psum_tensor("a_ps_" + name, [P, 512], F32))

        def sem(name):
            return ctx.enter_context(nc.semaphore("a_" + name))

        w = sb("w_qkv", [P, KD, (AH + 2 * AG) * HD])
        wo = sb("w_out", [P, AH, D])
        cos, sin = sb("cos", [P, S]), sb("sin_crossed", [P, S])
        mask, ones = sb("mask", [P, P]), sb("ones", [P, S])
        qf, kf = sb("q_features", [P, 2, REP, S]), sb("k_features", [P, 2, S])
        kt, v = sb("k_tokens", [P, 2, BT, HD]), sb("v_tokens", [P, 2, BT, HD])
        zc = sb("k_cumsum", [P, 2, S])
        t1, t2 = sb("roped", [P, 2, S]), sb("rope_sin", [P, 2, S])
        en = sb("exp_neg", [P, 2, S])
        sc = sb("masked_scores", [P, REP, P])
        qz = sb("q_times_cumsum", [P, REP, P])
        den, rden = sb("den", [P, REP * P]), sb("rden", [P, REP * P])
        st = sb("state", [P, 2, HD])
        o = sb("head_out", [P, 2, REP, P])
        y = [psum("y0"), psum("y1")]
        pj = [psum("proj0"), psum("proj1")]
        s_ps, o_ps, d_ps, st_ps = psum("scores"), psum("out"), psum("den"), psum("state_kT")

        ln = sem("ln_steps")
        ones_set = sem("ones_set")
        projected = sem("projected")
        v_read, roped = sem("v_read"), sem("roped")
        summed, neg_part, exp_neg, featured = sem("summed"), sem("neg_part"), sem("exp_neg"), sem("featured")
        kT_psum, kT_read, cumsum = sem("kT_psum"), sem("kT_read"), sem("cumsum")
        scored, masked, qz_done = sem("scored"), sem("masked"), sem("qz_done")
        out_psum, den_psum = sem("out_psum"), sem("den_psum")
        den_read, rden_done = sem("den_read"), sem("rden_done")
        st_psum, st_read = sem("state_psum"), sem("state_read")
        out_done, added_psum, added = sem("out_done"), sem("y_psum"), sem("added")

        def kx(G):
            return G * (REP + 1)

        block = ctx.enter_context(nc.Block())

        @block.sync
        def _(sp):
            load_x(c, sp)
            wv = c.dram["a_w"].rearrange("(k p) n -> p k n", p=P)
            sp.dma_start(w[:, :, :], wv).then_inc(c.a_loaded, 16)
            sp.dma_start(cos[:, :], c.dram["a_cos"]).then_inc(c.a_loaded, 16)
            sp.dma_start(sin[:, :], c.dram["a_sin"]).then_inc(c.a_loaded, 16)
            sp.dma_start(mask[:, :], c.dram["a_mask"]).then_inc(c.a_loaded, 16)
            load_rest_of_x(c, sp)
            sp.dma_start(wo[:, :, :], c.dram["a_wo"].rearrange("(h p) n -> p h n", p=P)).then_inc(c.a_loaded, 16)
            load_expert_weights(c, sp)

        @block.tensor
        def _(pe):
            def project(b, g, m, first):
                G = b * AG + g
                if not (first and m < 2):
                    if m == 0 or m == 1:
                        pe.wait_ge(roped, kx(G) - 2 + m + 1)
                    elif m == 2:
                        pe.wait_ge(v_read, G + 1)
                    else:
                        pe.wait_ge(roped, kx(G) + m - 2)
                bank = pj[m % 2]
                if m == 0:
                    lo = (AH + AG + g) * HD
                    for i in range(BT):
                        for k in range(KD):
                            last = nc.tensor.matmul(bank[:, i * HD:(i + 1) * HD], c.xT[:, k, i * P:(i + 1) * P],
                                                    w[:, k, lo:lo + HD], start=(k == 0), stop=(k == KD - 1))
                else:
                    lo = (AH + g if m == 1 else g * REP + m - 2) * HD
                    for k in range(KD):
                        last = nc.tensor.matmul(bank[:, :], w[:, k, lo:lo + HD], c.xT[:, k, :],
                                                start=(k == 0), stop=(k == KD - 1))
                last.then_inc(projected, 1)

            def transpose_k(b, g, drained):
                G = b * AG + g
                pe.wait_ge(featured, kx(G) + 1)
                if not drained:
                    pe.wait_ge(st_read, (G - 1) * (BT - 1) + 1)
                for i in range(BT):
                    last = nc.tensor.transpose(st_ps[:, i * P:(i + 1) * P], kf[:, g % 2, i * P:(i + 1) * P],
                                               c.ident[:, :])
                last.then_inc(kT_psum, 1)

            def scores(b, g, ch):
                G = b * AG + g
                n = G * BT + ch
                if ch == 0:
                    pe.wait_ge(featured, kx(G + 1))
                    pe.wait_ge(kT_read, G + 1)
                    pe.wait_ge(v_read, G + 1)
                if not (ch == 0 and g == 0):
                    pe.wait_ge(masked, n)
                nc.tensor.matmul(s_ps[:, :], kf[:, g % 2, ch * P:(ch + 1) * P], qf[:, g % 2, :, ch * P:(ch + 1) * P],
                                 start=True, stop=True).then_inc(scored, 1)

            def outputs(b, g, ch):
                G = b * AG + g
                n = G * BT + ch
                pe.wait_ge(masked, n + 1)
                if not (ch == 0 and g == 0):
                    pe.wait_ge(out_done, n)
                    pe.wait_ge(den_read, n)
                if ch > 0:
                    pe.wait_ge(st_read, G * (BT - 1) + ch)
                    nc.tensor.matmul(o_ps[:, :], st[:, (ch - 1) % 2, :], qf[:, g % 2, :, ch * P:(ch + 1) * P],
                                     start=True, stop=False)
                nc.tensor.matmul(o_ps[:, :], v[:, g % 2, ch, :], sc[:, :, :],
                                 start=(ch == 0), stop=True).then_inc(out_psum, 1)
                pe.wait_ge(qz_done, n + 1)
                nc.tensor.matmul(d_ps[:, :], ones[:, 0:P], qz[:, :, :], start=True, stop=True).then_inc(den_psum, 1)

            def state(b, g, ch):
                G = b * AG + g
                nc.tensor.matmul(st_ps[:, 0:HD], kt[:, g % 2, ch, :], v[:, g % 2, ch, :],
                                 start=(ch == 0), stop=True, skip_group_check=True).then_inc(st_psum, 1)

            def add_out(b, g, ch):
                n = (b * AG + g) * BT + ch
                pe.wait_ge(out_done, n + 1)
                for h in range(REP):
                    last = nc.tensor.matmul(y[ch // 2][:, (ch % 2) * D:(ch % 2 + 1) * D], o[:, ch % 2, h, :],
                                            wo[:, g * REP + h, :], start=(g == 0 and h == 0 and ch % 2 == 0),
                                            stop=(g == AG - 1 and h == REP - 1), skip_group_check=True)
                last.then_inc(added_psum, 1)

            pe.wait_ge(c.a_loaded, 16 * 6)
            pe.wait_ge(ones_set, 1)
            with pe.Fori(0, NB) as b:
                ln_tensor(nc, c, pe, ln, b, pj)
                pe.wait_ge(ln, LN.after("xT", b))
                for m in range(ITEMS):
                    project(b, 0, m, True)
                transpose_k(b, 0, True)
                for g in range(AG):
                    for ch in range(BT):
                        scores(b, g, ch)
                        if g + 1 < AG:
                            for m in SLOTS[ch]:
                                project(b, g + 1, m, False)
                        if ch == 0:
                            pe.wait_ge(kT_read, b * AG + g + 1)
                        if ch < BT - 1:
                            if ch > 0:
                                pe.wait_ge(st_read, (b * AG + g) * (BT - 1) + ch)
                            state(b, g, ch)
                        outputs(b, g, ch)
                        if ch > 0:
                            add_out(b, g, ch - 1)
                        elif g > 0:
                            add_out(b, g - 1, BT - 1)
                    if g + 1 < AG:
                        pe.wait_ge(st_read, (b * AG + g + 1) * (BT - 1))
                        transpose_k(b, g + 1, True)
                add_out(b, AG - 1, BT - 1)

        @block.vector
        def _(dve):
            def rope(b, g, m):
                G = b * AG + g
                j = m - 1
                r = m % 2
                dve.wait_ge(projected, G * ITEMS + m + 1)
                if not (g == 0 and j < 2):
                    dve.wait_ge(featured, kx(G) + j - 1)
                nc.vector.tensor_tensor(t1[:, r, :], pj[r][:, :], cos[:, :], ALU.mult)
                nc.vector.tensor_tensor(t2[0:64, r, :], pj[r][64:128, :], sin[64:128, :], ALU.mult)
                nc.vector.tensor_tensor(t2[64:128, r, :], pj[r][0:64, :], sin[0:64, :], ALU.mult)\
                    .then_inc(roped, 1)

            def feature(b, g, m):
                G = b * AG + g
                j = m - 1
                r = m % 2
                dve.wait_ge(exp_neg, kx(G) + j + 1)
                dst = kf[:, g % 2, :] if m == 1 else qf[:, g % 2, m - 2, :]
                nc.vector.scalar_tensor_tensor(out=dst, in0=t1[:, r, :], scalar=0.0, in1=en[:, r, :],
                                               op0=ALU.max, op1=ALU.add).then_inc(featured, 1)
                if m == 1:
                    dve.wait_ge(featured, kx(G) + 1)
                    nc.vector.tensor_tensor_scan(zc[:, g % 2, :], ones[:, :], kf[:, g % 2, :], 0.0,
                                                 ALU.mult, ALU.add).then_inc(cumsum, 1)

            def mask_scores(b, g, ch):
                n = (b * AG + g) * BT + ch
                dve.wait_ge(scored, n + 1)
                if not (g == 0 and ch == 0):
                    dve.wait_ge(out_psum, n)
                nc.vector.tensor_tensor(sc[:, :, :], s_ps[:, :].rearrange("p (h t) -> p h t", h=REP),
                                        mask[:, :].unsqueeze(1).to_broadcast([P, REP, P]), ALU.mult)\
                    .then_inc(masked, 1)

            def divide(b, g, ch):
                n = (b * AG + g) * BT + ch
                dve.wait_ge(den_read, n + 1)
                nc.vector.reciprocal(rden[:, :], den[:, :]).then_inc(rden_done, 1)
                dve.wait_ge(rden_done, n + 1)
                dve.wait_ge(out_psum, n + 1)
                if not (g == 0 and ch < 2):
                    dve.wait_ge(added_psum, n - 1)
                nc.vector.tensor_tensor(o[:, ch % 2, :, :].rearrange("p h t -> p (h t)"), o_ps[:, :],
                                        rden[:, :], ALU.mult).then_inc(out_done, 1)

            nc.vector.memset(ones[:, :], 1.0).then_inc(ones_set, 1)
            dve.wait_ge(c.a_loaded, 16 * 6)
            dve.wait_ge(c.x_loaded, 32)
            dve.wait_ge(ones_set, 1)
            with dve.Fori(0, NB) as b:
                ln_vector(nc, c, dve, ln, b, b)
                for m in range(1, ITEMS):
                    rope(b, 0, m)
                    if m > 1:
                        feature(b, 0, m - 1)
                feature(b, 0, ITEMS - 1)
                for g in range(AG):
                    pending = None
                    for ch in range(BT):
                        mask_scores(b, g, ch)
                        if g + 1 < AG:
                            for m in SLOTS[ch]:
                                if m == 0:
                                    continue
                                rope(b, g + 1, m)
                                if pending:
                                    feature(b, g + 1, pending)
                                pending = m
                        divide(b, g, ch)
                    if pending:
                        feature(b, g + 1, pending)
                dve.wait_ge(added_psum, (b + 1) * AG * BT)
                for i in range(2):
                    xs = c.x[:, ds(b * BT + 2 * i, 2), :]
                    last = nc.vector.tensor_tensor(xs, xs, y[i][:, :].rearrange("p (a d) -> p a d", a=2), ALU.add)
                last.then_inc(added, 1)
                dve.wait_ge(added, b + 1)

        @block.gpsimd
        def _(pool):
            def add_rope(b, g, m):
                G = b * AG + g
                j = m - 1
                r = m % 2
                pool.wait_ge(roped, kx(G) + j + 1)
                nc.gpsimd.tensor_tensor(t1[:, r, :], t1[:, r, :], t2[:, r, :], ALU.add).then_inc(summed, 1)

            def times_cumsum(b, g, ch):
                G = b * AG + g
                n = G * BT + ch
                if ch == 0:
                    pool.wait_ge(cumsum, G + 1)
                    pool.wait_ge(featured, kx(G + 1))
                if not (g == 0 and ch == 0):
                    pool.wait_ge(den_psum, n)
                z = zc[:, g % 2, ch * P:(ch + 1) * P].unsqueeze(1).to_broadcast([P, REP, P])
                nc.gpsimd.tensor_tensor(qz[:, :, :], qf[:, g % 2, :, ch * P:(ch + 1) * P], z, ALU.mult)\
                    .then_inc(qz_done, 1)

            with pool.Fori(0, NB) as b:
                for m in range(1, ITEMS):
                    add_rope(b, 0, m)
                for g in range(AG):
                    for ch in range(BT):
                        times_cumsum(b, g, ch)
                        if g + 1 < AG:
                            for m in SLOTS[ch]:
                                if m > 0:
                                    add_rope(b, g + 1, m)

        @block.scalar
        def _(act):
            def read_v(b, g):
                G = b * AG + g
                act.wait_ge(projected, G * ITEMS + 1)
                nc.scalar.activation(v[:, g % 2, :, :].rearrange("p t d -> p (t d)"), pj[0][:, :], ACT.Copy)\
                    .then_inc(v_read, 1)

            def exp_negative(b, g, m):
                G = b * AG + g
                j = m - 1
                r = m % 2
                act.wait_ge(summed, kx(G) + j + 1)
                if not (g == 0 and j < 2):
                    act.wait_ge(featured, kx(G) + j - 1)
                nc.scalar.activation(en[:, r, :], t1[:, r, :], ACT.Relu, scale=-1.0).then_inc(neg_part, 1)
                act.wait_ge(neg_part, kx(G) + j + 1)
                nc.scalar.activation(en[:, r, :], en[:, r, :], ACT.Exp, scale=-1.0).then_inc(exp_neg, 1)

            def read_k(b, g):
                act.wait_ge(kT_psum, b * AG + g + 1)
                nc.scalar.activation(kt[:, g % 2, :, :].rearrange("p t d -> p (t d)"), st_ps[:, :], ACT.Copy)\
                    .then_inc(kT_read, 1)

            def read_state(b, g, ch):
                G = b * AG + g
                act.wait_ge(st_psum, G * (BT - 1) + ch + 1)
                nc.scalar.activation(st[:, ch % 2, :], st_ps[:, 0:HD], ACT.Copy).then_inc(st_read, 1)

            def read_den(b, g, ch):
                n = (b * AG + g) * BT + ch
                act.wait_ge(den_psum, n + 1)
                if not (g == 0 and ch == 0):
                    act.wait_ge(out_done, n)
                nc.scalar.activation(den[:, :], d_ps[:, :], ACT.Copy, bias=A_EPS).then_inc(den_read, 1)

            with act.Fori(0, NB) as b:
                ln_scalar(nc, c, act, ln, b, pj)
                read_v(b, 0)
                for m in range(1, ITEMS):
                    exp_negative(b, 0, m)
                read_k(b, 0)
                for g in range(AG):
                    for ch in range(BT):
                        if g + 1 < AG:
                            for m in SLOTS[ch]:
                                if m == 0:
                                    read_v(b, g + 1)
                                else:
                                    exp_negative(b, g + 1, m)
                        if ch < BT - 1:
                            read_state(b, g, ch)
                        read_den(b, g, ch)
                    if g + 1 < AG:
                        read_k(b, g + 1)



def expert_weights(nc, c):
    with ExitStack() as ctx:
        def sb(name, shape, dt=F32):
            return ctx.enter_context(nc.sbuf_tensor("e_" + name, shape, dt))

        def sem(name):
            return ctx.enter_context(nc.semaphore("e_" + name))

        scale_gu = sb("scale_gate_up", [KR, EX * 2 * EI])
        scale_d = sb("scale_down", [P, EX // 2, D])
        mu = sb("mask_up", [P, KD, NE])
        mup = sb("mask_up_padded", [P, KD, EX * NE])
        idx, idxf = sb("mapping", [NE, NE], I32), sb("mapping_f32", [NE, NE])
        row = sb("row_number", [NE, 1])
        ps = [ctx.enter_context(nc.psum_tensor(f"e_ps{i}", [P, 512], F32)) for i in range(4)]
        loaded, gu_ready, ma_ready = sem("loaded"), sem("gu_psum"), sem("ma_psum")
        gu_read, ma_read, small = sem("gu_read"), sem("ma_read"), sem("small")
        block = ctx.enter_context(nc.Block())

        @block.sync
        def _(sp):
            sp.dma_start(scale_gu[:, :], c.dram["scale_gu"].partition_broadcast(KR)).then_inc(loaded, 16)
            for f in range(EX):
                sp.dma_start(scale_d[(f % 2) * KR:(f % 2 + 1) * KR, f // 2, :],
                             c.dram["scale_d"][f, :].partition_broadcast(KR)).then_inc(loaded, 16)
            sp.dma_start(mu[:, :, :], c.dram["mu"].rearrange("(k p) n -> p k n", p=P)).then_inc(loaded, 16)
            sp.dma_start(mup[:, :, :], c.dram["mup"].rearrange("(k p) n -> p k n", p=P)).then_inc(loaded, 16)
            sp.dma_start(idx[:, :], c.dram["mapping"].partition_broadcast(NE)).then_inc(loaded, 16)
            sp.dma_start(row[:, :], c.dram["row"]).then_inc(loaded, 16)

        @block.tensor
        def _(pe):
            pe.wait_ge(loaded, 16 * 13)
            for f in range(EX):
                if f >= 2:
                    pe.wait_ge(gu_read, f - 1)
                    pe.wait_ge(ma_read, f - 1)
                for k in range(KD):
                    last = nc.tensor.matmul(ps[f % 2][0:EK, 0:2 * EI], mu[:, k, f * EK:(f + 1) * EK],
                                            c.w1[:, k, f * W1N:f * W1N + 2 * EI], start=(k == 0), stop=(k == KD - 1))
                last.then_inc(gu_ready, 1)
                for k in range(KD):
                    last = nc.tensor.matmul(ps[2 + f % 2][0:NE, 0:2 * KR], mup[:, k, f * NE:(f + 1) * NE],
                                            c.w1[:, k, f * W1N + 2 * EI:(f + 1) * W1N],
                                            start=(k == 0), stop=(k == KD - 1))
                last.then_inc(ma_ready, 1)

        @block.scalar
        def _(act):
            for f in range(EX):
                act.wait_ge(gu_ready, f + 1)
                nc.scalar.activation(c.qb[KR:KR + EK, f * 2 * EI:(f + 1) * 2 * EI], ps[f % 2][0:EK, 0:2 * EI],
                                     ACT.Copy).then_inc(gu_read, 1)

        @block.vector
        def _(dve):
            dve.wait_ge(loaded, 16 * 13)
            nc.vector.tensor_tensor(c.qb[0:KR, :], c.qb[0:KR, :], scale_gu[:, :], ALU.mult)
            nc.vector.tensor_tensor(c.qbd[:, :, :], c.qbd[:, :, :], scale_d[:, :, :], ALU.mult)
            nc.vector.tensor_copy(idxf[:, :], idx[:, :]).then_inc(small, 1)
            dve.wait_ge(small, 1)
            nc.vector.tensor_scalar(c.onehot[:, :], idxf[:, :], row[:, 0:1], None, ALU.is_equal).then_inc(small, 1)
            for f in range(EX):
                dve.wait_ge(ma_ready, f + 1)
                nc.vector.tensor_copy(c.ma[:, f * 2 * KR:(f + 1) * 2 * KR], ps[2 + f % 2][0:NE, 0:2 * KR])\
                    .then_inc(ma_read, 1)



def experts(nc, c, tag, last_layer):
    prep = Steps(LN_STEPS + ROUTER_STEPS)
    UB = EX * BT
    with ExitStack() as ctx:
        def sb(name, shape, dt=F32):
            return ctx.enter_context(nc.sbuf_tensor(tag + name, shape, dt))

        def psum(name):
            return ctx.enter_context(nc.psum_tensor(tag + "ps_" + name, [P, 512], F32))

        def sem(name):
            return ctx.enter_context(nc.semaphore(tag + name))

        rmax, lg, ex = sb("row_max", [P, BT]), sb("shifted", [P, BT, NE]), sb("exp", [P, BT, NE])
        esum, erec = sb("exp_sum", [P, BT]), sb("exp_rec", [P, BT])
        pr = sb("probs", [P, BT, NE + 2])
        top, rest = sb("top8", [P, BT, 8]), sb("others", [P, BT, NE + 2])
        wd, wdT = sb("w_dense", [P, BT, NE]), sb("w_denseT", [NE, S])
        flat, pen = sb("flat", [P, BT, EX, EK]), sb("penalty", [P, BT, EX, EK])
        fm, gmax = sb("masked", [P, BT, EX, EK]), sb("group_max", [P, BT, EX])
        fe, gsum, grec = sb("group_exp", [P, BT, EX, EK]), sb("group_sum", [P, BT, EX]), sb("group_rec", [P, BT, EX])
        scal = sb("scalar", [P, BT, EX])
        soft, softT = sb("soft", [P, BT, NE]), sb("softT", [NE, S])
        ssg, shh = sb("shared_silu", [P, 2, SH]), sb("shared_h", [P, 2, SH])
        shT = sb("shared_hT", [P, 3, P])
        aw, awT = sb("low_rank", [P, 2, 2, KR + EK]), sb("low_rankT", [KR + EK, 2, 2, P])
        sg, h, hT = sb("silu_gate", [P, 2, EI]), sb("hidden", [P, 2, EI]), sb("hiddenT", [HJ, 2, 2, P])
        dw, dwT = sb("down_low_rank", [P, BT, EX * KR]), sb("down_low_rankT", [P, 2, 4 * P])
        m_ps = [psum("main0"), psum("main1")]
        t_ps, h_ps, d_ps, r_ps = psum("low_rankT"), psum("hiddenT"), psum("down_low"), psum("router")
        y = [psum("y0"), psum("y1")]
        sh_ps = [(m_ps[0], m_ps[1]), (d_ps, h_ps)]

        steps = sem("prep_steps")
        minus_ones = sem("minus_ones")
        sh_main, sh_silu, sh_h, sh_hT_ps, sh_hT, sh_down = (sem("sh_" + n) for n in
                                                            ["main", "silu", "h", "hT_psum", "hT", "down"])
        main_done, aw_done, aww_done, awT_ps, awT_done = (sem(n) for n in
                                                          ["main", "aw", "aw_soft", "awT_psum", "awT"])
        gate_up, silu_done, h_done, hT_ps, hT_done = (sem(n) for n in
                                                      ["gate_up", "silu", "h", "hT_psum", "hT"])
        down_done, dw_done = sem("down"), sem("dw")
        dwT_ps, dwT_done, closed, added = sem("dwT_psum"), sem("dwT"), sem("closed"), sem("added")
        stored = sem("stored")

        def unit(blk, e, i, back=0):
            e, i = (e, i - back) if i >= back else (e - 1, i - back + BT)
            return e, i, blk * UB + e * BT + i

        block = ctx.enter_context(nc.Block())

        def run_units(engine, blk, step):
            for i in range(BT):
                step(blk, 0, i, i)
            with engine.Fori(1, EX) as e:
                for i in range(BT):
                    step(blk, e, i, BT)
            step(blk, EX, 0, BT, tail=1)
            step(blk, EX, 1, BT, tail=2)

        @block.tensor
        def _(pe):
            def ychunk(i):
                return y[i // 2][:, (i % 2) * D:(i % 2 + 1) * D]

            def shared_main(blk, i):
                if i >= 2:
                    pe.wait_ge(sh_h, blk * BT + i - 1)
                for n in range(2):
                    for k in range(KD):
                        last = nc.tensor.matmul(sh_ps[i % 2][n][:, 0:SH], c.xT[:, k, i * P:(i + 1) * P],
                                                c.shgu[:, k, n * SH:(n + 1) * SH], start=(k == 0), stop=(k == KD - 1))
                last.then_inc(sh_main, 1)

            def shared_down(blk, i):
                pe.wait_ge(sh_h, blk * BT + i + 1)
                if i > 0:
                    pe.wait_ge(sh_hT, blk * BT + i)
                for j, (lo, n) in enumerate(SHC):
                    last = nc.tensor.transpose(t_ps[0:n, j * P:(j + 1) * P], shh[:, i % 2, lo:lo + n], c.ident[:, :])
                last.then_inc(sh_hT_ps, 1)
                pe.wait_ge(sh_hT, blk * BT + i + 1)
                for j, (lo, n) in enumerate(SHC):
                    last = nc.tensor.matmul(ychunk(i), shT[0:n, j, :], c.shd[0:n, j, :],
                                            start=(i % 2 == 0 and j == 0), stop=False, skip_group_check=True)
                last.then_inc(sh_down, 1)

            def step(blk, e0, i0, have, tail=0):
                if not tail:
                    e, i, n = unit(blk, e0, i0)
                    if have >= 2:
                        pe.wait_ge(h_done, n - 1)
                    bank = m_ps[i % 2]
                    for k in range(KD):
                        nc.tensor.matmul(bank[:, 0:W1N], c.xT[:, k, i * P:(i + 1) * P],
                                         c.w1[:, k, ds(e * W1N, W1N)], start=(k == 0), stop=False,
                                         skip_group_check=True)
                    nc.tensor.matmul(bank[:, 2 * EI:W1N], softT[:, i * P:(i + 1) * P],
                                     c.ma[:, ds(e * 2 * KR, 2 * KR)], start=False, stop=False,
                                     skip_group_check=True).then_inc(main_done, 1)
                if have >= 1 and tail < 2:
                    e, i, n = unit(blk, e0, i0, 1)
                    pe.wait_ge(awT_done, n + 1)
                    for s in range(2):
                        last = nc.tensor.matmul(m_ps[i % 2][:, s * EI:(s + 1) * EI], awT[:, i % 2, s, :],
                                                c.qb[:, ds(e * 2 * EI + s * EI, EI)], start=False, stop=(s == 1),
                                                skip_group_check=True)
                    last.then_inc(gate_up, 1)
                if not tail:
                    e, i, n = unit(blk, e0, i0)
                    pe.wait_ge(aw_done, n + 1)
                    pe.wait_ge(aww_done, n + 1)
                    for s in range(2):
                        last = nc.tensor.transpose(t_ps[0:KR + EK, s * P:(s + 1) * P], aw[:, i % 2, s, :],
                                                   c.ident[:, :])
                    last.then_inc(awT_ps, 1)
                if have >= 2:
                    e, i, n = unit(blk, e0, i0, 2)
                    pe.wait_ge(hT_done, n + 1)
                    if have >= 3:
                        pe.wait_ge(dw_done, n)
                    for j in range(2):
                        nc.tensor.matmul(ychunk(i), hT[:, i % 2, j, :], c.w2[:, j, ds(e * W2N, D)],
                                         start=False, stop=False, skip_group_check=True)
                    for j in range(2):
                        last = nc.tensor.matmul(d_ps[:, 0:KR], hT[:, i % 2, j, :],
                                                c.w2[:, j, ds(e * W2N + D, KR)], start=(j == 0), stop=(j == 1))
                    last.then_inc(down_done, 1)
                if have >= 1 and tail < 2:
                    e, i, n = unit(blk, e0, i0, 1)
                    pe.wait_ge(h_done, n + 1)
                    for j in range(2):
                        last = nc.tensor.transpose(h_ps[0:HJ, j * P:(j + 1) * P], h[:, i % 2, j * HJ:(j + 1) * HJ],
                                                   c.ident[:, :])
                    last.then_inc(hT_ps, 1)

            with pe.Fori(0, NB) as blk:
                ln_tensor(nc, c, pe, steps, blk, m_ps, prep)
                pe.wait_ge(steps, prep.after("xT", blk))
                for i in range(BT):
                    for k in range(KD):
                        last = nc.tensor.matmul(r_ps[:, i * NE:(i + 1) * NE], c.xT[:, k, i * P:(i + 1) * P],
                                                c.wrt[:, k, :], start=(k == 0), stop=(k == KD - 1))
                last.then_inc(steps, 1)
                shared_main(blk, 0)
                shared_main(blk, 1)
                pe.wait_ge(steps, prep.after("w_dense", blk))
                apart(pe, c)
                for i in range(BT):
                    last = nc.tensor.transpose(t_ps[0:NE, i * P:(i + 1) * P], wd[:, i, :], c.ident[:, :])
                last.then_inc(steps, 1)
                pe.wait_ge(steps, prep.after("w_denseT", blk))
                for i in range(BT):
                    last = nc.tensor.matmul(r_ps[:, i * NE:(i + 1) * NE], wdT[:, i * P:(i + 1) * P], c.onehot[:, :],
                                            start=True, stop=True)
                last.then_inc(steps, 1)
                pe.wait_ge(steps, prep.after("soft", blk))
                apart(pe, c)
                for i in range(BT):
                    last = nc.tensor.transpose(t_ps[0:NE, i * P:(i + 1) * P], soft[:, i, :], c.ident[:, :])
                last.then_inc(steps, 1)
                pe.wait_ge(steps, prep.after("softT", blk))
                for i in range(BT):
                    shared_down(blk, i)
                    if i + 2 < BT:
                        shared_main(blk, i + 2)
                run_units(pe, blk, step)
                for i in range(BT):
                    pe.wait_ge(dw_done, (blk + 1) * UB)
                    if i > 0:
                        pe.wait_ge(dwT_done, blk * BT + i)
                    for q in range(4):
                        last = nc.tensor.transpose(t_ps[:, q * P:(q + 1) * P], dw[:, i, q * P:(q + 1) * P],
                                                   c.ident[:, :])
                    last.then_inc(dwT_ps, 1)
                    pe.wait_ge(dwT_done, blk * BT + i + 1)
                    for q in range(4):
                        last = nc.tensor.matmul(ychunk(i), dwT[:, i % 2, q * P:(q + 1) * P], c.qbd[:, q, :],
                                                start=False, stop=(q == 3), skip_group_check=True)
                    last.then_inc(closed, 1)

        @block.vector
        def _(dve):
            def at(name, blk):
                dve.wait_ge(steps, prep.after(name, blk))

            def step(blk, e0, i0, have, tail=0):
                if not tail:
                    e, i, n = unit(blk, e0, i0)
                    dve.wait_ge(main_done, n + 1)
                    a = m_ps[i % 2][:, 2 * EI:W1N].rearrange("p (s k r) -> p s k r", s=2, k=EK)
                    w = soft[:, i, ds(e * EK, EK)].unsqueeze(1).unsqueeze(3).to_broadcast([P, 2, EK, ER])
                    nc.vector.tensor_tensor(aw[:, i % 2, :, 0:KR].rearrange("p s (k r) -> p s k r", k=EK), a, w,
                                            ALU.mult).then_inc(aw_done, 1)
                if have >= 1 and tail < 2:
                    e, i, n = unit(blk, e0, i0, 1)
                    dve.wait_ge(silu_done, n + 1)
                    nc.vector.scalar_tensor_tensor(out=h[:, i % 2, :], in0=sg[:, i % 2, :],
                                                   scalar=scal[:, i, ds(e, 1)], in1=m_ps[i % 2][:, EI:2 * EI],
                                                   op0=ALU.mult, op1=ALU.mult).then_inc(h_done, 1)
                if have >= 2:
                    e, i, n = unit(blk, e0, i0, 2)
                    dve.wait_ge(down_done, n + 1)
                    a = d_ps[:, 0:KR].rearrange("p (k r) -> p k r", k=EK)
                    w = soft[:, i, ds(e * EK, EK)].unsqueeze(2).to_broadcast([P, EK, ER])
                    nc.vector.tensor_tensor(dw[:, i, ds(e * KR, KR)].rearrange("p (k r) -> p k r", k=EK), a, w,
                                            ALU.mult).then_inc(dw_done, 1)

            nc.vector.memset(pr[:, :, NE:NE + 2], -1.0).then_inc(minus_ones, 1)
            dve.wait_ge(minus_ones, 1)
            with dve.Fori(0, NB) as blk:
                ln_vector(nc, c, dve, steps, blk, blk, prep)
                at("logits", blk)
                r4 = r_ps[:, 0:BT * NE].rearrange("p (t n) -> p t n", t=BT)
                nc.vector.reduce_max(rmax[:, :], r4, AX).then_inc(steps, 1)
                at("row_max", blk)
                nc.vector.tensor_tensor(lg[:, :, :], r4, rmax[:, :].unsqueeze(2).to_broadcast([P, BT, NE]),
                                        ALU.subtract).then_inc(steps, 1)
                at("exp", blk)
                nc.vector.reduce_sum(esum[:, :], ex[:, :, :], AX).then_inc(steps, 1)
                at("exp_sum", blk)
                nc.vector.reciprocal(erec[:, :], esum[:, :]).then_inc(steps, 1)
                at("exp_rec", blk)
                nc.vector.tensor_tensor(pr[:, :, 0:NE], ex[:, :, :], erec[:, :].unsqueeze(2).to_broadcast([P, BT, NE]),
                                        ALU.mult).then_inc(steps, 1)
                at("probs", blk)
                apart(dve, c)
                for i in range(BT):
                    last = nc.vector.max(top[:, i, :], pr[:, i, 0:NE])
                last.then_inc(steps, 1)
                at("top8", blk)
                nc.vector.memset(top[:, :, TOPK:8], -1.0).then_inc(steps, 1)
                at("top6", blk)
                apart(dve, c)
                for i in range(BT):
                    last = nc.vector.match_replace(rest[:, i, :], top[:, i, :], pr[:, i, :], 0.0)
                last.then_inc(steps, 1)
                at("others", blk)
                nc.vector.tensor_tensor(wd[:, :, :], pr[:, :, 0:NE], rest[:, :, 0:NE], ALU.subtract)\
                    .then_inc(steps, 1)
                at("flat_psum", blk)
                nc.vector.tensor_copy(flat[:, :, :, :].rearrange("p t f k -> p (t f k)"), r_ps[:, 0:BT * NE])\
                    .then_inc(steps, 1)
                at("flat", blk)
                nc.vector.reduce_sum(scal[:, :, :], flat[:, :, :, :], AX).then_inc(steps, 1)
                at("scalar", blk)
                nc.vector.tensor_scalar(pen[:, :, :, :], flat[:, :, :, :], 0.0, -1e9, ALU.is_equal, ALU.mult)\
                    .then_inc(steps, 1)
                at("penalty", blk)
                nc.vector.tensor_tensor(fm[:, :, :, :], flat[:, :, :, :], pen[:, :, :, :], ALU.add).then_inc(steps, 1)
                at("masked", blk)
                nc.vector.reduce_max(gmax[:, :, :], fm[:, :, :, :], AX).then_inc(steps, 1)
                at("group_max", blk)
                g4 = [P, BT, EX, EK]
                nc.vector.tensor_tensor(fm[:, :, :, :], fm[:, :, :, :], gmax[:, :, :].unsqueeze(3).to_broadcast(g4),
                                        ALU.subtract).then_inc(steps, 1)
                at("group_exp", blk)
                nc.vector.reduce_sum(gsum[:, :, :], fe[:, :, :, :], AX).then_inc(steps, 1)
                at("group_sum", blk)
                nc.vector.reciprocal(grec[:, :, :], gsum[:, :, :]).then_inc(steps, 1)
                at("group_rec", blk)
                nc.vector.tensor_tensor(soft[:, :, :].rearrange("p t (f k) -> p t f k", f=EX), fe[:, :, :, :],
                                        grec[:, :, :].unsqueeze(3).to_broadcast(g4), ALU.mult).then_inc(steps, 1)
                for i in range(BT):
                    dve.wait_ge(sh_silu, blk * BT + i + 1)
                    nc.vector.tensor_tensor(shh[:, i % 2, :], ssg[:, i % 2, :], sh_ps[i % 2][1][:, 0:SH], ALU.mult)\
                        .then_inc(sh_h, 1)
                run_units(dve, blk, step)
                dve.wait_ge(closed, (blk + 1) * BT)
                for j in range(2):
                    xs = c.x[:, ds(blk * BT + 2 * j, 2), :]
                    last = nc.vector.tensor_tensor(xs, xs, y[j][:, :].rearrange("p (a d) -> p a d", a=2), ALU.add)
                last.then_inc(added, 1)
                dve.wait_ge(added, blk + 1)

        @block.gpsimd
        def _(pool):
            def step(blk, e0, i0, have, tail=0):
                if tail:
                    return
                e, i, n = unit(blk, e0, i0)
                if have >= 2:
                    pool.wait_ge(awT_ps, n - 1)
                apart(pool, c)
                w = soft[:, i, ds(e * EK, EK)].unsqueeze(1).to_broadcast([P, 2, EK])
                nc.gpsimd.tensor_copy(aw[:, i % 2, :, KR:KR + EK], w).then_inc(aww_done, 1)

            with pool.Fori(0, NB) as blk:
                pool.wait_ge(steps, prep.after("soft", blk))
                run_units(pool, blk, step)

        @block.scalar
        def _(act):
            def step(blk, e0, i0, have, tail=0):
                if have >= 1 and tail < 2:
                    e, i, n = unit(blk, e0, i0, 1)
                    act.wait_ge(gate_up, n + 1)
                    if have >= 3:
                        act.wait_ge(h_done, n - 1)
                    nc.scalar.activation(sg[:, i % 2, :], m_ps[i % 2][:, 0:EI], ACT.Silu).then_inc(silu_done, 1)
                if not tail:
                    e, i, n = unit(blk, e0, i0)
                    act.wait_ge(awT_ps, n + 1)
                    nc.scalar.activation(awT[:, i % 2, :, :].rearrange("p s t -> p (s t)"), t_ps[0:KR + EK, 0:2 * P],
                                         ACT.Copy).then_inc(awT_done, 1)
                if have >= 1 and tail < 2:
                    e, i, n = unit(blk, e0, i0, 1)
                    act.wait_ge(hT_ps, n + 1)
                    nc.scalar.activation(hT[:, i % 2, :, :].rearrange("p s t -> p (s t)"), h_ps[0:HJ, 0:2 * P],
                                         ACT.Copy).then_inc(hT_done, 1)

            with act.Fori(0, NB) as blk:
                ln_scalar(nc, c, act, steps, blk, m_ps, prep)
                act.wait_ge(steps, prep.after("shifted", blk))
                nc.scalar.activation(ex[:, :, :], lg[:, :, :], ACT.Exp).then_inc(steps, 1)
                act.wait_ge(steps, prep.after("w_denseT_psum", blk))
                nc.scalar.activation(wdT[:, :], t_ps[0:NE, :], ACT.Copy).then_inc(steps, 1)
                act.wait_ge(steps, prep.after("group_shifted", blk))
                nc.scalar.activation(fe[:, :, :, :], fm[:, :, :, :], ACT.Exp).then_inc(steps, 1)
                act.wait_ge(steps, prep.after("softT_psum", blk))
                nc.scalar.activation(softT[:, :], t_ps[0:NE, :], ACT.Copy).then_inc(steps, 1)

                def shared_silu(i):
                    act.wait_ge(sh_main, blk * BT + i + 1)
                    nc.scalar.activation(ssg[:, i % 2, :], sh_ps[i % 2][0][:, 0:SH], ACT.Silu).then_inc(sh_silu, 1)

                shared_silu(0)
                for i in range(BT):
                    if i + 1 < BT:
                        if i >= 1:
                            act.wait_ge(sh_h, blk * BT + i)
                        shared_silu(i + 1)
                    act.wait_ge(sh_hT_ps, blk * BT + i + 1)
                    if i > 0:
                        act.wait_ge(sh_down, blk * BT + i)
                    nc.scalar.activation(shT[:, 0:2, :].rearrange("p s t -> p (s t)"), t_ps[:, 0:2 * P], ACT.Copy)
                    n = SHC[2][1]
                    nc.scalar.activation(shT[0:n, 2, :], t_ps[0:n, 2 * P:3 * P], ACT.Copy).then_inc(sh_hT, 1)
                run_units(act, blk, step)
                for i in range(BT):
                    act.wait_ge(dwT_ps, blk * BT + i + 1)
                    if i >= 2:
                        act.wait_ge(closed, blk * BT + i - 1)
                    nc.scalar.activation(dwT[:, i % 2, :], t_ps[:, :], ACT.Copy).then_inc(dwT_done, 1)

        @block.sync
        def _(sp):
            if last_layer:
                out = c.dram["out"].rearrange("(n p) d -> p n d", p=P)
                for b in range(NB):
                    sp.wait_ge(added, b + 1)
                    sp.dma_start(out[:, b * BT:(b + 1) * BT, :], c.x[:, b * BT:(b + 1) * BT, :]).then_inc(stored, 16)
                sp.wait_ge(stored, NB * 16)



def softmax_attention(nc, c):
    BSTEPS = Steps(LN_STEPS)
    QT = [(qi, h) for qi in range(BT) for h in range(HG)]
    NU = len(QT)
    with ExitStack() as ctx:
        def sb(name, shape, dt=F32):
            return ctx.enter_context(nc.sbuf_tensor("b_" + name, shape, dt))

        def psum(name):
            return ctx.enter_context(nc.psum_tensor("b_ps_" + name, [P, 512], F32))

        def sem(name):
            return ctx.enter_context(nc.semaphore("b_" + name))

        w, wo = sb("w_qkv", [P, KD, 3 * D]), sb("w_out", [P, KD, D])
        bias, bias_o = sb("bias_qkv", [P, 3 * D]), sb("bias_out", [P, D])
        cos, sin = sb("cos", [P, BT, 2, BD]), sb("sin", [P, BT, 2, BD])
        maskf, maskb, identb = sb("mask_f32", [P, P]), sb("mask", [P, P], BF16), sb("ident_bf16", [P, P], BF16)
        qk, t1, t2 = sb("qk", [P, 2, D]), sb("rope_cos", [P, 2, D]), sb("rope_sin", [P, 2, D])
        qkr = sb("qk_roped", [P, BT, 2, D])
        v = sb("v", [P, BT, D])
        hi = sb("qk_high", [P, 2, BT, HG, BD], F32R)
        stk = sb("stack_tokens", [P, 2, BT, HG, 4, BD], F32R)
        identr = sb("ident_f32r", [P, P], F32R)
        qs, ks = sb("q_stack", [P, 2, S], F32R), sb("k_stack", [P, 2, S], F32R)
        nmax, prob = sb("neg_max", [P, 2, 1]), sb("prob", [P, 2, S])
        rsum, rrec = sb("row_sum", [P, BT, BH]), sb("row_rec", [P, BT, BH])
        pT = sb("probT", [P, 2, S])
        on, oT = sb("out_normalised", [P, 2, D]), sb("outT", [P, KD, P])
        s_ps, p_ps = [psum("scores0"), psum("scores1")], [psum("probT0"), psum("probT1")]
        o_ps = [psum("out0"), psum("out1")]
        k_ps, y_ps = psum("stack"), psum("y")

        ln, loaded, consts = sem("ln_steps"), sem("loaded"), sem("consts")
        qkv_ps, biased, vread = sem("qkv_psum"), sem("biased"), sem("v_read")
        rope_a, rope_done = sem("rope_parts"), sem("rope_done")
        hi_done, stacked, stack_ps, stack_done = sem("high"), sem("stacked"), sem("stack_psum"), sem("stack_done")
        scored, maxed, exped = sem("scored"), sem("maxed"), sem("exped")
        pT_psum, pT_done, out_done = sem("pT_psum"), sem("pT"), sem("out_psum")
        rec, normed, oT_psum, oT_done = sem("rec"), sem("normed"), sem("oT_psum"), sem("oT")
        y_done, biased_o, added = sem("y_psum"), sem("y_bias"), sem("added")

        block = ctx.enter_context(nc.Block())

        def groups(engine, prepare, heads, b):
            prepare(b, 0, 0)
            with engine.Fori(0, NHG // 2 - 1) as t:
                for p in range(2):
                    prepare(b, 2 * t + p + 1, 1 - p)
                    heads(b, 2 * t + p, p)
            prepare(b, NHG - 1, 1)
            heads(b, NHG - 2, 0)
            heads(b, NHG - 1, 1)

        @block.sync
        def _(sp):
            sp.dma_start(w[:, :, :], c.dram["b_w"].rearrange("(k p) n -> p k n", p=P)).then_inc(loaded, 16)
            sp.dma_start(wo[:, :, :], c.dram["b_wo"].rearrange("(k p) n -> p k n", p=P)).then_inc(loaded, 16)
            sp.dma_start(bias[:, :], c.dram["b_bias"].partition_broadcast(P)).then_inc(loaded, 16)
            sp.dma_start(bias_o[:, :], c.dram["b_bias_o"].partition_broadcast(P)).then_inc(loaded, 16)
            sp.dma_start(cos[:, :, :, :].rearrange("p t a d -> p (t a d)"), c.dram["b_cos"]).then_inc(loaded, 16)
            sp.dma_start(sin[:, :, :, :].rearrange("p t a d -> p (t a d)"), c.dram["b_sin"]).then_inc(loaded, 16)
            sp.dma_start(maskf[:, :], c.dram["b_mask"]).then_inc(loaded, 16)

        @block.tensor
        def _(pe):
            def prepare(b, g, par):
                G = b * NHG + g
                for s in range(2):
                    pe.wait_ge(stacked, G + 1)
                    if s == 1 or not (isinstance(g, int) and g == 0):
                        pe.wait_ge(stack_done, 2 * G + s)
                    for i in range(BT):
                        last = nc.tensor.matmul(k_ps[:, i * P:(i + 1) * P].bitcast(F32R),
                                                stk[:, s, i, :, :, :].rearrange("p h a d -> p (h a d)"),
                                                identr[:, :], is_transpose=True, start=True, stop=True)
                    last.then_inc(stack_ps, 1)

            def heads(b, g, par):
                G = b * NHG + g
                pe.wait_ge(stack_done, 2 * G + 2)
                for u in range(NU + 2):
                    if u < NU:
                        qi, h = QT[u]
                        n = G * NU + u
                        N = (qi + 1) * P
                        if not (u < 2):
                            pe.wait_ge(exped, n - 1)
                        rows = slice(h * 32, (h + 1) * 32)
                        nc.tensor.matmul(s_ps[u % 2][:, 0:N], qs[rows, par, qi * P:(qi + 1) * P],
                                         ks[rows, par, 0:N], start=True, stop=False, skip_group_check=True)
                        nc.tensor.matmul(s_ps[u % 2][:, qi * P:N], identb[:, :], maskb[:, :], start=False, stop=True,
                                         skip_group_check=True).then_inc(scored, 1)
                    if 1 <= u <= NU:
                        qi, h = QT[u - 1]
                        n = G * NU + u - 1
                        pe.wait_ge(exped, n + 1)
                        if u - 1 >= 2:
                            pe.wait_ge(pT_done, n - 1)
                        for kj in range(qi + 1):
                            last = nc.tensor.transpose(p_ps[(u - 1) % 2][:, kj * P:(kj + 1) * P],
                                                       prob[:, (u - 1) % 2, kj * P:(kj + 1) * P], c.ident[:, :])
                        last.then_inc(pT_psum, 1)
                    if u >= 2:
                        qi, h = QT[u - 2]
                        n = G * NU + u - 2
                        pe.wait_ge(pT_done, n + 1)
                        head = g * HG + h
                        for kj in range(qi + 1):
                            last = nc.tensor.matmul(o_ps[qi // 2][:, ds((qi % 2) * D + head * BD, BD)],
                                                    pT[:, u % 2, kj * P:(kj + 1) * P],
                                                    v[:, kj, ds(head * BD, BD)], start=(kj == 0), stop=(kj == qi),
                                                    skip_group_check=True)
                        last.then_inc(out_done, 1)

            pe.wait_ge(consts, 4)
            with pe.Fori(0, NB) as b:
                ln_tensor(nc, c, pe, ln, b, s_ps)
                pe.wait_ge(ln, LN.after("xT", b))
                for i in range(BT):
                    if i >= 1:
                        pe.wait_ge(biased, b * BT + i)
                        pe.wait_ge(vread, b * BT + i)
                    for k in range(KD):
                        nc.tensor.matmul(p_ps[0][:, :], c.xT[:, k, i * P:(i + 1) * P], w[:, k, 0:2 * D],
                                         start=(k == 0), stop=(k == KD - 1))
                    for k in range(KD):
                        last = nc.tensor.matmul(p_ps[1][:, 0:D], c.xT[:, k, i * P:(i + 1) * P], w[:, k, 2 * D:3 * D],
                                                start=(k == 0), stop=(k == KD - 1))
                    last.then_inc(qkv_ps, 1)
                pe.wait_ge(vread, (b + 1) * BT)
                groups(pe, prepare, heads, b)
                for i in range(BT):
                    pe.wait_ge(normed, b * BT + i + 1)
                    if i > 0:
                        pe.wait_ge(oT_done, b * BT + i)
                    for k in range(KD):
                        last = nc.tensor.transpose(k_ps[:, k * P:(k + 1) * P], on[:, i % 2, k * P:(k + 1) * P],
                                                   c.ident[:, :])
                    last.then_inc(oT_psum, 1)
                    pe.wait_ge(oT_done, b * BT + i + 1)
                    if i > 0:
                        pe.wait_ge(added, b * BT + i)
                    for k in range(KD):
                        last = nc.tensor.matmul(y_ps[:, 0:D], oT[:, k, :], wo[:, k, :], start=(k == 0),
                                                stop=(k == KD - 1))
                    last.then_inc(y_done, 1)

        @block.vector
        def _(dve):
            def prepare(b, g, par):
                G = b * NHG + g
                if not (isinstance(g, int) and g == 0):
                    dve.wait_ge(stack_ps, 2 * G)
                for s in range(2):
                    src = qkr[:, :, s, ds(g * HG * BD, HG * BD)].rearrange("p t (h d) -> p t h d", h=HG)
                    last = nc.vector.tensor_copy(hi[:, s, :, :, :], src)
                last.then_inc(hi_done, 1)
                dve.wait_ge(hi_done, G + 1)
                for s in range(2):
                    src = qkr[:, :, s, ds(g * HG * BD, HG * BD)].rearrange("p t (h d) -> p t h d", h=HG)
                    top = hi[:, s, :, :, :]
                    highs, lows = ((0, 1), (2, 3)) if s == 0 else ((0, 2), (1, 3))
                    for a in highs:
                        nc.vector.tensor_copy(stk[:, s, :, :, a, :], top)
                    for a in lows:
                        last = nc.vector.tensor_tensor(stk[:, s, :, :, a, :], src, top.bitcast(F32), ALU.subtract)
                last.then_inc(stacked, 1)

            def heads(b, g, par):
                G = b * NHG + g
                for u in range(NU + 1):
                    if u < NU:
                        qi, h = QT[u]
                        n = G * NU + u
                        dve.wait_ge(scored, n + 1)
                        if u >= 2:
                            dve.wait_ge(exped, n - 1)
                        nc.vector.reduce_max(nmax[:, u % 2, :], s_ps[u % 2][:, 0:(qi + 1) * P], AX, negate=True)\
                            .then_inc(maxed, 1)
                    if u >= 1:
                        qi, h = QT[u - 1]
                        n = G * NU + u - 1
                        dve.wait_ge(pT_psum, n + 1)
                        if u - 1 >= 2:
                            dve.wait_ge(out_done, n - 1)
                        nc.vector.tensor_copy(pT[:, (u - 1) % 2, 0:(qi + 1) * P],
                                              p_ps[(u - 1) % 2][:, 0:(qi + 1) * P]).then_inc(pT_done, 1)

            dve.wait_ge(loaded, 16 * 7)
            nc.vector.tensor_copy(maskb[:, :], maskf[:, :]).then_inc(consts, 1)
            nc.vector.tensor_copy(identb[:, :], c.ident[:, :]).then_inc(consts, 1)
            nc.vector.tensor_copy(identr[:, :], c.ident[:, :]).then_inc(consts, 2)
            with dve.Fori(0, NB) as b:
                ln_vector(nc, c, dve, ln, b, b)
                for i in range(BT):
                    n = b * BT + i
                    dve.wait_ge(qkv_ps, n + 1)
                    nc.vector.tensor_tensor(qk[:, :, :].rearrange("p a d -> p (a d)"), p_ps[0][:, :],
                                            bias[:, 0:2 * D], ALU.add).then_inc(biased, 1)
                    nc.vector.tensor_tensor(v[:, i, :], p_ps[1][:, 0:D], bias[:, 2 * D:], ALU.add).then_inc(vread, 1)
                    dve.wait_ge(biased, n + 1)
                    H2 = BD // 2
                    for s in range(2):
                        q4 = qk[:, s, :].rearrange("p (h d) -> p h d", d=BD)
                        a4, b4 = (t[:, s, :].rearrange("p (h d) -> p h d", d=BD) for t in (t1, t2))
                        full, half = [P, BH, BD], [P, BH, H2]
                        nc.vector.tensor_tensor(a4, q4, cos[:, i, s, :].unsqueeze(1).to_broadcast(full), ALU.mult)
                        nc.vector.tensor_tensor(b4[:, :, 0:H2], q4[:, :, H2:BD],
                                                sin[:, i, s, 0:H2].unsqueeze(1).to_broadcast(half), ALU.mult)
                        last = nc.vector.tensor_tensor(b4[:, :, H2:BD], q4[:, :, 0:H2],
                                                       sin[:, i, s, H2:BD].unsqueeze(1).to_broadcast(half), ALU.mult)
                    last.then_inc(rope_a, 1)
                    dve.wait_ge(rope_a, n + 1)
                    nc.vector.tensor_tensor(qkr[:, i, :, :], t1[:, :, :], t2[:, :, :], ALU.add).then_inc(rope_done, 1)
                dve.wait_ge(rope_done, (b + 1) * BT)
                groups(dve, prepare, heads, b)
                dve.wait_ge(exped, (b + 1) * NHG * NU)
                nc.vector.reciprocal(rrec[:, :, :], rsum[:, :, :]).then_inc(rec, 1)
                dve.wait_ge(rec, b + 1)
                dve.wait_ge(out_done, (b + 1) * NHG * NU)
                for i in range(BT):
                    n = b * BT + i
                    o4 = o_ps[i // 2][:, (i % 2) * D:(i % 2 + 1) * D].rearrange("p (h d) -> p h d", d=BD)
                    if i >= 2:
                        dve.wait_ge(oT_psum, n - 1)
                    nc.vector.tensor_tensor(on[:, i % 2, :].rearrange("p (h d) -> p h d", d=BD), o4,
                                            rrec[:, i, :].unsqueeze(2).to_broadcast([P, BH, BD]), ALU.mult)\
                        .then_inc(normed, 1)
                for i in range(BT):
                    n = b * BT + i
                    xs = c.x[:, ds(n, 1), :].rearrange("p a d -> p (a d)")
                    nc.vector.tensor_tensor(xs, xs, bias_o[:, :], ALU.add).then_inc(biased_o, 1)
                    dve.wait_ge(biased_o, n + 1)
                    dve.wait_ge(y_done, n + 1)
                    nc.vector.tensor_tensor(xs, xs, y_ps[:, 0:D], ALU.add).then_inc(added, 1)
                dve.wait_ge(added, (b + 1) * BT)

        @block.scalar
        def _(act):
            def prepare(b, g, par):
                G = b * NHG + g
                for s, dst in ((0, qs), (1, ks)):
                    act.wait_ge(stack_ps, 2 * G + s + 1)
                    nc.scalar.activation(dst[:, par, :], k_ps[:, :], ACT.Copy).then_inc(stack_done, 1)

            def heads(b, g, par):
                G = b * NHG + g
                for u in range(NU):
                    qi, h = QT[u]
                    n = G * NU + u
                    act.wait_ge(maxed, n + 1)
                    if u >= 2:
                        act.wait_ge(pT_psum, n - 1)
                    nc.scalar.activation(prob[:, u % 2, 0:(qi + 1) * P], s_ps[u % 2][:, 0:(qi + 1) * P], ACT.Exp,
                                         bias=nmax[:, u % 2, :], accum_out=rsum[:, qi, ds(g * HG + h, 1)])\
                        .then_inc(exped, 1)

            with act.Fori(0, NB) as b:
                ln_scalar(nc, c, act, ln, b, s_ps)
                groups(act, prepare, heads, b)
                for i in range(BT):
                    act.wait_ge(oT_psum, b * BT + i + 1)
                    if i > 0:
                        act.wait_ge(y_done, b * BT + i)
                    nc.scalar.activation(oT[:, :, :].rearrange("p k t -> p (k t)"), k_ps[:, 0:D], ACT.Copy)\
                        .then_inc(oT_done, 1)


def build(nc, dram):
    with ExitStack() as ctx:
        c = Chip()
        resident(nc, ctx, c, dram)
        linear_attention(nc, c)
        expert_weights(nc, c)
        experts(nc, c, "f0_", False)
        softmax_attention(nc, c)
        experts(nc, c, "f1_", True)


def _layouts(np, a):
    f4 = np.float32

    def t(x):
        return np.ascontiguousarray(np.asarray(x).T)

    get = {k: np.asarray(v) for k, v in a.items()}
    d = {"x": get["L0_attn_a_x"].reshape(NB * S, D)}
    d["a_w"] = np.concatenate([t(get["L0_attn_a_W" + n]) for n in "qkv"], axis=1)
    d["a_wo"] = t(get["L0_attn_a_Wo"])
    d["b_w"] = np.concatenate([t(get["L0_attn_b_W" + n]) for n in "qkv"], axis=1)
    d["b_wo"] = t(get["L0_attn_b_Wo"])
    d["b_bias"] = np.concatenate([get["L0_attn_b_b" + n] for n in "qkv"])
    d["b_bias_o"] = get["L0_attn_b_bo"]
    f = {k[7:]: v for k, v in get.items() if k.startswith("L0_ffn_")}
    d["wrt"] = t(f["gate_weight"])
    d["mapping"] = f["inv_mapping"].reshape(NE)
    w1 = np.concatenate([f["gate_W"], f["up_W"], f["gate_qa"].reshape(EX, KR, D), f["up_qa"].reshape(EX, KR, D)], axis=1)
    d["w1"] = np.ascontiguousarray(w1.transpose(2, 0, 1).reshape(D, EX * W1N))
    w2 = np.concatenate([f["down_W"].transpose(0, 2, 1), f["down_qa"].reshape(EX, KR, EI).transpose(0, 2, 1)], axis=2)
    d["w2"] = np.ascontiguousarray(w2.transpose(1, 0, 2).reshape(EI, EX * W2N))
    qb = [f[n].transpose(0, 1, 3, 2).reshape(EX, KR, EI) for n in ("gate_qb", "up_qb")]
    d["qb"] = np.ascontiguousarray(np.concatenate(qb, axis=2).transpose(1, 0, 2).reshape(KR, EX * 2 * EI))
    d["scale_gu"] = np.concatenate([f["gate_scale"], f["up_scale"]], axis=1).reshape(EX * 2 * EI)
    d["qbd"] = np.ascontiguousarray(f["down_qb"].transpose(0, 1, 3, 2).reshape(EX * KR, D))
    d["scale_d"] = f["down_scale"]
    d["mu"] = np.ascontiguousarray(f["mask_up_W"].transpose(1, 0, 2).reshape(D, NE))
    mup = np.zeros((D, EX, NE), f["mask_up_W"].dtype)
    for e in range(EX):
        mup[:, e, e * EK:(e + 1) * EK] = f["mask_up_W"][e]
    d["mup"] = mup.reshape(D, EX * NE)
    d["shgu"] = np.concatenate([t(f["sh_gate_W"]), t(f["sh_up_W"])], axis=1)
    d["shd"] = t(f["sh_down_W"])
    d["ident"] = np.eye(P, dtype=f4)
    d["row"] = np.arange(NE, dtype=f4).reshape(NE, 1)
    pos = np.arange(P)
    d["a_mask"] = (pos[:, None] <= pos[None, :]).astype(f4)
    d["b_mask"] = np.where(pos[:, None] >= pos[None, :], 0.0, NEG).astype(f4)
    inv = (f4(1.0) / f4(10000.0) ** (np.arange(0, HD, 2, dtype=f4) / f4(HD))).astype(f4)
    ang = np.outer(np.arange(S, dtype=f4), inv).astype(f4).T
    d["a_cos"] = np.concatenate([np.cos(ang), np.cos(ang)]).astype(f4)
    d["a_sin"] = np.concatenate([np.sin(ang), -np.sin(ang)]).astype(f4)
    theta = (f4(10000.0) ** (-np.arange(0, BD, 2, dtype=f4) / f4(BD))).astype(f4)
    frame = np.floor((np.arange(S) // 72).astype(f4) * 0.5)
    ang = (np.arange(S, dtype=f4)[:, None] * theta).astype(np.float64) + (frame.astype(f4)[:, None] * theta)
    co, si = np.cos(ang), np.sin(ang)
    for name, tab in (("b_cos", np.concatenate([co, co], 1)), ("b_sin", np.concatenate([-si, si], 1))):
        both = np.stack([tab / np.sqrt(BD), tab], axis=1).astype(f4)
        d[name] = np.ascontiguousarray(both.reshape(BT, P, 2 * BD).transpose(1, 0, 2).reshape(P, BT * 2 * BD))
    return d


def kernel(**inputs):
    import numpy as np
    import concourse.bacc as bacc
    from concourse.bass_utils import run_bass_kernel_spmd

    nc = bacc.Bacc("TRN2", target_bir_lowering=False, num_devices=1)
    arrays, dram = {}, {}
    for name, a in _layouts(np, inputs).items():
        arrays[f"in_{name}"] = np.ascontiguousarray(a)
        dram[name] = nc.dram_tensor(f"in_{name}", a.shape, mybir.dt.from_np(a.dtype), kind="ExternalInput").ap()
    dram["out"] = nc.dram_tensor("out_0", (NB * S, D), F32, kind="ExternalOutput").ap()
    build(nc, dram)
    r = run_bass_kernel_spmd(nc, [arrays], core_ids=[0])
    return r.results[0]["out_0"].reshape(NB, S, D)
```

```python
from contextlib import ExitStack

import concourse.bass as bass
from concourse import mybir

F32 = mybir.dt.float32
F32R = mybir.dt.float32r
BF16 = mybir.dt.bfloat16
I32 = mybir.dt.int32
ALU = mybir.AluOpType
ACT = mybir.ActivationFunctionType
AX = mybir.AxisListType.X
ds = bass.ds

P = 128
D = 256
KD = D // P
NB = 4
BT = 4
S = BT * P
LN_EPS = 1e-5

AH, AG, HD = 16, 4, 128
REP = AH // AG
A_EPS = 1e-6
BH, BD = 32, 8
HG = 4
NHG = BH // HG
NEG = -1e30
EX, EK, ER, EI = 8, 8, 8, 176
NE = EX * EK
KR = EK * ER
TOPK = 6
HJ = EI // 2
W1N = 2 * EI + 2 * KR
W2N = D + KR
SH = 2 * EI
SHC = [(0, 128), (128, 128), (256, SH - 256)]

LN_STEPS = ["stats", "aggregate", "var_eps", "std", "rstd", "normalised", "xT_psum", "xT"]
ROUTER_STEPS = ["logits", "row_max", "shifted", "exp", "exp_sum", "exp_rec", "probs", "top8", "top6",
                "others", "w_dense", "w_denseT_psum", "w_denseT", "flat_psum", "flat", "scalar", "penalty",
                "masked", "group_max", "group_shifted", "group_exp", "group_sum", "group_rec", "soft",
                "softT_psum", "softT"]


class Steps:

    def __init__(self, names):
        self.names = names

    def after(self, name, rounds=0):
        return rounds * len(self.names) + self.names.index(name) + 1


class Chip:
    pass


def resident(nc, ctx, c, dram):
    def sb(name, shape, dt=F32):
        return ctx.enter_context(nc.sbuf_tensor(name, shape, dt))

    c.dram = dram
    c.x = sb("x_resident", [P, NB * BT, D])
    c.xT = sb("xT", [P, KD, S])
    c.ident = sb("ident", [P, P])
    c.w1 = sb("w1", [P, KD, EX * W1N])
    c.w2 = sb("w2", [HJ, 2, EX * W2N])
    c.qb = sb("qb_gate_up", [KR + EK, EX * 2 * EI])
    c.qbd = sb("qb_down", [P, EX // 2, D])
    c.ma = sb("mask_up_low_rank", [NE, EX * 2 * KR])
    c.shgu = sb("shared_gate_up", [P, KD, 2 * SH])
    c.shd = sb("shared_down", [P, 3, D])
    c.wrt = sb("router_w", [P, KD, NE])
    c.onehot = sb("onehot", [NE, NE])
    c.xn = sb("x_normalised", [P, BT, D])
    c.ln_stats = sb("ln_stats", [P, BT, 6])
    c.ln_mv = sb("ln_mean_var", [P, BT, 2])
    c.ln_ve = sb("ln_var_eps", [P, BT])
    c.ln_std = sb("ln_std", [P, BT])
    c.ln_rstd = sb("ln_rstd", [P, BT])
    c.x_loaded = ctx.enter_context(nc.semaphore("x_loaded"))
    c.a_loaded = ctx.enter_context(nc.semaphore("first_loaded"))
    c.waits_met = ctx.enter_context(nc.semaphore("waits_met"))
    c.f_loaded = ctx.enter_context(nc.semaphore("f_loaded"))


def load_x(c, sp):
    xv = c.dram["x"].rearrange("(n p) d -> p n d", p=P)
    sp.dma_start(c.x[:, 0:BT, :], xv[:, 0:BT, :]).then_inc(c.x_loaded, 16)
    sp.dma_start(c.ident[:, :], c.dram["ident"]).then_inc(c.x_loaded, 16)


def load_rest_of_x(c, sp):
    xv = c.dram["x"].rearrange("(n p) d -> p n d", p=P)
    sp.dma_start(c.x[:, BT:, :], xv[:, BT:, :]).then_inc(c.a_loaded, 16)


def load_expert_weights(c, sp):
    sp.dma_start(c.w1[:, :, :], c.dram["w1"].rearrange("(k p) n -> p k n", p=P)).then_inc(c.f_loaded, 16)
    sp.dma_start(c.w2[:, :, :], c.dram["w2"].rearrange("(j p) n -> p j n", p=HJ)).then_inc(c.f_loaded, 16)
    sp.dma_start(c.qb[0:KR, :], c.dram["qb"]).then_inc(c.f_loaded, 16)
    sp.dma_start(c.qbd[:, :, :], c.dram["qbd"].rearrange("(q p) n -> p q n", p=P)).then_inc(c.f_loaded, 16)
    sp.dma_start(c.shgu[:, :, :], c.dram["shgu"].rearrange("(k p) n -> p k n", p=P)).then_inc(c.f_loaded, 16)
    for j, (lo, n) in enumerate(SHC):
        sp.dma_start(c.shd[0:n, j, :], c.dram["shd"][lo:lo + n, :]).then_inc(c.f_loaded, 16)
    sp.dma_start(c.wrt[:, :, :], c.dram["wrt"].rearrange("(k p) n -> p k n", p=P)).then_inc(c.f_loaded, 16)
    sp.wait_ge(c.f_loaded, 16 * 9)


def apart(engine, c):
    engine.sem_inc(c.waits_met, 1)



LN = Steps(LN_STEPS)


def ln_vector(nc, c, dve, sem, blk, rounds, t=LN):
    for i in range(BT):
        last = nc.vector.bn_stats(c.ln_stats[:, i, :], c.x[:, ds(blk * BT + i, 1), :].rearrange("p a d -> p (a d)"))
    last.then_inc(sem, 1)
    dve.wait_ge(sem, t.after("stats", rounds))
    apart(dve, c)
    for i in range(BT):
        last = nc.vector.bn_aggr(c.ln_mv[:, i, :], c.ln_stats[:, i, :])
    last.then_inc(sem, 1)
    dve.wait_ge(sem, t.after("aggregate", rounds))
    nc.vector.tensor_scalar(c.ln_ve[:, :], c.ln_mv[:, :, 1], LN_EPS, None, ALU.add).then_inc(sem, 1)
    dve.wait_ge(sem, t.after("std", rounds))
    nc.vector.reciprocal(c.ln_rstd[:, :], c.ln_std[:, :]).then_inc(sem, 1)
    dve.wait_ge(sem, t.after("rstd", rounds))
    for i in range(BT):
        last = nc.vector.tensor_scalar(c.xn[:, i, :], c.x[:, ds(blk * BT + i, 1), :].rearrange("p a d -> p (a d)"),
                                       c.ln_mv[:, i, 0:1], c.ln_rstd[:, i:i + 1], ALU.subtract, ALU.mult)
    last.then_inc(sem, 1)


def ln_scalar(nc, c, act, sem, rounds, banks, t=LN):
    act.wait_ge(sem, t.after("var_eps", rounds))
    nc.scalar.activation(c.ln_std[:, :], c.ln_ve[:, :], ACT.Sqrt).then_inc(sem, 1)
    act.wait_ge(sem, t.after("xT_psum", rounds))
    for k in range(KD):
        last = nc.scalar.activation(c.xT[:, k, :], banks[k][:, :], ACT.Copy)
    last.then_inc(sem, 1)


def ln_tensor(nc, c, pe, sem, rounds, banks, t=LN):
    pe.wait_ge(sem, t.after("normalised", rounds))
    for k in range(KD):
        for i in range(BT):
            last = nc.tensor.transpose(banks[k][:, i * P:(i + 1) * P], c.xn[:, i, k * P:(k + 1) * P], c.ident[:, :])
    last.then_inc(sem, 1)



def linear_attention(nc, c):
    ITEMS = REP + 2
    SLOTS = [[0, 1], [2], [3, 4], [5]]
    with ExitStack() as ctx:
        def sb(name, shape, dt=F32):
            return ctx.enter_context(nc.sbuf_tensor("a_" + name, shape, dt))

        def psum(name):
            return ctx.enter_context(nc.psum_tensor("a_ps_" + name, [P, 512], F32))

        def sem(name):
            return ctx.enter_context(nc.semaphore("a_" + name))

        w = sb("w_qkv", [P, KD, (AH + 2 * AG) * HD])
        wo = sb("w_out", [P, AH, D])
        cos, sin = sb("cos", [P, S]), sb("sin_crossed", [P, S])
        mask = sb("mask", [P, P])
        qf, kf = sb("q_features", [P, 2, REP, S]), sb("k_features", [P, 2, S])
        kt, v = sb("k_tokens", [P, 2, BT, HD]), sb("v_tokens_ones", [P, 2, BT, HD + 1])
        t1, t2 = sb("roped", [P, 2, S]), sb("rope_sin", [P, 2, S])
        en = sb("exp_neg", [P, 2, S])
        sc = sb("masked_scores", [P, REP, P])
        den, rden = sb("den", [P, 2, REP // 2, 1]), sb("rden", [P, 2, REP // 2, 1])
        st = sb("state", [P, 2, HD + 1])
        ot = sb("out_tokens", [P, 2, REP // 2, HD])
        o = sb("out_features", [P, 2, REP, P])
        y = [psum("y0"), psum("y1")]
        pj = [psum("proj0"), psum("proj1")]
        s_ps, st_ps = psum("scores_outT"), psum("state_kT")
        o_ps = ctx.enter_context(nc.psum_tensor("a_ps_out", [P, 2, 512], F32))
        o4 = o_ps[:, :, 0:REP // 2 * (HD + 1)].rearrange("p a (h d) -> p a h d", d=HD + 1)

        ln = sem("ln_steps")
        ones_set = sem("ones_set")
        projected = sem("projected")
        v_read, roped = sem("v_read"), sem("roped")
        summed, neg_part, exp_neg, featured = sem("summed"), sem("neg_part"), sem("exp_neg"), sem("featured")
        kT_psum, kT_read = sem("kT_psum"), sem("kT_read")
        scored, masked = sem("scored"), sem("masked")
        out_psum, den_read, rden_done, normed = sem("out_psum"), sem("den_read"), sem("rden_done"), sem("normed")
        outT_psum = sem("outT_psum")
        st_psum, st_read = sem("state_psum"), sem("state_read")
        out_done, added_psum, added = sem("out_done"), sem("y_psum"), sem("added")

        def kx(G):
            return G * (REP + 1)

        block = ctx.enter_context(nc.Block())

        @block.sync
        def _(sp):
            load_x(c, sp)
            wv = c.dram["a_w"].rearrange("(k p) n -> p k n", p=P)
            sp.dma_start(w[:, :, :], wv).then_inc(c.a_loaded, 16)
            sp.dma_start(cos[:, :], c.dram["a_cos"]).then_inc(c.a_loaded, 16)
            sp.dma_start(sin[:, :], c.dram["a_sin"]).then_inc(c.a_loaded, 16)
            sp.dma_start(mask[:, :], c.dram["a_mask"]).then_inc(c.a_loaded, 16)
            load_rest_of_x(c, sp)
            sp.dma_start(wo[:, :, :], c.dram["a_wo"].rearrange("(h p) n -> p h n", p=P)).then_inc(c.a_loaded, 16)
            load_expert_weights(c, sp)

        @block.tensor
        def _(pe):
            def project(b, g, m, first):
                G = b * AG + g
                if not (first and m < 2):
                    if m == 0 or m == 1:
                        pe.wait_ge(roped, kx(G) - 2 + m + 1)
                    elif m == 2:
                        pe.wait_ge(v_read, G + 1)
                    else:
                        pe.wait_ge(roped, kx(G) + m - 2)
                bank = pj[m % 2]
                if m == 0:
                    lo = (AH + AG + g) * HD
                    for i in range(BT):
                        for k in range(KD):
                            last = nc.tensor.matmul(bank[:, i * HD:(i + 1) * HD], c.xT[:, k, i * P:(i + 1) * P],
                                                    w[:, k, lo:lo + HD], start=(k == 0), stop=(k == KD - 1))
                else:
                    lo = (AH + g if m == 1 else g * REP + m - 2) * HD
                    for k in range(KD):
                        last = nc.tensor.matmul(bank[:, :], w[:, k, lo:lo + HD], c.xT[:, k, :],
                                                start=(k == 0), stop=(k == KD - 1))
                last.then_inc(projected, 1)

            def transpose_k(b, g):
                G = b * AG + g
                pe.wait_ge(featured, kx(G) + 1)
                for i in range(BT):
                    last = nc.tensor.transpose(st_ps[:, i * P:(i + 1) * P], kf[:, g % 2, i * P:(i + 1) * P],
                                               c.ident[:, :])
                last.then_inc(kT_psum, 1)

            def scores(b, g, ch):
                G = b * AG + g
                if ch == 0:
                    pe.wait_ge(featured, kx(G + 1))
                    pe.wait_ge(kT_read, G + 1)
                    pe.wait_ge(v_read, G + 1)
                if not (ch == 0 and g == 0):
                    pe.wait_ge(out_done, G * BT + ch)
                nc.tensor.matmul(s_ps[:, :], kf[:, g % 2, ch * P:(ch + 1) * P], qf[:, g % 2, :, ch * P:(ch + 1) * P],
                                 start=True, stop=True).then_inc(scored, 1)

            def outputs(b, g, ch):
                G = b * AG + g
                n = G * BT + ch
                pe.wait_ge(masked, n + 1)
                if not (ch == 0 and g == 0):
                    pe.wait_ge(normed, n)
                if ch > 0:
                    pe.wait_ge(st_read, G * (BT - 1) + ch)
                for h in range(REP):
                    bank = o4[:, h // 2, h % 2, :]
                    if ch > 0:
                        nc.tensor.matmul(bank, qf[:, g % 2, h, ch * P:(ch + 1) * P], st[:, (ch - 1) % 2, :],
                                         start=True, stop=False)
                    last = nc.tensor.matmul(bank, sc[:, h, :], v[:, g % 2, ch, :], start=(ch == 0), stop=True)
                last.then_inc(out_psum, 1)

            def transpose_out(b, n):
                pe.wait_ge(normed, b * AG * BT + n + 1)
                for h in range(REP):
                    last = nc.tensor.transpose(s_ps[:, h * P:(h + 1) * P], ot[:, h // 2, h % 2, :], c.ident[:, :])
                last.then_inc(outT_psum, 1)

            def state(b, g, ch):
                G = b * AG + g
                if ch > 0:
                    pe.wait_ge(st_read, G * (BT - 1) + ch)
                nc.tensor.matmul(st_ps[:, 0:HD + 1], kt[:, g % 2, ch, :], v[:, g % 2, ch, :],
                                 start=(ch == 0), stop=True, skip_group_check=True).then_inc(st_psum, 1)

            def add_out(b, n, heads):
                g, ch = n // BT, n % BT
                if heads[0] == 0:
                    pe.wait_ge(out_done, b * AG * BT + n + 1)
                for h in heads:
                    last = nc.tensor.matmul(y[ch // 2][:, (ch % 2) * D:(ch % 2 + 1) * D], o[:, ch % 2, h, :],
                                            wo[:, g * REP + h, :], start=(g == 0 and h == 0 and ch % 2 == 0),
                                            stop=(g == AG - 1 and h == REP - 1), skip_group_check=True)
                if heads[-1] == REP - 1:
                    last.then_inc(added_psum, 1)

            pe.wait_ge(c.a_loaded, 16 * 6)
            with pe.Fori(0, NB) as b:
                ln_tensor(nc, c, pe, ln, b, pj)
                pe.wait_ge(ln, LN.after("xT", b))
                for m in range(ITEMS):
                    project(b, 0, m, True)
                transpose_k(b, 0)
                for g in range(AG):
                    for ch in range(BT):
                        n = g * BT + ch
                        items = SLOTS[ch] if g + 1 < AG else []
                        for m in items[0:1]:
                            project(b, g + 1, m, False)
                        if n >= 1:
                            transpose_out(b, n - 1)
                        for m in items[1:]:
                            project(b, g + 1, m, False)
                        if n >= 2:
                            add_out(b, n - 2, [0, 1])
                        scores(b, g, ch)
                        if n >= 2:
                            add_out(b, n - 2, [2, 3])
                        if ch < BT - 1:
                            state(b, g, ch)
                        outputs(b, g, ch)
                    if g + 1 < AG:
                        pe.wait_ge(st_read, (b * AG + g + 1) * (BT - 1))
                        transpose_k(b, g + 1)
                n = AG * BT
                add_out(b, n - 2, [0, 1, 2, 3])
                transpose_out(b, n - 1)
                add_out(b, n - 1, [0, 1, 2, 3])

        @block.vector
        def _(dve):
            def rope(b, g, m):
                G = b * AG + g
                j = m - 1
                r = m % 2
                dve.wait_ge(projected, G * ITEMS + m + 1)
                if not (g == 0 and j < 2):
                    dve.wait_ge(featured, kx(G) + max(j - 1, 0))
                nc.vector.tensor_tensor(t1[:, r, :], pj[r][:, :], cos[:, :], ALU.mult)
                nc.vector.tensor_tensor(t2[0:64, r, :], pj[r][64:128, :], sin[64:128, :], ALU.mult)
                nc.vector.tensor_tensor(t2[64:128, r, :], pj[r][0:64, :], sin[0:64, :], ALU.mult)\
                    .then_inc(roped, 1)

            def feature(b, g, m):
                G = b * AG + g
                j = m - 1
                r = m % 2
                dve.wait_ge(exp_neg, kx(G) + j + 1)
                dst = kf[:, g % 2, :] if m == 1 else qf[:, g % 2, m - 2, :]
                nc.vector.scalar_tensor_tensor(out=dst, in0=t1[:, r, :], scalar=0.0, in1=en[:, r, :],
                                               op0=ALU.max, op1=ALU.add).then_inc(featured, 1)

            def mask_scores(b, g, ch):
                n = (b * AG + g) * BT + ch
                dve.wait_ge(scored, n + 1)
                if not (g == 0 and ch == 0):
                    dve.wait_ge(out_psum, n)
                nc.vector.tensor_tensor(sc[:, :, :], s_ps[:, :].rearrange("p (h t) -> p h t", h=REP),
                                        mask[:, :].unsqueeze(1).to_broadcast([P, REP, P]), ALU.mult)\
                    .then_inc(masked, 1)

            def divide(b, g, ch):
                n = (b * AG + g) * BT + ch
                dve.wait_ge(out_psum, n + 1)
                nc.vector.tensor_scalar(den[:, :, :, :], o4[:, :, :, HD:HD + 1], A_EPS, None, ALU.add)\
                    .then_inc(den_read, 1)
                dve.wait_ge(den_read, n + 1)
                nc.vector.reciprocal(rden[:, :, :, :], den[:, :, :, :]).then_inc(rden_done, 1)
                dve.wait_ge(rden_done, n + 1)
                nc.vector.tensor_tensor(ot[:, :, :, :], o4[:, :, :, 0:HD],
                                        rden[:, :, :, :].to_broadcast([P, 2, REP // 2, HD]), ALU.mult)\
                    .then_inc(normed, 1)

            nc.vector.memset(v[:, :, :, HD:HD + 1], 1.0).then_inc(ones_set, 1)
            dve.wait_ge(c.a_loaded, 16 * 6)
            dve.wait_ge(c.x_loaded, 32)
            dve.wait_ge(ones_set, 1)
            with dve.Fori(0, NB) as b:
                ln_vector(nc, c, dve, ln, b, b)
                for m in range(1, ITEMS):
                    rope(b, 0, m)
                    if m > 1:
                        feature(b, 0, m - 1)
                feature(b, 0, ITEMS - 1)
                for g in range(AG):
                    pending = None
                    for ch in range(BT):
                        if g + ch > 0:
                            divide(b, g - (ch == 0), (ch - 1) % BT)
                        for m in SLOTS[ch] if g + 1 < AG else []:
                            if m == 0:
                                continue
                            rope(b, g + 1, m)
                            if pending:
                                feature(b, g + 1, pending)
                            pending = m
                        mask_scores(b, g, ch)
                    if pending:
                        feature(b, g + 1, pending)
                divide(b, AG - 1, BT - 1)
                dve.wait_ge(added_psum, (b + 1) * AG * BT)
                for i in range(2):
                    xs = c.x[:, ds(b * BT + 2 * i, 2), :]
                    last = nc.vector.tensor_tensor(xs, xs, y[i][:, :].rearrange("p (a d) -> p a d", a=2), ALU.add)
                last.then_inc(added, 1)
                dve.wait_ge(added, b + 1)

        @block.gpsimd
        def _(pool):
            def add_rope(b, g, m):
                G = b * AG + g
                j = m - 1
                r = m % 2
                pool.wait_ge(roped, kx(G) + j + 1)
                nc.gpsimd.tensor_tensor(t1[:, r, :], t1[:, r, :], t2[:, r, :], ALU.add).then_inc(summed, 1)

            with pool.Fori(0, NB) as b:
                for m in range(1, ITEMS):
                    add_rope(b, 0, m)
                for g in range(AG):
                    if g + 1 < AG:
                        for m in range(1, ITEMS):
                            add_rope(b, g + 1, m)

        @block.scalar
        def _(act):
            def read_v(b, g):
                G = b * AG + g
                act.wait_ge(projected, G * ITEMS + 1)
                nc.scalar.activation(v[:, g % 2, :, 0:HD], pj[0][:, :].rearrange("p (t d) -> p t d", t=BT), ACT.Copy)\
                    .then_inc(v_read, 1)

            def exp_negative(b, g, m):
                G = b * AG + g
                j = m - 1
                r = m % 2
                act.wait_ge(summed, kx(G) + j + 1)
                if not (g == 0 and j < 2):
                    act.wait_ge(featured, kx(G) + max(j - 1, 0))
                nc.scalar.activation(en[:, r, :], t1[:, r, :], ACT.Relu, scale=-1.0).then_inc(neg_part, 1)
                act.wait_ge(neg_part, kx(G) + j + 1)
                nc.scalar.activation(en[:, r, :], en[:, r, :], ACT.Exp, scale=-1.0).then_inc(exp_neg, 1)

            def read_k(b, g):
                act.wait_ge(kT_psum, b * AG + g + 1)
                nc.scalar.activation(kt[:, g % 2, :, :].rearrange("p t d -> p (t d)"), st_ps[:, :], ACT.Copy)\
                    .then_inc(kT_read, 1)

            def read_state(b, g, ch):
                G = b * AG + g
                act.wait_ge(st_psum, G * (BT - 1) + ch + 1)
                nc.scalar.activation(st[:, ch % 2, :], st_ps[:, 0:HD + 1], ACT.Copy).then_inc(st_read, 1)

            def read_out(b, n):
                act.wait_ge(outT_psum, b * AG * BT + n + 1)
                nc.scalar.activation(o[:, n % 2, :, :].rearrange("p h t -> p (h t)"), s_ps[:, :], ACT.Copy)\
                    .then_inc(out_done, 1)

            act.wait_ge(ones_set, 1)
            with act.Fori(0, NB) as b:
                ln_scalar(nc, c, act, ln, b, pj)
                read_v(b, 0)
                for m in range(1, ITEMS):
                    exp_negative(b, 0, m)
                read_k(b, 0)
                for g in range(AG):
                    for ch in range(BT):
                        items = SLOTS[ch] if g + 1 < AG else []
                        if 0 in items:
                            read_v(b, g + 1)
                        if g + ch > 0:
                            read_out(b, g * BT + ch - 1)
                        if ch < BT - 1:
                            read_state(b, g, ch)
                        for m in items:
                            if m > 0:
                                exp_negative(b, g + 1, m)
                    if g + 1 < AG:
                        read_k(b, g + 1)
                read_out(b, AG * BT - 1)



def expert_weights(nc, c):
    with ExitStack() as ctx:
        def sb(name, shape, dt=F32):
            return ctx.enter_context(nc.sbuf_tensor("e_" + name, shape, dt))

        def sem(name):
            return ctx.enter_context(nc.semaphore("e_" + name))

        scale_gu = sb("scale_gate_up", [KR, EX * 2 * EI])
        scale_d = sb("scale_down", [P, EX // 2, D])
        mu = sb("mask_up", [P, KD, NE])
        mup = sb("mask_up_padded", [P, KD, EX * NE])
        idx, idxf = sb("mapping", [NE, NE], I32), sb("mapping_f32", [NE, NE])
        row = sb("row_number", [NE, 1])
        ps = [ctx.enter_context(nc.psum_tensor(f"e_ps{i}", [P, 512], F32)) for i in range(4)]
        loaded, gu_ready, ma_ready = sem("loaded"), sem("gu_psum"), sem("ma_psum")
        gu_read, ma_read, small = sem("gu_read"), sem("ma_read"), sem("small")
        block = ctx.enter_context(nc.Block())

        @block.sync
        def _(sp):
            sp.dma_start(scale_gu[:, :], c.dram["scale_gu"].partition_broadcast(KR)).then_inc(loaded, 16)
            for f in range(EX):
                sp.dma_start(scale_d[(f % 2) * KR:(f % 2 + 1) * KR, f // 2, :],
                             c.dram["scale_d"][f, :].partition_broadcast(KR)).then_inc(loaded, 16)
            sp.dma_start(mu[:, :, :], c.dram["mu"].rearrange("(k p) n -> p k n", p=P)).then_inc(loaded, 16)
            sp.dma_start(mup[:, :, :], c.dram["mup"].rearrange("(k p) n -> p k n", p=P)).then_inc(loaded, 16)
            sp.dma_start(idx[:, :], c.dram["mapping"].partition_broadcast(NE)).then_inc(loaded, 16)
            sp.dma_start(row[:, :], c.dram["row"]).then_inc(loaded, 16)

        @block.tensor
        def _(pe):
            pe.wait_ge(loaded, 16 * 13)
            for f in range(EX):
                if f >= 2:
                    pe.wait_ge(gu_read, f - 1)
                    pe.wait_ge(ma_read, f - 1)
                for k in range(KD):
                    last = nc.tensor.matmul(ps[f % 2][0:EK, 0:2 * EI], mu[:, k, f * EK:(f + 1) * EK],
                                            c.w1[:, k, f * W1N:f * W1N + 2 * EI], start=(k == 0), stop=(k == KD - 1))
                last.then_inc(gu_ready, 1)
                for k in range(KD):
                    last = nc.tensor.matmul(ps[2 + f % 2][0:NE, 0:2 * KR], mup[:, k, f * NE:(f + 1) * NE],
                                            c.w1[:, k, f * W1N + 2 * EI:(f + 1) * W1N],
                                            start=(k == 0), stop=(k == KD - 1))
                last.then_inc(ma_ready, 1)

        @block.scalar
        def _(act):
            for f in range(EX):
                act.wait_ge(gu_ready, f + 1)
                nc.scalar.activation(c.qb[KR:KR + EK, f * 2 * EI:(f + 1) * 2 * EI], ps[f % 2][0:EK, 0:2 * EI],
                                     ACT.Copy).then_inc(gu_read, 1)

        @block.vector
        def _(dve):
            dve.wait_ge(loaded, 16 * 13)
            nc.vector.tensor_tensor(c.qb[0:KR, :], c.qb[0:KR, :], scale_gu[:, :], ALU.mult)
            nc.vector.tensor_tensor(c.qbd[:, :, :], c.qbd[:, :, :], scale_d[:, :, :], ALU.mult)
            nc.vector.tensor_copy(idxf[:, :], idx[:, :]).then_inc(small, 1)
            dve.wait_ge(small, 1)
            nc.vector.tensor_scalar(c.onehot[:, :], idxf[:, :], row[:, 0:1], None, ALU.is_equal).then_inc(small, 1)
            for f in range(EX):
                dve.wait_ge(ma_ready, f + 1)
                nc.vector.tensor_copy(c.ma[:, f * 2 * KR:(f + 1) * 2 * KR], ps[2 + f % 2][0:NE, 0:2 * KR])\
                    .then_inc(ma_read, 1)



def experts(nc, c, tag, last_layer):
    prep = Steps(LN_STEPS + ROUTER_STEPS)
    UB = EX * BT
    with ExitStack() as ctx:
        def sb(name, shape, dt=F32):
            return ctx.enter_context(nc.sbuf_tensor(tag + name, shape, dt))

        def psum(name):
            return ctx.enter_context(nc.psum_tensor(tag + "ps_" + name, [P, 512], F32))

        def sem(name):
            return ctx.enter_context(nc.semaphore(tag + name))

        rmax, lg, ex = sb("row_max", [P, BT]), sb("shifted", [P, BT, NE]), sb("exp", [P, BT, NE])
        esum, erec = sb("exp_sum", [P, BT]), sb("exp_rec", [P, BT])
        pr = sb("probs", [P, BT, NE + 2])
        top, rest = sb("top8", [P, BT, 8]), sb("others", [P, BT, NE + 2])
        wd, wdT = sb("w_dense", [P, BT, NE]), sb("w_denseT", [NE, S])
        flat, pen = sb("flat", [P, BT, EX, EK]), sb("penalty", [P, BT, EX, EK])
        fm, gmax = sb("masked", [P, BT, EX, EK]), sb("group_max", [P, BT, EX])
        fe, gsum, grec = sb("group_exp", [P, BT, EX, EK]), sb("group_sum", [P, BT, EX]), sb("group_rec", [P, BT, EX])
        scal = sb("scalar", [P, BT, EX])
        soft, softT = sb("soft", [P, BT, NE]), sb("softT", [NE, S])
        ssg, shh = sb("shared_silu", [P, 2, SH]), sb("shared_h", [P, 2, SH])
        shT = sb("shared_hT", [P, 3, P])
        aw, awT = sb("low_rank", [P, 2, 2, KR + EK]), sb("low_rankT", [KR + EK, 2, 2, P])
        sg, h, hT = sb("silu_gate", [P, 2, EI]), sb("hidden", [P, 2, EI]), sb("hiddenT", [HJ, 2, 2, P])
        dw, dwT = sb("down_low_rank", [P, BT, EX * KR]), sb("down_low_rankT", [P, 2, 4 * P])
        m_ps = [psum("main0"), psum("main1")]
        t_ps, h_ps, d_ps, r_ps = psum("low_rankT"), psum("hiddenT"), psum("down_low"), psum("router")
        y = [psum("y0"), psum("y1")]
        sh_ps = [(m_ps[0], m_ps[1]), (d_ps, h_ps)]

        steps = sem("prep_steps")
        minus_ones = sem("minus_ones")
        sh_main, sh_silu, sh_h, sh_hT_ps, sh_hT, sh_down = (sem("sh_" + n) for n in
                                                            ["main", "silu", "h", "hT_psum", "hT", "down"])
        main_done, aw_done, aww_done, awT_ps, awT_done = (sem(n) for n in
                                                          ["main", "aw", "aw_soft", "awT_psum", "awT"])
        gate_up, silu_done, h_done, hT_ps, hT_done = (sem(n) for n in
                                                      ["gate_up", "silu", "h", "hT_psum", "hT"])
        down_done, dw_done = sem("down"), sem("dw")
        dwT_ps, dwT_done, closed, added = sem("dwT_psum"), sem("dwT"), sem("closed"), sem("added")
        stored = sem("stored")

        def unit(blk, e, i, back=0):
            e, i = (e, i - back) if i >= back else (e - 1, i - back + BT)
            return e, i, blk * UB + e * BT + i

        block = ctx.enter_context(nc.Block())

        def run_units(engine, blk, step):
            for i in range(BT):
                step(blk, 0, i, i)
            with engine.Fori(1, EX) as e:
                for i in range(BT):
                    step(blk, e, i, BT)
            step(blk, EX, 0, BT, tail=1)
            step(blk, EX, 1, BT, tail=2)

        @block.tensor
        def _(pe):
            def ychunk(i):
                return y[i // 2][:, (i % 2) * D:(i % 2 + 1) * D]

            def shared_main(blk, i):
                if i >= 2:
                    pe.wait_ge(sh_h, blk * BT + i - 1)
                for n in range(2):
                    for k in range(KD):
                        last = nc.tensor.matmul(sh_ps[i % 2][n][:, 0:SH], c.xT[:, k, i * P:(i + 1) * P],
                                                c.shgu[:, k, n * SH:(n + 1) * SH], start=(k == 0), stop=(k == KD - 1))
                last.then_inc(sh_main, 1)

            def shared_down(blk, i):
                pe.wait_ge(sh_h, blk * BT + i + 1)
                if i > 0:
                    pe.wait_ge(sh_hT, blk * BT + i)
                for j, (lo, n) in enumerate(SHC):
                    last = nc.tensor.transpose(t_ps[0:n, j * P:(j + 1) * P], shh[:, i % 2, lo:lo + n], c.ident[:, :])
                last.then_inc(sh_hT_ps, 1)
                pe.wait_ge(sh_hT, blk * BT + i + 1)
                for j, (lo, n) in enumerate(SHC):
                    last = nc.tensor.matmul(ychunk(i), shT[0:n, j, :], c.shd[0:n, j, :],
                                            start=(i % 2 == 0 and j == 0), stop=False, skip_group_check=True)
                last.then_inc(sh_down, 1)

            def step(blk, e0, i0, have, tail=0):
                if not tail:
                    e, i, n = unit(blk, e0, i0)
                    if have >= 2:
                        pe.wait_ge(h_done, n - 1)
                    bank = m_ps[i % 2]
                    for k in range(KD):
                        nc.tensor.matmul(bank[:, 0:W1N], c.xT[:, k, i * P:(i + 1) * P],
                                         c.w1[:, k, ds(e * W1N, W1N)], start=(k == 0), stop=False,
                                         skip_group_check=True)
                    nc.tensor.matmul(bank[:, 2 * EI:W1N], softT[:, i * P:(i + 1) * P],
                                     c.ma[:, ds(e * 2 * KR, 2 * KR)], start=False, stop=False,
                                     skip_group_check=True).then_inc(main_done, 1)
                if have >= 1 and tail < 2:
                    e, i, n = unit(blk, e0, i0, 1)
                    pe.wait_ge(awT_done, n + 1)
                    for s in range(2):
                        last = nc.tensor.matmul(m_ps[i % 2][:, s * EI:(s + 1) * EI], awT[:, i % 2, s, :],
                                                c.qb[:, ds(e * 2 * EI + s * EI, EI)], start=False, stop=(s == 1),
                                                skip_group_check=True)
                    last.then_inc(gate_up, 1)
                if not tail:
                    e, i, n = unit(blk, e0, i0)
                    pe.wait_ge(aw_done, n + 1)
                    pe.wait_ge(aww_done, n + 1)
                    for s in range(2):
                        last = nc.tensor.transpose(t_ps[0:KR + EK, s * P:(s + 1) * P], aw[:, i % 2, s, :],
                                                   c.ident[:, :])
                    last.then_inc(awT_ps, 1)
                if have >= 2:
                    e, i, n = unit(blk, e0, i0, 2)
                    pe.wait_ge(hT_done, n + 1)
                    if have >= 3:
                        pe.wait_ge(dw_done, n)
                    for j in range(2):
                        nc.tensor.matmul(ychunk(i), hT[:, i % 2, j, :], c.w2[:, j, ds(e * W2N, D)],
                                         start=False, stop=False, skip_group_check=True)
                    for j in range(2):
                        last = nc.tensor.matmul(d_ps[:, 0:KR], hT[:, i % 2, j, :],
                                                c.w2[:, j, ds(e * W2N + D, KR)], start=(j == 0), stop=(j == 1))
                    last.then_inc(down_done, 1)
                if have >= 1 and tail < 2:
                    e, i, n = unit(blk, e0, i0, 1)
                    pe.wait_ge(h_done, n + 1)
                    for j in range(2):
                        last = nc.tensor.transpose(h_ps[0:HJ, j * P:(j + 1) * P], h[:, i % 2, j * HJ:(j + 1) * HJ],
                                                   c.ident[:, :])
                    last.then_inc(hT_ps, 1)

            with pe.Fori(0, NB) as blk:
                ln_tensor(nc, c, pe, steps, blk, m_ps, prep)
                pe.wait_ge(steps, prep.after("xT", blk))
                for i in range(BT):
                    for k in range(KD):
                        last = nc.tensor.matmul(r_ps[:, i * NE:(i + 1) * NE], c.xT[:, k, i * P:(i + 1) * P],
                                                c.wrt[:, k, :], start=(k == 0), stop=(k == KD - 1))
                last.then_inc(steps, 1)
                shared_main(blk, 0)
                shared_main(blk, 1)
                pe.wait_ge(steps, prep.after("w_dense", blk))
                apart(pe, c)
                for i in range(BT):
                    last = nc.tensor.transpose(t_ps[0:NE, i * P:(i + 1) * P], wd[:, i, :], c.ident[:, :])
                last.then_inc(steps, 1)
                pe.wait_ge(steps, prep.after("w_denseT", blk))
                for i in range(BT):
                    last = nc.tensor.matmul(r_ps[:, i * NE:(i + 1) * NE], wdT[:, i * P:(i + 1) * P], c.onehot[:, :],
                                            start=True, stop=True)
                last.then_inc(steps, 1)
                pe.wait_ge(steps, prep.after("soft", blk))
                apart(pe, c)
                for i in range(BT):
                    last = nc.tensor.transpose(t_ps[0:NE, i * P:(i + 1) * P], soft[:, i, :], c.ident[:, :])
                last.then_inc(steps, 1)
                pe.wait_ge(steps, prep.after("softT", blk))
                for i in range(BT):
                    shared_down(blk, i)
                    if i + 2 < BT:
                        shared_main(blk, i + 2)
                run_units(pe, blk, step)
                for i in range(BT):
                    pe.wait_ge(dw_done, (blk + 1) * UB)
                    if i > 0:
                        pe.wait_ge(dwT_done, blk * BT + i)
                    for q in range(4):
                        last = nc.tensor.transpose(t_ps[:, q * P:(q + 1) * P], dw[:, i, q * P:(q + 1) * P],
                                                   c.ident[:, :])
                    last.then_inc(dwT_ps, 1)
                    pe.wait_ge(dwT_done, blk * BT + i + 1)
                    for q in range(4):
                        last = nc.tensor.matmul(ychunk(i), dwT[:, i % 2, q * P:(q + 1) * P], c.qbd[:, q, :],
                                                start=False, stop=(q == 3), skip_group_check=True)
                    last.then_inc(closed, 1)

        @block.vector
        def _(dve):
            def at(name, blk):
                dve.wait_ge(steps, prep.after(name, blk))

            def step(blk, e0, i0, have, tail=0):
                if not tail:
                    e, i, n = unit(blk, e0, i0)
                    dve.wait_ge(main_done, n + 1)
                    a = m_ps[i % 2][:, 2 * EI:W1N].rearrange("p (s k r) -> p s k r", s=2, k=EK)
                    w = soft[:, i, ds(e * EK, EK)].unsqueeze(1).unsqueeze(3).to_broadcast([P, 2, EK, ER])
                    nc.vector.tensor_tensor(aw[:, i % 2, :, 0:KR].rearrange("p s (k r) -> p s k r", k=EK), a, w,
                                            ALU.mult).then_inc(aw_done, 1)
                if have >= 1 and tail < 2:
                    e, i, n = unit(blk, e0, i0, 1)
                    dve.wait_ge(silu_done, n + 1)
                    nc.vector.scalar_tensor_tensor(out=h[:, i % 2, :], in0=sg[:, i % 2, :],
                                                   scalar=scal[:, i, ds(e, 1)], in1=m_ps[i % 2][:, EI:2 * EI],
                                                   op0=ALU.mult, op1=ALU.mult).then_inc(h_done, 1)
                if have >= 2:
                    e, i, n = unit(blk, e0, i0, 2)
                    dve.wait_ge(down_done, n + 1)
                    a = d_ps[:, 0:KR].rearrange("p (k r) -> p k r", k=EK)
                    w = soft[:, i, ds(e * EK, EK)].unsqueeze(2).to_broadcast([P, EK, ER])
                    nc.vector.tensor_tensor(dw[:, i, ds(e * KR, KR)].rearrange("p (k r) -> p k r", k=EK), a, w,
                                            ALU.mult).then_inc(dw_done, 1)

            nc.vector.memset(pr[:, :, NE:NE + 2], -1.0).then_inc(minus_ones, 1)
            dve.wait_ge(minus_ones, 1)
            with dve.Fori(0, NB) as blk:
                ln_vector(nc, c, dve, steps, blk, blk, prep)
                at("logits", blk)
                r4 = r_ps[:, 0:BT * NE].rearrange("p (t n) -> p t n", t=BT)
                nc.vector.reduce_max(rmax[:, :], r4, AX).then_inc(steps, 1)
                at("row_max", blk)
                nc.vector.tensor_tensor(lg[:, :, :], r4, rmax[:, :].unsqueeze(2).to_broadcast([P, BT, NE]),
                                        ALU.subtract).then_inc(steps, 1)
                at("exp", blk)
                nc.vector.reduce_sum(esum[:, :], ex[:, :, :], AX).then_inc(steps, 1)
                at("exp_sum", blk)
                nc.vector.reciprocal(erec[:, :], esum[:, :]).then_inc(steps, 1)
                at("exp_rec", blk)
                nc.vector.tensor_tensor(pr[:, :, 0:NE], ex[:, :, :], erec[:, :].unsqueeze(2).to_broadcast([P, BT, NE]),
                                        ALU.mult).then_inc(steps, 1)
                at("probs", blk)
                apart(dve, c)
                for i in range(BT):
                    last = nc.vector.max(top[:, i, :], pr[:, i, 0:NE])
                last.then_inc(steps, 1)
                at("top8", blk)
                nc.vector.memset(top[:, :, TOPK:8], -1.0).then_inc(steps, 1)
                at("top6", blk)
                apart(dve, c)
                for i in range(BT):
                    last = nc.vector.match_replace(rest[:, i, :], top[:, i, :], pr[:, i, :], 0.0)
                last.then_inc(steps, 1)
                at("others", blk)
                nc.vector.tensor_tensor(wd[:, :, :], pr[:, :, 0:NE], rest[:, :, 0:NE], ALU.subtract)\
                    .then_inc(steps, 1)
                at("flat_psum", blk)
                nc.vector.tensor_copy(flat[:, :, :, :].rearrange("p t f k -> p (t f k)"), r_ps[:, 0:BT * NE])\
                    .then_inc(steps, 1)
                at("flat", blk)
                nc.vector.reduce_sum(scal[:, :, :], flat[:, :, :, :], AX).then_inc(steps, 1)
                at("scalar", blk)
                nc.vector.tensor_scalar(pen[:, :, :, :], flat[:, :, :, :], 0.0, -1e9, ALU.is_equal, ALU.mult)\
                    .then_inc(steps, 1)
                at("penalty", blk)
                nc.vector.tensor_tensor(fm[:, :, :, :], flat[:, :, :, :], pen[:, :, :, :], ALU.add).then_inc(steps, 1)
                at("masked", blk)
                nc.vector.reduce_max(gmax[:, :, :], fm[:, :, :, :], AX).then_inc(steps, 1)
                at("group_max", blk)
                g4 = [P, BT, EX, EK]
                nc.vector.tensor_tensor(fm[:, :, :, :], fm[:, :, :, :], gmax[:, :, :].unsqueeze(3).to_broadcast(g4),
                                        ALU.subtract).then_inc(steps, 1)
                at("group_exp", blk)
                nc.vector.reduce_sum(gsum[:, :, :], fe[:, :, :, :], AX).then_inc(steps, 1)
                at("group_sum", blk)
                nc.vector.reciprocal(grec[:, :, :], gsum[:, :, :]).then_inc(steps, 1)
                at("group_rec", blk)
                nc.vector.tensor_tensor(soft[:, :, :].rearrange("p t (f k) -> p t f k", f=EX), fe[:, :, :, :],
                                        grec[:, :, :].unsqueeze(3).to_broadcast(g4), ALU.mult).then_inc(steps, 1)
                for i in range(BT):
                    dve.wait_ge(sh_silu, blk * BT + i + 1)
                    nc.vector.tensor_tensor(shh[:, i % 2, :], ssg[:, i % 2, :], sh_ps[i % 2][1][:, 0:SH], ALU.mult)\
                        .then_inc(sh_h, 1)
                run_units(dve, blk, step)
                dve.wait_ge(closed, (blk + 1) * BT)
                for j in range(2):
                    xs = c.x[:, ds(blk * BT + 2 * j, 2), :]
                    last = nc.vector.tensor_tensor(xs, xs, y[j][:, :].rearrange("p (a d) -> p a d", a=2), ALU.add)
                last.then_inc(added, 1)
                dve.wait_ge(added, blk + 1)

        @block.gpsimd
        def _(pool):
            def step(blk, e0, i0, have, tail=0):
                if tail:
                    return
                e, i, n = unit(blk, e0, i0)
                if have >= 2:
                    pool.wait_ge(awT_ps, n - 1)
                apart(pool, c)
                w = soft[:, i, ds(e * EK, EK)].unsqueeze(1).to_broadcast([P, 2, EK])
                nc.gpsimd.tensor_copy(aw[:, i % 2, :, KR:KR + EK], w).then_inc(aww_done, 1)

            with pool.Fori(0, NB) as blk:
                pool.wait_ge(steps, prep.after("soft", blk))
                run_units(pool, blk, step)

        @block.scalar
        def _(act):
            def step(blk, e0, i0, have, tail=0):
                if have >= 1 and tail < 2:
                    e, i, n = unit(blk, e0, i0, 1)
                    act.wait_ge(gate_up, n + 1)
                    if have >= 3:
                        act.wait_ge(h_done, n - 1)
                    nc.scalar.activation(sg[:, i % 2, :], m_ps[i % 2][:, 0:EI], ACT.Silu).then_inc(silu_done, 1)
                if not tail:
                    e, i, n = unit(blk, e0, i0)
                    act.wait_ge(awT_ps, n + 1)
                    nc.scalar.activation(awT[:, i % 2, :, :].rearrange("p s t -> p (s t)"), t_ps[0:KR + EK, 0:2 * P],
                                         ACT.Copy).then_inc(awT_done, 1)
                if have >= 1 and tail < 2:
                    e, i, n = unit(blk, e0, i0, 1)
                    act.wait_ge(hT_ps, n + 1)
                    nc.scalar.activation(hT[:, i % 2, :, :].rearrange("p s t -> p (s t)"), h_ps[0:HJ, 0:2 * P],
                                         ACT.Copy).then_inc(hT_done, 1)

            with act.Fori(0, NB) as blk:
                ln_scalar(nc, c, act, steps, blk, m_ps, prep)
                act.wait_ge(steps, prep.after("shifted", blk))
                nc.scalar.activation(ex[:, :, :], lg[:, :, :], ACT.Exp).then_inc(steps, 1)
                act.wait_ge(steps, prep.after("w_denseT_psum", blk))
                nc.scalar.activation(wdT[:, :], t_ps[0:NE, :], ACT.Copy).then_inc(steps, 1)
                act.wait_ge(steps, prep.after("group_shifted", blk))
                nc.scalar.activation(fe[:, :, :, :], fm[:, :, :, :], ACT.Exp).then_inc(steps, 1)
                act.wait_ge(steps, prep.after("softT_psum", blk))
                nc.scalar.activation(softT[:, :], t_ps[0:NE, :], ACT.Copy).then_inc(steps, 1)

                def shared_silu(i):
                    act.wait_ge(sh_main, blk * BT + i + 1)
                    nc.scalar.activation(ssg[:, i % 2, :], sh_ps[i % 2][0][:, 0:SH], ACT.Silu).then_inc(sh_silu, 1)

                shared_silu(0)
                for i in range(BT):
                    if i + 1 < BT:
                        if i >= 1:
                            act.wait_ge(sh_h, blk * BT + i)
                        shared_silu(i + 1)
                    act.wait_ge(sh_hT_ps, blk * BT + i + 1)
                    if i > 0:
                        act.wait_ge(sh_down, blk * BT + i)
                    nc.scalar.activation(shT[:, 0:2, :].rearrange("p s t -> p (s t)"), t_ps[:, 0:2 * P], ACT.Copy)
                    n = SHC[2][1]
                    nc.scalar.activation(shT[0:n, 2, :], t_ps[0:n, 2 * P:3 * P], ACT.Copy).then_inc(sh_hT, 1)
                run_units(act, blk, step)
                for i in range(BT):
                    act.wait_ge(dwT_ps, blk * BT + i + 1)
                    if i >= 2:
                        act.wait_ge(closed, blk * BT + i - 1)
                    nc.scalar.activation(dwT[:, i % 2, :], t_ps[:, :], ACT.Copy).then_inc(dwT_done, 1)

        @block.sync
        def _(sp):
            if last_layer:
                out = c.dram["out"].rearrange("(n p) d -> p n d", p=P)
                for b in range(NB):
                    sp.wait_ge(added, b + 1)
                    sp.dma_start(out[:, b * BT:(b + 1) * BT, :], c.x[:, b * BT:(b + 1) * BT, :]).then_inc(stored, 16)
                sp.wait_ge(stored, NB * 16)



def softmax_attention(nc, c):
    VC = 32
    UNITS = [(t, h) for t in range(BT) for h in range(HG)]
    NU = len(UNITS)
    NPB = 3
    STACK_AT, SCORE_STEPS, NEG_AT, OUT_AT = [8, 13], 12, 14, 2
    READ_Q_AT = [8, 9, 10, 11]
    MASK_K_AT, NORMALISE_AT = [3, 6, 9, 12], 5
    with ExitStack() as ctx:
        def sb(name, shape, dt=F32):
            return ctx.enter_context(nc.sbuf_tensor("b_" + name, shape, dt))

        def psum(name):
            return ctx.enter_context(nc.psum_tensor("b_ps_" + name, [P, 512], F32))

        def sem(name):
            return ctx.enter_context(nc.semaphore("b_" + name))

        w, wo = sb("w_qkv", [P, KD, 3 * D]), sb("w_out", [P, KD, D])
        bias, bias_o = sb("bias_qkv", [P, 3 * D]), sb("bias_out", [P, D])
        cos, sin = sb("cos", [P, BT, 2, BD]), sb("sin", [P, BT, 2, BD])
        maskf = sb("masks_f32", [P, 2, P])
        maskb, identb = sb("masks", [P, 2, P], BF16), sb("ident_bf16", [P, P], BF16)
        identr = sb("ident_f32r", [P, P], F32R)
        qkr = sb("qk_roped", [P, BT, 2, D])
        v = sb("v", [P, BT, D])
        stk = sb("stack_tokens", [P, 2, 2, BT, HG, 4, BD], F32R)
        vv = sb("v_ones", [P, 2, BT, HG, VC])
        ks, qn = sb("k_stack", [P, 2, S], F32R), sb("q_stack_neg", [P, 2, S], F32R)
        qz, kz = sb("q_stack_one", [P, 2, HG, S], F32R), sb("k_stack_one", [P, 2, HG, S], F32R)
        own = sb("own_rows", [P, 2, HG])
        nmax = sb("neg_max", [P, BT, HG])
        ex = sb("exp", [P, 2, HG, S])
        qk, t1, t2 = (ex[:, :, :, :].rearrange("p a h s -> p (a h s)")[:, j * 4 * D:(j + 1) * 4 * D].rearrange(
            "p (r s d) -> p r s d", r=2, s=2) for j in range(3))
        oS = sb("outT", [P, S])
        rrec, on = sb("row_rec", [P, BT, HG, 1]), sb("out_normalised", [P, BT, D])
        s_ps, p_ps = [psum("scores0"), psum("scores1")], [psum(f"by_keys{i}") for i in range(NPB)]
        o_ps, k_ps, m_ps = psum("out"), psum("stack"), psum("neg_and_out")

        ln, loaded, consts, zeroed = sem("ln_steps"), sem("loaded"), sem("consts"), sem("zeroed")
        qkv_ps, biased, vread = sem("qkv_psum"), sem("biased"), sem("v_read")
        rope_a, rope_done = sem("rope_parts"), sem("rope_done")
        v_placed = sem("v_placed")
        hi_done, stacked, stack_ps, q_stacked, k_stacked = [sem(name) for name in (
            "high", "stacked", "stack_psum", "q_stacked", "k_stacked")]
        k_masked = sem("k_masked")
        scored, maxed, halved_hi, halved = sem("scored"), sem("maxed"), sem("max_high"), sem("max_halves")
        neg_psum, neg_done = sem("neg_psum"), sem("neg_done")
        by_keys, exped, weighted = sem("by_keys"), sem("exped"), sem("weighted")
        o_read, oT_ps, rec, normed = sem("out_read"), sem("outT_psum"), sem("rec"), sem("normed")
        f_ps, f_done, y_done, biased_o, added = sem("feat_psum"), sem("feat"), sem("y_psum"), sem("y_bias"), sem("added")

        block = ctx.enter_context(nc.Block())

        def groups(engine, slot, b):
            slot(b, 0, 0)
            with engine.Fori(0, NHG // 2 - 2) as t:
                for p in range(2):
                    slot(b, 2 * t + p + 1, 1 - p)
            for g in range(NHG - 3, NHG):
                slot(b, g, g % 2)

        def at(g, n):
            return isinstance(g, int) and g == n

        @block.sync
        def _(sp):
            sp.dma_start(w[:, :, :], c.dram["b_w"].rearrange("(k p) n -> p k n", p=P)).then_inc(loaded, 16)
            sp.dma_start(wo[:, :, :], c.dram["b_wo"].rearrange("(k p) n -> p k n", p=P)).then_inc(loaded, 16)
            sp.dma_start(bias[:, :], c.dram["b_bias"].partition_broadcast(P)).then_inc(loaded, 16)
            sp.dma_start(bias_o[:, :], c.dram["b_bias_o"].partition_broadcast(P)).then_inc(loaded, 16)
            sp.dma_start(cos[:, :, :, :].rearrange("p t a d -> p (t a d)"), c.dram["b_cos"]).then_inc(loaded, 16)
            sp.dma_start(sin[:, :, :, :].rearrange("p t a d -> p (t a d)"), c.dram["b_sin"]).then_inc(loaded, 16)
            sp.dma_start(own[:, :, :].rearrange("p s h -> p (s h)"), c.dram["b_own"]).then_inc(loaded, 16)
            sp.dma_start(maskf[:, :, :].rearrange("p a n -> p (a n)"), c.dram["b_mask"]).then_inc(loaded, 16)

        @block.tensor
        def _(pe):
            def stack(b, g, par, s):
                G = b * NHG + g
                if s == 0:
                    pe.wait_ge(stacked, G + 1)
                    if not (isinstance(g, int) and g == 0):
                        pe.wait_ge(k_stacked, G)
                else:
                    pe.wait_ge(q_stacked, G + 1)
                for i in range(BT):
                    last = nc.tensor.matmul(k_ps[:, i * P:(i + 1) * P].bitcast(F32R),
                                            stk[:, par, s, i, :, :, :].rearrange("p h a d -> p (h a d)"),
                                            identr[:, :], is_transpose=True, start=True, stop=True)
                last.then_inc(stack_ps, 1)

            def score(b, g, par, u):
                G = b * NHG + g
                qi, h = UNITS[u]
                N = (qi + 1) * P
                if u == 0:
                    pe.wait_ge(q_stacked, G + 1)
                    pe.wait_ge(k_stacked, G + 1)
                if not (isinstance(g, int) and g == 0 and u < 2):
                    pe.wait_ge(maxed, G * NU + u - 1)
                nc.tensor.matmul(s_ps[u % 2][:, 0:N], qz[:, par, h, qi * P:(qi + 1) * P],
                                 ks[:, par, 0:N], start=True, stop=False, skip_group_check=True)
                nc.tensor.matmul(s_ps[u % 2][:, qi * P:N], identb[:, :], maskb[:, 0, :], start=False, stop=True,
                                 skip_group_check=True).then_inc(scored, 1)

            def neg(b, g, par, free):
                G = b * NHG + g
                pe.wait_ge(halved, G + 1)
                if not free:
                    pe.wait_ge(normed, G - 1)
                for i in range(BT):
                    last = nc.tensor.matmul(m_ps[:, i * P:(i + 1) * P].bitcast(F32R),
                                            stk[:, par, 0, i, :, :, :].rearrange("p h a d -> p (h a d)"), identr[:, :],
                                            is_transpose=True, start=True, stop=True)
                last.then_inc(neg_psum, 1)

            def keys(b, g, par, u):
                G = b * NHG + g
                kj, h = UNITS[u]
                N = S - kj * P
                bank = p_ps[u % NPB]
                if u == 0:
                    pe.wait_ge(k_masked, (G + 1) * HG)
                    pe.wait_ge(neg_done, G + 1)
                if u < NPB:
                    if not (isinstance(g, int) and g == 0):
                        pe.wait_ge(exped, G * NU)
                else:
                    pe.wait_ge(exped, G * NU + u - NPB + 1)
                nc.tensor.matmul(bank[:, 0:N], kz[:, par, h, kj * P:(kj + 1) * P], qn[:, par, kj * P:S],
                                 start=True, stop=False, skip_group_check=True)
                nc.tensor.matmul(bank[:, 0:P], identb[:, :], maskb[:, 1, :], start=False, stop=True,
                                 skip_group_check=True).then_inc(by_keys, 1)

            def weigh(b, g, par, kj):
                G = b * NHG + g
                pe.wait_ge(exped, G * NU + (kj + 1) * HG)
                if kj == 0:
                    pe.wait_ge(v_placed, G + 1)
                if kj == 0 and not (isinstance(g, int) and g == 0):
                    pe.wait_ge(o_read, G)
                for h in range(HG):
                    last = nc.tensor.matmul(o_ps[h * 32:(h + 1) * 32, kj * P:S], vv[:, par, kj, h, :],
                                            ex[:, kj % 2, h, 0:S - kj * P], start=(kj == 0), stop=(kj == BT - 1),
                                            skip_group_check=True)
                last.then_inc(weighted, 1)

            def out_tokens(b, g):
                G = b * NHG + g
                pe.wait_ge(o_read, G + 1)
                if isinstance(g, int) and g == NHG - 1:
                    pe.wait_ge(normed, G)
                else:
                    pe.wait_ge(neg_done, G + 2)
                for i in range(BT):
                    last = nc.tensor.transpose(m_ps[:, i * P:(i + 1) * P], oS[:, i * P:(i + 1) * P], c.ident[:, :])
                last.then_inc(oT_ps, 1)

            def slot(b, g, par):
                first, last = at(g, 0), at(g, NHG - 1)
                for u in range(NU):
                    keys(b, g, par, u)
                    if u == OUT_AT and not first:
                        out_tokens(b, g - 1)
                    if not last:
                        for a in range(-(-NU * u // SCORE_STEPS), min(NU, -(-NU * (u + 1) // SCORE_STEPS))):
                            score(b, g + 1, 1 - par, a)
                    if not last and not at(g, NHG - 2) and u in STACK_AT:
                        stack(b, g + 2, par, STACK_AT.index(u))
                    if u % HG == HG - 1 and u > HG:
                        weigh(b, g, par, u // HG - 1)
                    if u == NEG_AT and not last:
                        neg(b, g + 1, 1 - par, first)
                weigh(b, g, par, BT - 1)

            pe.wait_ge(consts, 3)
            with pe.Fori(0, NB) as b:
                ln_tensor(nc, c, pe, ln, b, s_ps)
                pe.wait_ge(ln, LN.after("xT", b))
                for i in range(BT):
                    if i >= 1:
                        pe.wait_ge(biased, b * BT + i)
                        pe.wait_ge(vread, b * BT + i)
                    for k in range(KD):
                        nc.tensor.matmul(p_ps[0][:, :], c.xT[:, k, i * P:(i + 1) * P], w[:, k, 0:2 * D],
                                         start=(k == 0), stop=(k == KD - 1))
                    for k in range(KD):
                        last = nc.tensor.matmul(p_ps[1][:, 0:D], c.xT[:, k, i * P:(i + 1) * P], w[:, k, 2 * D:3 * D],
                                                start=(k == 0), stop=(k == KD - 1))
                    last.then_inc(qkv_ps, 1)
                pe.wait_ge(vread, (b + 1) * BT)
                stack(b, 0, 0, 0)
                stack(b, 0, 0, 1)
                stack(b, 1, 1, 0)
                stack(b, 1, 1, 1)
                for u in range(NU):
                    score(b, 0, 0, u)
                neg(b, 0, 0, True)
                groups(pe, slot, b)
                out_tokens(b, NHG - 1)
                for i in range(BT):
                    pe.wait_ge(normed, (b + 1) * NHG)
                    if i >= 2:
                        pe.wait_ge(f_done, b * BT + i - 1)
                    for k in range(KD):
                        last = nc.tensor.transpose(s_ps[i % 2][:, k * P:(k + 1) * P], on[:, i, k * P:(k + 1) * P],
                                                   c.ident[:, :])
                    last.then_inc(f_ps, 1)
                for i in range(BT):
                    pe.wait_ge(f_done, b * BT + i + 1)
                    if i >= 2:
                        pe.wait_ge(added, b * BT + i - 1)
                    for k in range(KD):
                        last = nc.tensor.matmul(p_ps[i % 2][:, 0:D], c.xT[:, k, i * P:(i + 1) * P], wo[:, k, :], start=(k == 0),
                                                stop=(k == KD - 1))
                    last.then_inc(y_done, 1)

        @block.gpsimd
        def _(pool):
            def split(b, g, par):
                G = b * NHG + g
                if not (isinstance(g, int) and g < 2):
                    pool.wait_ge(neg_psum, G - 1)
                apart(pool, c)
                highs, low = [(0, 1), (0, 2)], [2, 1]
                srcs = [qkr[:, :, s, ds(g * HG * BD, HG * BD)].rearrange("p t (h d) -> p t h d", h=HG)
                        for s in range(2)]
                for s in range(2):
                    for a in highs[s]:
                        last = nc.gpsimd.tensor_copy(stk[:, par, s, :, :, a, :], srcs[s])
                last.then_inc(hi_done, 1)
                pool.wait_ge(hi_done, G + 1)
                apart(pool, c)
                for s in range(2):
                    last = nc.gpsimd.tensor_tensor(stk[:, par, s, :, :, low[s], :], srcs[s],
                                                   stk[:, par, s, :, :, 0, :].bitcast(F32), ALU.subtract)
                last.then_inc(stacked, 1)

            def place_v(b, g, par):
                G = b * NHG + g
                if not (isinstance(g, int) and g < 2):
                    pool.wait_ge(weighted, BT * (G - 1))
                apart(pool, c)
                nc.gpsimd.tensor_copy(vv[:, par, :, :, 0:BD],
                                      v[:, :, ds(g * HG * BD, HG * BD)].rearrange("p t (h d) -> p t h d", h=HG))\
                    .then_inc(v_placed, 1)

            pool.wait_ge(loaded, 16 * 8)
            for par in range(2):
                nc.gpsimd.memset(stk[:, par, 0, :, :, 3, :].bitcast(F32), 0.0)
                nc.gpsimd.memset(stk[:, par, 1, :, :, 3, 2:BD].bitcast(F32), 0.0)
                nc.gpsimd.memset(stk[:, par, 1, :, :, 3, 0:2].bitcast(F32), 1.0)
            nc.gpsimd.memset(vv[:, :, :, :, BD + 1:VC], 0.0)
            nc.gpsimd.memset(vv[:, :, :, :, BD:BD + 1], 1.0).then_inc(zeroed, 1)
            with pool.Fori(0, NB) as b:
                pool.wait_ge(rope_done, (b + 1) * BT)
                split(b, 0, 0)
                place_v(b, 0, 0)
                split(b, 1, 1)
                place_v(b, 1, 1)
                with pool.Fori(0, NHG // 2 - 1) as t:
                    for p in range(2):
                        split(b, 2 * t + p + 2, p)
                        place_v(b, 2 * t + p + 2, p)

        @block.vector
        def _(dve):
            def read_k(b, g, par):
                G = b * NHG + g
                dve.wait_ge(stack_ps, 2 * G + 2)
                nc.vector.tensor_copy(ks[:, par, :], k_ps[:, :]).then_inc(k_stacked, 1)

            def mask_k(b, g, par, h):
                G = b * NHG + g
                if h == 0:
                    dve.wait_ge(k_stacked, G + 1)
                nc.vector.tensor_scalar(kz[:, par, h, :], ks[:, par, :].bitcast(F32), own[:, 1, h:h + 1], None,
                                        ALU.mult).then_inc(k_masked, 1)

            def maxima(b, g, par):
                G = b * NHG + g
                for u in range(NU):
                    qi, h = UNITS[u]
                    n = G * NU + u
                    if u == 0 and not (isinstance(g, int) and g == 0):
                        dve.wait_ge(halved, G)
                    dve.wait_ge(scored, n + 1)
                    nc.vector.reduce_max(nmax[:, qi, h:h + 1], s_ps[u % 2][:, 0:(qi + 1) * P], AX, negate=True)\
                        .then_inc(maxed, 1)
                    if u in MASK_K_AT:
                        mask_k(b, g, par, MASK_K_AT.index(u))
                    if u == NORMALISE_AT and not at(g, 0) and not at(g, 1):
                        normalise(b, g - 2)
                dve.wait_ge(maxed, (G + 1) * NU)
                top = stk[:, par, 0, :, :, 3, 0]
                nc.vector.tensor_copy(top, nmax[:, :, :]).then_inc(halved_hi, 1)
                dve.wait_ge(halved_hi, G + 1)
                nc.vector.tensor_tensor(stk[:, par, 0, :, :, 3, 1], nmax[:, :, :], top.bitcast(F32), ALU.subtract)\
                    .then_inc(halved, 1)

            def normalise(b, g):
                G = b * NHG + g
                dve.wait_ge(oT_ps, G + 1)
                o4 = m_ps[:, :].rearrange("p (t h d) -> p t h d", t=BT, h=HG)
                nc.vector.reciprocal(rrec[:, :, :, :], o4[:, :, :, BD:BD + 1]).then_inc(rec, 1)
                dve.wait_ge(rec, G + 1)
                dst = on[:, :, ds(g * HG * BD, HG * BD)].rearrange("p t (h d) -> p t h d", h=HG)
                nc.vector.tensor_tensor(dst, o4[:, :, :, 0:BD], rrec[:, :, :, :].to_broadcast([P, BT, HG, BD]),
                                        ALU.mult).then_inc(normed, 1)

            def slot(b, g, par):
                if at(g, NHG - 1):
                    normalise(b, g - 1)
                else:
                    maxima(b, g + 1, 1 - par)
                    if not at(g, NHG - 2):
                        read_k(b, g + 2, par)

            dve.wait_ge(loaded, 16 * 8)
            nc.vector.tensor_copy(maskb[:, :, :], maskf[:, :, :]).then_inc(consts, 1)
            nc.vector.tensor_copy(identb[:, :], c.ident[:, :]).then_inc(consts, 1)
            nc.vector.tensor_copy(identr[:, :], c.ident[:, :]).then_inc(consts, 1)
            dve.wait_ge(zeroed, 1)
            with dve.Fori(0, NB) as b:
                ln_vector(nc, c, dve, ln, b, b)
                H2 = BD // 2
                full, half = [P, BH, BD], [P, BH, H2]
                for i in range(BT):
                    n = b * BT + i
                    r = i % 2
                    dve.wait_ge(qkv_ps, n + 1)
                    nc.vector.tensor_tensor(qk[:, r, :, :].rearrange("p a d -> p (a d)"), p_ps[0][:, :],
                                            bias[:, 0:2 * D], ALU.add).then_inc(biased, 1)
                    nc.vector.tensor_tensor(v[:, i, :], p_ps[1][:, 0:D], bias[:, 2 * D:], ALU.add).then_inc(vread, 1)
                    dve.wait_ge(biased, n + 1)
                    for s in range(2):
                        q4 = qk[:, r, s, :].rearrange("p (h d) -> p h d", d=BD)
                        a4, b4 = (t[:, r, s, :].rearrange("p (h d) -> p h d", d=BD) for t in (t1, t2))
                        nc.vector.tensor_tensor(a4, q4, cos[:, i, s, :].unsqueeze(1).to_broadcast(full), ALU.mult)
                        nc.vector.tensor_tensor(b4[:, :, 0:H2], q4[:, :, H2:BD],
                                                sin[:, i, s, 0:H2].unsqueeze(1).to_broadcast(half), ALU.mult)
                        last = nc.vector.tensor_tensor(b4[:, :, H2:BD], q4[:, :, 0:H2],
                                                       sin[:, i, s, H2:BD].unsqueeze(1).to_broadcast(half), ALU.mult)
                    last.then_inc(rope_a, 1)
                    dve.wait_ge(rope_a, n + 1)
                    nc.vector.tensor_tensor(qkr[:, i, :, :], t1[:, r, :, :], t2[:, r, :, :], ALU.add)\
                        .then_inc(rope_done, 1)
                read_k(b, 0, 0)
                read_k(b, 1, 1)
                maxima(b, 0, 0)
                groups(dve, slot, b)
                normalise(b, NHG - 1)
                for i in range(BT):
                    n = b * BT + i
                    xs = c.x[:, ds(n, 1), :].rearrange("p a d -> p (a d)")
                    nc.vector.tensor_tensor(xs, xs, bias_o[:, :], ALU.add).then_inc(biased_o, 1)
                    dve.wait_ge(biased_o, n + 1)
                    dve.wait_ge(y_done, n + 1)
                    nc.vector.tensor_tensor(xs, xs, p_ps[i % 2][:, 0:D], ALU.add).then_inc(added, 1)
                dve.wait_ge(added, (b + 1) * BT)

        @block.scalar
        def _(act):
            def read_q(b, g, par, h):
                if h == 0:
                    act.wait_ge(stack_ps, 2 * (b * NHG + g) + 1)
                last = nc.scalar.activation(qz[:, par, h, :], k_ps[:, :], ACT.Copy, scale=own[:, 0, h:h + 1])
                if h == HG - 1:
                    last.then_inc(q_stacked, 1)

            def read_neg(b, g, par):
                act.wait_ge(neg_psum, b * NHG + g + 1)
                nc.scalar.activation(qn[:, par, :], m_ps[:, :], ACT.Copy).then_inc(neg_done, 1)

            def read_out(b, g):
                G = b * NHG + g
                act.wait_ge(weighted, BT * (G + 1))
                if not (isinstance(g, int) and g == 0):
                    act.wait_ge(oT_ps, G)
                nc.scalar.activation(oS[:, :], o_ps[:, :], ACT.Copy).then_inc(o_read, 1)

            def slot(b, g, par):
                G = b * NHG + g
                last = at(g, NHG - 1)
                for u in range(NU):
                    kj, h = UNITS[u]
                    act.wait_ge(by_keys, G * NU + u + 1)
                    if kj >= 2 and h == 0:
                        act.wait_ge(weighted, BT * G + kj - 1)
                    nc.scalar.activation(ex[:, kj % 2, h, 0:S - kj * P], p_ps[u % NPB][:, 0:S - kj * P], ACT.Exp)\
                        .then_inc(exped, 1)
                    if u in READ_Q_AT and not last and not at(g, NHG - 2):
                        read_q(b, g + 2, par, READ_Q_AT.index(u))
                    if u == NEG_AT and not last:
                        read_neg(b, g + 1, 1 - par)
                read_out(b, g)

            act.wait_ge(loaded, 16 * 8)
            with act.Fori(0, NB) as b:
                ln_scalar(nc, c, act, ln, b, s_ps)
                for g in range(2):
                    for h in range(HG):
                        read_q(b, g, g, h)
                read_neg(b, 0, 0)
                groups(act, slot, b)
                for i in range(BT):
                    n = b * BT + i
                    act.wait_ge(f_ps, n + 1)
                    nc.scalar.activation(c.xT[:, :, i * P:(i + 1) * P], s_ps[i % 2][:, 0:D].rearrange(
                        "p (k t) -> p k t", k=KD), ACT.Copy).then_inc(f_done, 1)


def build(nc, dram):
    with ExitStack() as ctx:
        c = Chip()
        resident(nc, ctx, c, dram)
        linear_attention(nc, c)
        expert_weights(nc, c)
        experts(nc, c, "f0_", False)
        softmax_attention(nc, c)
        experts(nc, c, "f1_", True)


def _layouts(np, a):
    f4 = np.float32

    def t(x):
        return np.ascontiguousarray(np.asarray(x).T)

    get = {k: np.asarray(v) for k, v in a.items()}
    d = {"x": get["L0_attn_a_x"].reshape(NB * S, D)}
    d["a_w"] = np.concatenate([t(get["L0_attn_a_W" + n]) for n in "qkv"], axis=1)
    d["a_wo"] = t(get["L0_attn_a_Wo"])
    d["b_w"] = np.concatenate([t(get["L0_attn_b_W" + n]) for n in "qkv"], axis=1)
    d["b_wo"] = t(get["L0_attn_b_Wo"])
    d["b_bias"] = np.concatenate([get["L0_attn_b_b" + n] for n in "qkv"])
    d["b_bias_o"] = get["L0_attn_b_bo"]
    f = {k[7:]: v for k, v in get.items() if k.startswith("L0_ffn_")}
    d["wrt"] = t(f["gate_weight"])
    d["mapping"] = f["inv_mapping"].reshape(NE)
    w1 = np.concatenate([f["gate_W"], f["up_W"], f["gate_qa"].reshape(EX, KR, D), f["up_qa"].reshape(EX, KR, D)], axis=1)
    d["w1"] = np.ascontiguousarray(w1.transpose(2, 0, 1).reshape(D, EX * W1N))
    w2 = np.concatenate([f["down_W"].transpose(0, 2, 1), f["down_qa"].reshape(EX, KR, EI).transpose(0, 2, 1)], axis=2)
    d["w2"] = np.ascontiguousarray(w2.transpose(1, 0, 2).reshape(EI, EX * W2N))
    qb = [f[n].transpose(0, 1, 3, 2).reshape(EX, KR, EI) for n in ("gate_qb", "up_qb")]
    d["qb"] = np.ascontiguousarray(np.concatenate(qb, axis=2).transpose(1, 0, 2).reshape(KR, EX * 2 * EI))
    d["scale_gu"] = np.concatenate([f["gate_scale"], f["up_scale"]], axis=1).reshape(EX * 2 * EI)
    d["qbd"] = np.ascontiguousarray(f["down_qb"].transpose(0, 1, 3, 2).reshape(EX * KR, D))
    d["scale_d"] = f["down_scale"]
    d["mu"] = np.ascontiguousarray(f["mask_up_W"].transpose(1, 0, 2).reshape(D, NE))
    mup = np.zeros((D, EX, NE), f["mask_up_W"].dtype)
    for e in range(EX):
        mup[:, e, e * EK:(e + 1) * EK] = f["mask_up_W"][e]
    d["mup"] = mup.reshape(D, EX * NE)
    d["shgu"] = np.concatenate([t(f["sh_gate_W"]), t(f["sh_up_W"])], axis=1)
    d["shd"] = t(f["sh_down_W"])
    d["ident"] = np.eye(P, dtype=f4)
    d["row"] = np.arange(NE, dtype=f4).reshape(NE, 1)
    pos = np.arange(P)
    d["a_mask"] = (pos[:, None] <= pos[None, :]).astype(f4)
    by_query = np.where(pos[:, None] >= pos[None, :], 0.0, NEG).astype(f4)
    d["b_mask"] = np.concatenate([by_query, by_query.T], axis=1)
    head = pos[:, None] // 32 == np.arange(HG)[None, :]
    d["b_own"] = np.concatenate([head & (pos[:, None] % 32 < 3 * BD), head], axis=1).astype(f4)
    inv = (f4(1.0) / f4(10000.0) ** (np.arange(0, HD, 2, dtype=f4) / f4(HD))).astype(f4)
    ang = np.outer(np.arange(S, dtype=f4), inv).astype(f4).T
    d["a_cos"] = np.concatenate([np.cos(ang), np.cos(ang)]).astype(f4)
    d["a_sin"] = np.concatenate([np.sin(ang), -np.sin(ang)]).astype(f4)
    theta = (f4(10000.0) ** (-np.arange(0, BD, 2, dtype=f4) / f4(BD))).astype(f4)
    frame = np.floor((np.arange(S) // 72).astype(f4) * 0.5)
    ang = (np.arange(S, dtype=f4)[:, None] * theta).astype(np.float64) + (frame.astype(f4)[:, None] * theta)
    co, si = np.cos(ang), np.sin(ang)
    for name, tab in (("b_cos", np.concatenate([co, co], 1)), ("b_sin", np.concatenate([-si, si], 1))):
        both = np.stack([tab / np.sqrt(BD), tab], axis=1).astype(f4)
        d[name] = np.ascontiguousarray(both.reshape(BT, P, 2 * BD).transpose(1, 0, 2).reshape(P, BT * 2 * BD))
    return d


def kernel(**inputs):
    import numpy as np
    import concourse.bacc as bacc
    from concourse.bass_utils import run_bass_kernel_spmd

    nc = bacc.Bacc("TRN2", target_bir_lowering=False, num_devices=1)
    arrays, dram = {}, {}
    for name, a in _layouts(np, inputs).items():
        arrays[f"in_{name}"] = np.ascontiguousarray(a)
        dram[name] = nc.dram_tensor(f"in_{name}", a.shape, mybir.dt.from_np(a.dtype), kind="ExternalInput").ap()
    dram["out"] = nc.dram_tensor("out_0", (NB * S, D), F32, kind="ExternalOutput").ap()
    build(nc, dram)
    r = run_bass_kernel_spmd(nc, [arrays], core_ids=[0])
    return r.results[0]["out_0"].reshape(NB, S, D)
```

```python
from contextlib import ExitStack

import concourse.bass as bass
from concourse import mybir

F32 = mybir.dt.float32
F32R = mybir.dt.float32r
BF16 = mybir.dt.bfloat16
I32 = mybir.dt.int32
ALU = mybir.AluOpType
ACT = mybir.ActivationFunctionType
AX = mybir.AxisListType.X
ds = bass.ds

P = 128
D = 256
KD = D // P
NB = 4
BT = 4
S = BT * P
LN_EPS = 1e-5

AH, AG, HD = 16, 4, 128
REP = AH // AG
A_EPS = 1e-6
BH, BD = 32, 8
HG = 4
NHG = BH // HG
NEG = -1e30
EX, EK, ER, EI = 8, 8, 8, 176
NE = EX * EK
KR = EK * ER
TOPK = 6
HJ = EI // 2
W1N = 2 * EI + 2 * KR
W2N = D + KR
SH = 2 * EI
SHC = [(0, 128), (128, 128), (256, SH - 256)]

LN_STEPS = ["stats", "aggregate", "var_eps", "std", "rstd", "normalised", "xT_psum", "xT"]
ROUTER_STEPS = ["logits", "row_max", "shifted", "exp", "exp_sum", "exp_rec", "probs", "top8", "top6",
                "others", "w_dense", "w_denseT_psum", "w_denseT", "flat_psum", "flat", "scalar", "penalty",
                "masked", "group_max", "group_shifted", "group_exp", "group_sum", "group_rec", "soft",
                "softT_psum", "softT"]


class Steps:

    def __init__(self, names):
        self.names = names

    def after(self, name, rounds=0):
        return rounds * len(self.names) + self.names.index(name) + 1


class Chip:
    pass


def resident(nc, ctx, c, dram):
    def sb(name, shape, dt=F32):
        return ctx.enter_context(nc.sbuf_tensor(name, shape, dt))

    c.dram = dram
    c.x = sb("x_resident", [P, NB * BT, D])
    c.xT = sb("xT", [P, KD, S])
    c.ident = sb("ident", [P, P])
    c.w1 = sb("w1", [P, KD, EX * W1N])
    c.w2 = sb("w2", [HJ, 2, EX * W2N])
    c.qb = sb("qb_gate_up", [KR + EK, EX * 2 * EI])
    c.qbd = sb("qb_down", [P, EX // 2, D])
    c.ma = sb("mask_up_low_rank", [NE, EX * 2 * KR])
    c.shgu = sb("shared_gate_up", [P, KD, 2 * SH])
    c.shd = sb("shared_down", [P, 3, D])
    c.wrt = sb("router_w", [P, KD, NE])
    c.onehot = sb("onehot", [NE, NE])
    c.xn = sb("x_normalised", [P, BT, D])
    c.ln_stats = sb("ln_stats", [P, BT, 6])
    c.ln_mv = sb("ln_mean_var", [P, BT, 2])
    c.ln_ve = sb("ln_var_eps", [P, BT])
    c.ln_std = sb("ln_std", [P, BT])
    c.ln_rstd = sb("ln_rstd", [P, BT])
    c.x_loaded = ctx.enter_context(nc.semaphore("x_loaded"))
    c.a_loaded = ctx.enter_context(nc.semaphore("first_loaded"))
    c.waits_met = ctx.enter_context(nc.semaphore("waits_met"))
    c.f_loaded = ctx.enter_context(nc.semaphore("f_loaded"))


def load_x(c, sp):
    xv = c.dram["x"].rearrange("(n p) d -> p n d", p=P)
    sp.dma_start(c.x[:, 0:BT, :], xv[:, 0:BT, :]).then_inc(c.x_loaded, 16)
    sp.dma_start(c.ident[:, :], c.dram["ident"]).then_inc(c.x_loaded, 16)


def load_rest_of_x(c, sp):
    xv = c.dram["x"].rearrange("(n p) d -> p n d", p=P)
    sp.dma_start(c.x[:, BT:, :], xv[:, BT:, :]).then_inc(c.a_loaded, 16)


def load_expert_weights(c, sp):
    sp.dma_start(c.w1[:, :, :], c.dram["w1"].rearrange("(k p) n -> p k n", p=P)).then_inc(c.f_loaded, 16)
    sp.dma_start(c.w2[:, :, :], c.dram["w2"].rearrange("(j p) n -> p j n", p=HJ)).then_inc(c.f_loaded, 16)
    sp.dma_start(c.qb[0:KR, :], c.dram["qb"]).then_inc(c.f_loaded, 16)
    sp.dma_start(c.qbd[:, :, :], c.dram["qbd"].rearrange("(q p) n -> p q n", p=P)).then_inc(c.f_loaded, 16)
    sp.dma_start(c.shgu[:, :, :], c.dram["shgu"].rearrange("(k p) n -> p k n", p=P)).then_inc(c.f_loaded, 16)
    for j, (lo, n) in enumerate(SHC):
        sp.dma_start(c.shd[0:n, j, :], c.dram["shd"][lo:lo + n, :]).then_inc(c.f_loaded, 16)
    sp.dma_start(c.wrt[:, :, :], c.dram["wrt"].rearrange("(k p) n -> p k n", p=P)).then_inc(c.f_loaded, 16)
    sp.wait_ge(c.f_loaded, 16 * 9)


def apart(engine, c):
    engine.sem_inc(c.waits_met, 1)



LN = Steps(LN_STEPS)


def block_of(turn):
    return 0 if isinstance(turn, int) and turn == NB else turn


def ln_vector_stats(nc, c, sem, blk):
    for i in range(BT):
        last = nc.vector.bn_stats(c.ln_stats[:, i, :], c.x[:, ds(blk * BT + i, 1), :].rearrange("p a d -> p (a d)"))
    last.then_inc(sem, 1)


def ln_vector_variance(nc, c, dve, sem, rounds, t=LN):
    dve.wait_ge(sem, t.after("stats", rounds))
    apart(dve, c)
    for i in range(BT):
        last = nc.vector.bn_aggr(c.ln_mv[:, i, :], c.ln_stats[:, i, :])
    last.then_inc(sem, 1)
    dve.wait_ge(sem, t.after("aggregate", rounds))
    nc.vector.tensor_scalar(c.ln_ve[:, :], c.ln_mv[:, :, 1], LN_EPS, None, ALU.add).then_inc(sem, 1)


def ln_vector_normalise(nc, c, dve, sem, blk, rounds, t=LN):
    dve.wait_ge(sem, t.after("std", rounds))
    nc.vector.reciprocal(c.ln_rstd[:, :], c.ln_std[:, :]).then_inc(sem, 1)
    dve.wait_ge(sem, t.after("rstd", rounds))
    for i in range(BT):
        last = nc.vector.tensor_scalar(c.xn[:, i, :], c.x[:, ds(blk * BT + i, 1), :].rearrange("p a d -> p (a d)"),
                                       c.ln_mv[:, i, 0:1], c.ln_rstd[:, i:i + 1], ALU.subtract, ALU.mult)
    last.then_inc(sem, 1)


def ln_vector(nc, c, dve, sem, blk, rounds, t=LN):
    ln_vector_stats(nc, c, sem, blk)
    ln_vector_variance(nc, c, dve, sem, rounds, t)
    ln_vector_normalise(nc, c, dve, sem, blk, rounds, t)


def ln_scalar_root(nc, c, act, sem, rounds, t=LN):
    act.wait_ge(sem, t.after("var_eps", rounds))
    nc.scalar.activation(c.ln_std[:, :], c.ln_ve[:, :], ACT.Sqrt).then_inc(sem, 1)


def ln_scalar_read(nc, c, act, sem, rounds, banks, t=LN):
    act.wait_ge(sem, t.after("xT_psum", rounds))
    for k in range(KD):
        last = nc.scalar.activation(c.xT[:, k, :], banks[k][:, :], ACT.Copy)
    last.then_inc(sem, 1)


def ln_tensor(nc, c, pe, sem, rounds, banks, t=LN):
    pe.wait_ge(sem, t.after("normalised", rounds))
    for k in range(KD):
        for i in range(BT):
            last = nc.tensor.transpose(banks[k][:, i * P:(i + 1) * P], c.xn[:, i, k * P:(k + 1) * P], c.ident[:, :])
    last.then_inc(sem, 1)


def ln_scalar(nc, c, act, sem, rounds, banks, t=LN):
    ln_scalar_root(nc, c, act, sem, rounds, t)
    ln_scalar_read(nc, c, act, sem, rounds, banks, t)



def linear_attention(nc, c):
    ITEMS = REP + 2
    SLOTS = [[0, 1], [2], [3, 4], [5]]
    SLOTS_NEXT = [[], [0, 1], [2, 3], [4, 5]]
    CB = AG * BT
    with ExitStack() as ctx:
        def sb(name, shape, dt=F32):
            return ctx.enter_context(nc.sbuf_tensor("a_" + name, shape, dt))

        def psum(name):
            return ctx.enter_context(nc.psum_tensor("a_ps_" + name, [P, 512], F32))

        def sem(name):
            return ctx.enter_context(nc.semaphore("a_" + name))

        w = sb("w_qkv", [P, KD, (AH + 2 * AG) * HD])
        wo = sb("w_out", [P, AH, D])
        cos, sin = sb("cos", [P, S]), sb("sin_crossed", [P, S])
        mask = sb("mask", [P, P])
        qf, kf = sb("q_features", [P, 2, REP, S]), sb("k_features", [P, 2, S])
        kt, v = sb("k_tokens", [P, 2, BT, HD]), sb("v_tokens_ones", [P, 2, BT, HD + 1])
        t1, t2 = sb("roped", [P, 2, S]), sb("rope_sin", [P, 2, S])
        en = sb("exp_neg", [P, 2, S])
        sc = sb("masked_scores", [P, REP, P])
        den, rden = sb("den", [P, 2, REP // 2, 1]), sb("rden", [P, 2, REP // 2, 1])
        st = sb("state", [P, 2, HD + 1])
        ot = sb("out_tokens", [P, 2, REP // 2, HD])
        o = sb("out_features", [P, 2, REP, P])
        y = [psum("y0"), psum("y1")]
        pj = [psum("proj0"), psum("proj1")]
        s_ps, st_ps = psum("scores_outT"), psum("state_kT")
        o_ps = ctx.enter_context(nc.psum_tensor("a_ps_out", [P, 2, 512], F32))
        o4 = o_ps[:, :, 0:REP // 2 * (HD + 1)].rearrange("p a (h d) -> p a h d", d=HD + 1)

        ln = sem("ln_steps")
        w_loaded, tables_loaded = [sem(f"w_loaded{g}") for g in range(AG)], sem("tables_loaded")
        ones_set = sem("ones_set")
        projected = sem("projected")
        v_read, roped = sem("v_read"), sem("roped")
        summed, neg_part, exp_neg, featured = sem("summed"), sem("neg_part"), sem("exp_neg"), sem("featured")
        kT_psum, kT_read = sem("kT_psum"), sem("kT_read")
        scored, masked = sem("scored"), sem("masked")
        out_psum, den_read, rden_done, normed = sem("out_psum"), sem("den_read"), sem("rden_done"), sem("normed")
        outT_psum = sem("outT_psum")
        st_psum, st_read = sem("state_psum"), sem("state_read")
        out_done, added_psum, added = sem("out_done"), sem("y_psum"), sem("added")

        def kx(G):
            return G * (REP + 1)

        def making(g, ch, last):
            if g + 1 < AG:
                return (0, g + 1), SLOTS[ch]
            return (1, 0), [] if last else SLOTS_NEXT[ch]

        def blocks(engine, first, body):
            first()
            body(0, True, False)
            with engine.Fori(1, NB - 1) as b:
                body(b, False, False)
            body(NB - 1, False, True)

        block = ctx.enter_context(nc.Block())

        @block.sync
        def _(sp):
            load_x(c, sp)
            wv, wide = c.dram["a_w"].rearrange("(k p) n -> p k n", p=P), ITEMS * HD
            for g in range(AG):
                sp.dma_start(w[:, :, g * wide:(g + 1) * wide], wv[:, :, g * wide:(g + 1) * wide])\
                    .then_inc(w_loaded[g], 16)
                if g == 0:
                    sp.dma_start(cos[:, :], c.dram["a_cos"]).then_inc(tables_loaded, 16)
                    sp.dma_start(sin[:, :], c.dram["a_sin"]).then_inc(tables_loaded, 16)
                    sp.dma_start(mask[:, :], c.dram["a_mask"]).then_inc(tables_loaded, 16)
            load_rest_of_x(c, sp)
            sp.dma_start(wo[:, :, :], c.dram["a_wo"].rearrange("(h p) n -> p h n", p=P)).then_inc(c.a_loaded, 16)
            load_expert_weights(c, sp)

        @block.tensor
        def _(pe):
            def project(b, g, m, first):
                G = b * AG + g
                if not (first and m < 2):
                    if m == 0 or m == 1:
                        pe.wait_ge(roped, kx(G) - 2 + m + 1)
                    elif m == 2:
                        pe.wait_ge(v_read, G + 1)
                    else:
                        pe.wait_ge(roped, kx(G) + m - 2)
                if m == 0 and (first or isinstance(b, int) and b == 0):
                    pe.wait_ge(w_loaded[g], 16)
                bank = pj[m % 2]
                lo = (g * ITEMS + m) * HD
                if m == 0:
                    for i in range(BT):
                        for k in range(KD):
                            last = nc.tensor.matmul(bank[:, i * HD:(i + 1) * HD], c.xT[:, k, i * P:(i + 1) * P],
                                                    w[:, k, lo:lo + HD], start=(k == 0), stop=(k == KD - 1))
                else:
                    for k in range(KD):
                        last = nc.tensor.matmul(bank[:, :], w[:, k, lo:lo + HD], c.xT[:, k, :],
                                                start=(k == 0), stop=(k == KD - 1))
                last.then_inc(projected, 1)

            def transpose_k(b, g):
                G = b * AG + g
                pe.wait_ge(featured, kx(G) + 1)
                for i in range(BT):
                    last = nc.tensor.transpose(st_ps[:, i * P:(i + 1) * P], kf[:, g % 2, i * P:(i + 1) * P],
                                               c.ident[:, :])
                last.then_inc(kT_psum, 1)

            def scores(b, g, ch, first):
                G = b * AG + g
                if ch == 0:
                    pe.wait_ge(featured, kx(G + 1))
                    pe.wait_ge(kT_read, G + 1)
                    pe.wait_ge(v_read, G + 1)
                if not (first and ch == 0 and g == 0):
                    pe.wait_ge(out_done, G * BT + ch)
                nc.tensor.matmul(s_ps[:, :], kf[:, g % 2, ch * P:(ch + 1) * P], qf[:, g % 2, :, ch * P:(ch + 1) * P],
                                 start=True, stop=True).then_inc(scored, 1)

            def outputs(b, g, ch, first):
                G = b * AG + g
                n = G * BT + ch
                pe.wait_ge(masked, n + 1)
                if not (first and ch == 0 and g == 0):
                    pe.wait_ge(normed, n)
                if ch > 0:
                    pe.wait_ge(st_read, G * (BT - 1) + ch)
                for h in range(REP):
                    bank = o4[:, h // 2, h % 2, :]
                    if ch > 0:
                        nc.tensor.matmul(bank, qf[:, g % 2, h, ch * P:(ch + 1) * P], st[:, (ch - 1) % 2, :],
                                         start=True, stop=False)
                    last = nc.tensor.matmul(bank, sc[:, h, :], v[:, g % 2, ch, :], start=(ch == 0), stop=True)
                last.then_inc(out_psum, 1)

            def transpose_out(b, n):
                pe.wait_ge(normed, b * CB + n + 1)
                for h in range(REP):
                    last = nc.tensor.transpose(s_ps[:, h * P:(h + 1) * P], ot[:, h // 2, h % 2, :], c.ident[:, :])
                last.then_inc(outT_psum, 1)

            def state(b, g, ch):
                G = b * AG + g
                if ch > 0:
                    pe.wait_ge(st_read, G * (BT - 1) + ch)
                nc.tensor.matmul(st_ps[:, 0:HD + 1], kt[:, g % 2, ch, :], v[:, g % 2, ch, :],
                                 start=(ch == 0), stop=True, skip_group_check=True).then_inc(st_psum, 1)

            def add_out(b, n, heads, first):
                g, ch = n % CB // BT, n % BT
                if g == 0 and heads[0] == 0 and ch % 2 == 0 and not first:
                    pe.wait_ge(added, 2 * b - (ch == 0))
                if first and n == 0 and heads[0] == 0:
                    pe.wait_ge(c.a_loaded, 32)
                if heads[0] == 0:
                    pe.wait_ge(out_done, b * CB + n + 1)
                for h in heads:
                    last = nc.tensor.matmul(y[ch // 2][:, (ch % 2) * D:(ch % 2 + 1) * D], o[:, ch % 2, h, :],
                                            wo[:, g * REP + h, :], start=(g == 0 and h == 0 and ch % 2 == 0),
                                            stop=(g == AG - 1 and h == REP - 1), skip_group_check=True)
                if heads[-1] == REP - 1:
                    last.then_inc(added_psum, 1)

            pe.wait_ge(c.x_loaded, 32)
            def first():
                ln_tensor(nc, c, pe, ln, 0, pj)
                pe.wait_ge(ln, LN.after("xT", 0))
                for m in range(ITEMS):
                    project(0, 0, m, True)
                transpose_k(0, 0)

            def body(b, first, last):
                for g in range(AG):
                    for ch in range(BT):
                        n = g * BT + ch
                        (ahead, g2), items = making(g, ch, last)
                        late = ahead == 1 and 0 in items
                        if late:
                            add_out(b, n - 2, [0, 1], first)
                        for m in [] if late else items[0:1]:
                            project(b + ahead, g2, m, False)
                        if n >= 1 or not first:
                            transpose_out(b, n - 1)
                        if late:
                            pe.wait_ge(ln, LN.after("xT", b + 1))
                        for m in items if late else items[1:]:
                            project(b + ahead, g2, m, False)
                        if not late and (n >= 2 or not first):
                            add_out(b, n - 2, [0, 1], first)
                        scores(b, g, ch, first)
                        if n >= 2 or not first:
                            add_out(b, n - 2, [2, 3], first)
                        if ch < BT - 1:
                            state(b, g, ch)
                        outputs(b, g, ch, first)
                        if g == AG - 1 and ch == 0:
                            pe.wait_ge(roped, kx(b * AG + AG))
                            ln_tensor(nc, c, pe, ln, b + 1, pj)
                    if g + 1 < AG or not last:
                        pe.wait_ge(st_read, (b * AG + g + 1) * (BT - 1))
                        transpose_k(b + ahead, g2)
                if last:
                    add_out(b, CB - 2, [0, 1, 2, 3], False)
                    transpose_out(b, CB - 1)
                    add_out(b, CB - 1, [0, 1, 2, 3], False)

            blocks(pe, first, body)

        @block.vector
        def _(dve):
            def rope(b, g, m, start=False):
                G = b * AG + g
                j = m - 1
                r = m % 2
                dve.wait_ge(projected, G * ITEMS + m + 1)
                if not (start and j < 2):
                    dve.wait_ge(featured, kx(G) + max(j - 1, 0))
                nc.vector.tensor_tensor(t1[:, r, :], pj[r][:, :], cos[:, :], ALU.mult)
                nc.vector.tensor_tensor(t2[0:64, r, :], pj[r][64:128, :], sin[64:128, :], ALU.mult)
                nc.vector.tensor_tensor(t2[64:128, r, :], pj[r][0:64, :], sin[0:64, :], ALU.mult)\
                    .then_inc(roped, 1)

            def feature(b, g, m):
                G = b * AG + g
                j = m - 1
                r = m % 2
                dve.wait_ge(exp_neg, kx(G) + j + 1)
                dst = kf[:, g % 2, :] if m == 1 else qf[:, g % 2, m - 2, :]
                nc.vector.scalar_tensor_tensor(out=dst, in0=t1[:, r, :], scalar=0.0, in1=en[:, r, :],
                                               op0=ALU.max, op1=ALU.add).then_inc(featured, 1)

            def mask_scores(b, g, ch, first):
                n = (b * AG + g) * BT + ch
                dve.wait_ge(scored, n + 1)
                if not (first and g == 0 and ch == 0):
                    dve.wait_ge(out_psum, n)
                nc.vector.tensor_tensor(sc[:, :, :], s_ps[:, :].rearrange("p (h t) -> p h t", h=REP),
                                        mask[:, :].unsqueeze(1).to_broadcast([P, REP, P]), ALU.mult)\
                    .then_inc(masked, 1)

            def divide(n):
                dve.wait_ge(out_psum, n + 1)
                nc.vector.tensor_scalar(den[:, :, :, :], o4[:, :, :, HD:HD + 1], A_EPS, None, ALU.add)\
                    .then_inc(den_read, 1)
                dve.wait_ge(den_read, n + 1)
                nc.vector.reciprocal(rden[:, :, :, :], den[:, :, :, :]).then_inc(rden_done, 1)
                dve.wait_ge(rden_done, n + 1)
                nc.vector.tensor_tensor(ot[:, :, :, :], o4[:, :, :, 0:HD],
                                        rden[:, :, :, :].to_broadcast([P, 2, REP // 2, HD]), ALU.mult)\
                    .then_inc(normed, 1)

            nc.vector.memset(v[:, :, :, HD:HD + 1], 1.0).then_inc(ones_set, 1)
            dve.wait_ge(c.x_loaded, 32)
            dve.wait_ge(ones_set, 1)

            def residual(b, j):
                dve.wait_ge(added_psum, b * CB + CB - 2 + 2 * j)
                xs = c.x[:, ds(b * BT + 2 * j, 2), :]
                nc.vector.tensor_tensor(xs, xs, y[j][:, :].rearrange("p (a d) -> p a d", a=2), ALU.add)\
                    .then_inc(added, 1)

            def first():
                ln_vector(nc, c, dve, ln, 0, 0)
                dve.wait_ge(tables_loaded, 48)
                for m in range(1, ITEMS):
                    rope(0, 0, m, start=True)
                    if m > 1:
                        feature(0, 0, m - 1)
                feature(0, 0, ITEMS - 1)

            def body(b, first, last):
                for g in range(AG):
                    pending = []
                    for ch in range(BT):
                        (ahead, g2), items = making(g, ch, last)
                        if g + ch > 0 or not first:
                            divide((b * AG + g) * BT + ch - 1)
                        for m in items:
                            if m == 0:
                                continue
                            rope(b + ahead, g2, m)
                            if pending and pending[0] not in items:
                                feature(b + ahead, g2, pending.pop(0))
                            pending.append(m)
                        mask_scores(b, g, ch, first)
                        if g == AG - 2 and ch == 2:
                            if first:
                                dve.wait_ge(c.a_loaded, 32)
                            if last:
                                dve.wait_ge(added, 2)
                            ln_vector_stats(nc, c, ln, block_of(b + 1))
                        if g == AG - 2 and ch == 3:
                            ln_vector_variance(nc, c, dve, ln, b + 1)
                        if len(pending) > 1:
                            feature(b + ahead, g2, pending.pop(0))
                        if g == 0 and ch < 2 and not first:
                            residual(b - 1, ch)
                        if g == AG - 1 and ch == 0:
                            ln_vector_normalise(nc, c, dve, ln, block_of(b + 1), b + 1)
                    for m in pending:
                        feature(b + ahead, g2, m)
                if last:
                    residual(b, 0)
                    divide((b + 1) * CB - 1)
                    residual(b, 1)
                    dve.wait_ge(added, 2 * NB)

            blocks(dve, first, body)

        @block.gpsimd
        def _(pool):
            def add_rope(b, g, m):
                G = b * AG + g
                j = m - 1
                r = m % 2
                pool.wait_ge(roped, kx(G) + j + 1)
                nc.gpsimd.tensor_tensor(t1[:, r, :], t1[:, r, :], t2[:, r, :], ALU.add).then_inc(summed, 1)

            def first():
                for m in range(1, ITEMS):
                    add_rope(0, 0, m)

            def body(b, first, last):
                for g in range(AG):
                    (ahead, g2), _ = making(g, 0, last)
                    if not (last and ahead):
                        for m in range(1, ITEMS):
                            add_rope(b + ahead, g2, m)

            blocks(pool, first, body)

        @block.scalar
        def _(act):
            def read_v(b, g):
                G = b * AG + g
                act.wait_ge(projected, G * ITEMS + 1)
                nc.scalar.activation(v[:, g % 2, :, 0:HD], pj[0][:, :].rearrange("p (t d) -> p t d", t=BT), ACT.Copy)\
                    .then_inc(v_read, 1)

            def exp_negative(b, g, m, start=False):
                G = b * AG + g
                j = m - 1
                r = m % 2
                act.wait_ge(summed, kx(G) + j + 1)
                if not (start and j < 2):
                    act.wait_ge(featured, kx(G) + max(j - 1, 0))
                nc.scalar.activation(en[:, r, :], t1[:, r, :], ACT.Relu, scale=-1.0).then_inc(neg_part, 1)
                act.wait_ge(neg_part, kx(G) + j + 1)
                nc.scalar.activation(en[:, r, :], en[:, r, :], ACT.Exp, scale=-1.0).then_inc(exp_neg, 1)

            def read_k(b, g):
                act.wait_ge(kT_psum, b * AG + g + 1)
                nc.scalar.activation(kt[:, g % 2, :, :].rearrange("p t d -> p (t d)"), st_ps[:, :], ACT.Copy)\
                    .then_inc(kT_read, 1)

            def read_state(b, g, ch):
                G = b * AG + g
                act.wait_ge(st_psum, G * (BT - 1) + ch + 1)
                nc.scalar.activation(st[:, ch % 2, :], st_ps[:, 0:HD + 1], ACT.Copy).then_inc(st_read, 1)

            def read_out(b, n):
                act.wait_ge(outT_psum, b * CB + n + 1)
                nc.scalar.activation(o[:, n % 2, :, :].rearrange("p h t -> p (h t)"), s_ps[:, :], ACT.Copy)\
                    .then_inc(out_done, 1)

            act.wait_ge(ones_set, 1)
            def first():
                ln_scalar(nc, c, act, ln, 0, pj)
                read_v(0, 0)
                for m in range(1, ITEMS):
                    exp_negative(0, 0, m, start=True)
                read_k(0, 0)

            def body(b, first, last):
                for g in range(AG):
                    for ch in range(BT):
                        (ahead, g2), items = making(g, ch, last)
                        if 0 in items:
                            read_v(b + ahead, g2)
                        if g + ch > 0 or not first:
                            read_out(b, g * BT + ch - 1)
                        if ch < BT - 1:
                            read_state(b, g, ch)
                        for m in items:
                            if m > 0:
                                exp_negative(b + ahead, g2, m)
                        if g == AG - 1 and ch == 0:
                            ln_scalar_read(nc, c, act, ln, b + 1, pj)
                    if g == AG - 2:
                        ln_scalar_root(nc, c, act, ln, b + 1)
                    if g + 1 < AG or not last:
                        read_k(b + ahead, g2)
                if last:
                    read_out(b, CB - 1)

            blocks(act, first, body)



def expert_weights(nc, c):
    with ExitStack() as ctx:
        def sb(name, shape, dt=F32):
            return ctx.enter_context(nc.sbuf_tensor("e_" + name, shape, dt))

        def sem(name):
            return ctx.enter_context(nc.semaphore("e_" + name))

        scale_gu = sb("scale_gate_up", [KR, EX * 2 * EI])
        scale_d = sb("scale_down", [P, EX // 2, D])
        mu = sb("mask_up", [P, KD, NE])
        mup = sb("mask_up_padded", [P, KD, EX * NE])
        idx, idxf = sb("mapping", [NE, NE], I32), sb("mapping_f32", [NE, NE])
        row = sb("row_number", [NE, 1])
        ps = [ctx.enter_context(nc.psum_tensor(f"e_ps{i}", [P, 512], F32)) for i in range(4)]
        masks_loaded, loaded, gu_ready, ma_ready = sem("masks_loaded"), sem("loaded"), sem("gu_psum"), sem("ma_psum")
        gu_read, ma_read, small = sem("gu_read"), sem("ma_read"), sem("small")
        block = ctx.enter_context(nc.Block())

        @block.sync
        def _(sp):
            sp.dma_start(mu[:, :, :], c.dram["mu"].rearrange("(k p) n -> p k n", p=P)).then_inc(masks_loaded, 16)
            sp.dma_start(mup[:, :, :], c.dram["mup"].rearrange("(k p) n -> p k n", p=P)).then_inc(masks_loaded, 16)
            sp.dma_start(scale_gu[:, :], c.dram["scale_gu"].partition_broadcast(KR)).then_inc(loaded, 16)
            for f in range(EX):
                sp.dma_start(scale_d[(f % 2) * KR:(f % 2 + 1) * KR, f // 2, :],
                             c.dram["scale_d"][f, :].partition_broadcast(KR)).then_inc(loaded, 16)
            sp.dma_start(idx[:, :], c.dram["mapping"].partition_broadcast(NE)).then_inc(loaded, 16)
            sp.dma_start(row[:, :], c.dram["row"]).then_inc(loaded, 16)

        @block.tensor
        def _(pe):
            pe.wait_ge(masks_loaded, 32)
            for f in range(EX):
                if f >= 2:
                    pe.wait_ge(gu_read, f - 1)
                    pe.wait_ge(ma_read, f - 1)
                for k in range(KD):
                    last = nc.tensor.matmul(ps[f % 2][0:EK, 0:2 * EI], mu[:, k, f * EK:(f + 1) * EK],
                                            c.w1[:, k, f * W1N:f * W1N + 2 * EI], start=(k == 0), stop=(k == KD - 1))
                last.then_inc(gu_ready, 1)
                for k in range(KD):
                    last = nc.tensor.matmul(ps[2 + f % 2][0:NE, 0:2 * KR], mup[:, k, f * NE:(f + 1) * NE],
                                            c.w1[:, k, f * W1N + 2 * EI:(f + 1) * W1N],
                                            start=(k == 0), stop=(k == KD - 1))
                last.then_inc(ma_ready, 1)

        @block.scalar
        def _(act):
            for f in range(EX):
                act.wait_ge(gu_ready, f + 1)
                nc.scalar.activation(c.qb[KR:KR + EK, f * 2 * EI:(f + 1) * 2 * EI], ps[f % 2][0:EK, 0:2 * EI],
                                     ACT.Copy).then_inc(gu_read, 1)

        @block.vector
        def _(dve):
            for f in range(EX):
                dve.wait_ge(ma_ready, f + 1)
                nc.vector.tensor_copy(c.ma[:, f * 2 * KR:(f + 1) * 2 * KR], ps[2 + f % 2][0:NE, 0:2 * KR])\
                    .then_inc(ma_read, 1)
                if f == EX // 2:
                    dve.wait_ge(loaded, 16 * 11)
                    nc.vector.tensor_tensor(c.qb[0:KR, :], c.qb[0:KR, :], scale_gu[:, :], ALU.mult)
                if f == EX - 2:
                    nc.vector.tensor_tensor(c.qbd[:, :, :], c.qbd[:, :, :], scale_d[:, :, :], ALU.mult)
            nc.vector.tensor_copy(idxf[:, :], idx[:, :]).then_inc(small, 1)
            dve.wait_ge(small, 1)
            nc.vector.tensor_scalar(c.onehot[:, :], idxf[:, :], row[:, 0:1], None, ALU.is_equal).then_inc(small, 1)



def experts(nc, c, tag, last_layer, ready=False):
    prep = Steps(LN_STEPS + ROUTER_STEPS)
    UB = EX * BT
    EARLY = 4
    with ExitStack() as ctx:
        def sb(name, shape, dt=F32):
            return ctx.enter_context(nc.sbuf_tensor(tag + name, shape, dt))

        def psum(name):
            return ctx.enter_context(nc.psum_tensor(tag + "ps_" + name, [P, 512], F32))

        def sem(name):
            return ctx.enter_context(nc.semaphore(tag + name))

        rmax, lg, ex = sb("row_max", [P, BT]), sb("shifted", [P, BT, NE]), sb("exp", [P, BT, NE])
        esum, erec = sb("exp_sum", [P, BT]), sb("exp_rec", [P, BT])
        pr = sb("probs", [P, BT, NE + 2])
        top, rest = sb("top8", [P, BT, 8]), sb("others", [P, BT, NE + 2])
        wd, wdT = sb("w_dense", [P, BT, NE]), sb("w_denseT", [NE, S])
        flat, pen = sb("flat", [P, BT, EX, EK]), sb("penalty", [P, BT, EX, EK])
        fm, gmax = sb("masked", [P, BT, EX, EK]), sb("group_max", [P, BT, EX])
        gsum, grec = sb("group_sum", [P, BT, EX]), sb("group_rec", [P, BT, EX])
        fe = ex[:, :, :].rearrange("p t (f k) -> p t f k", f=EX)
        scal = sb("scalar", [P, BT, EX])
        soft, softT = sb("soft", [P, BT, NE]), sb("softT", [NE, S])
        shT = sb("shared_hT", [P, 2, 3, P])
        aw, awT = sb("low_rank", [P, 2, 2, KR + EK]), sb("low_rankT", [KR + EK, 2, 2, P])
        sg, h, hT = sb("silu_gate", [P, 2, EI]), sb("hidden", [P, 2, EI]), sb("hiddenT", [HJ, 2, 2, P])
        xh, xl = sb("xT_high", [P, KD, S], F32R), sb("xT_low", [P, KD, S], F32R)
        w1h, w1l = sb("w1_high", [P, KD, EX * W1N], F32R), sb("w1_low", [P, KD, EX * W1N], F32R)
        dw, dwT = sb("down_low_rank", [P, BT, EX * KR]), sb("down_low_rankT", [P, 2, 4 * P])
        ssg, shh = (dw[:, :, :].rearrange("p t n -> p (t n)")[:, j * 2 * SH:(j + 1) * 2 * SH].rearrange(
            "p (i n) -> p i n", i=2) for j in range(2))
        m_ps = [psum("main0"), psum("main1")]
        t_ps, h_ps, d_ps, r_ps = psum("low_rankT"), psum("hiddenT"), psum("down_low"), psum("router")
        y = [psum("y0"), psum("y1")]
        sh_ps = [(m_ps[0], m_ps[1]), (d_ps, h_ps)]

        steps = sem("prep_steps")
        minus_ones = sem("minus_ones")
        sh_main, sh_silu, sh_h, sh_hT_ps, sh_hT, sh_down = (sem("sh_" + n) for n in
                                                            ["main", "silu", "h", "hT_psum", "hT", "down"])
        main_done, aw_done, aww_done, awT_ps, awT_done = (sem(n) for n in
                                                          ["main", "aw", "aw_soft", "awT_psum", "awT"])
        gate_up, silu_done, h_done, hT_ps, hT_done = (sem(n) for n in
                                                      ["gate_up", "silu", "h", "hT_psum", "hT"])
        xh_done, x_split, w1_high, w1_split = sem("x_high"), sem("x_split"), sem("w1_high"), sem("w1_split")
        w1_rest_high, w1_rest_split = sem("w1_rest_high"), sem("w1_rest_split")
        down_done, dw_done = sem("down"), sem("dw")
        dwT_ps, dwT_done, closed, added = sem("dwT_psum"), sem("dwT"), sem("closed"), sem("added")
        stored = sem("stored")

        def unit(blk, e, i, back=0):
            e, i = (e, i - back) if i >= back else (e - 1, i - back + BT)
            return e, i, blk * UB + e * BT + i

        def split_w1(compute, engine, e, before, high_done, done):
            src, high, low = (w[:, :, e * W1N:(e + 1) * W1N] for w in (c.w1, w1h, w1l))
            compute.tensor_copy(high, src).then_inc(high_done, 1)
            engine.wait_ge(high_done, before + 1)
            compute.tensor_tensor(low, src, high.bitcast(F32), ALU.subtract).then_inc(done, 1)

        def blocks(engine, start, body, closing):
            start(0)
            body(0)
            with engine.Fori(1, NB) as b:
                start(b, between=True)
                body(b)
            if last_layer:
                closing(NB - 1)
            else:
                start(NB, between=True)

        block = ctx.enter_context(nc.Block())

        def run_units(engine, blk, step):
            for i in range(BT):
                step(blk, 0, i, i)
            with engine.Fori(1, EX) as e:
                for i in range(BT):
                    step(blk, e, i, BT)
            step(blk, EX, 0, BT, tail=1)
            step(blk, EX, 1, BT, tail=2)

        @block.tensor
        def _(pe):
            def ychunk(i):
                return y[i // 2][:, (i % 2) * D:(i % 2 + 1) * D]

            def shared_main(blk, i):
                if i >= 2:
                    pe.wait_ge(sh_h, blk * BT + i - 1)
                for n in range(2):
                    for k in range(KD):
                        last = nc.tensor.matmul(sh_ps[i % 2][n][:, 0:SH], c.xT[:, k, i * P:(i + 1) * P],
                                                c.shgu[:, k, n * SH:(n + 1) * SH], start=(k == 0), stop=(k == KD - 1))
                last.then_inc(sh_main, 1)

            def shared_transpose(blk, i):
                pe.wait_ge(sh_h, blk * BT + i + 1)
                if i > 0:
                    pe.wait_ge(sh_hT, blk * BT + i)
                for j, (lo, n) in enumerate(SHC):
                    last = nc.tensor.transpose(t_ps[0:n, j * P:(j + 1) * P], shh[:, i % 2, lo:lo + n], c.ident[:, :])
                last.then_inc(sh_hT_ps, 1)

            def shared_down(blk, i):
                if i == 0 and not isinstance(blk, int):
                    pe.wait_ge(added, blk)
                pe.wait_ge(sh_hT, blk * BT + i + 1)
                for j, (lo, n) in enumerate(SHC):
                    last = nc.tensor.matmul(ychunk(i), shT[0:n, i % 2, j, :], c.shd[0:n, j, :],
                                            start=(i % 2 == 0 and j == 0), stop=False, skip_group_check=True)
                last.then_inc(sh_down, 1)

            def step(blk, e0, i0, have, tail=0):
                if not tail:
                    e, i, n = unit(blk, e0, i0)
                    if have >= 2:
                        pe.wait_ge(h_done, n - 1)
                    if isinstance(blk, int) and i0 == 0 and have == BT:
                        pe.wait_ge(w1_rest_split, EX - EARLY)
                    bank = m_ps[i % 2]
                    for k in range(KD):
                        high, low = w1h[:, k, ds(e * W1N, W1N)], w1l[:, k, ds(e * W1N, W1N)]
                        for j, (xs, ws) in enumerate([(xh, high), (xh, low), (xl, high)]):
                            nc.tensor.matmul(bank[:, 0:W1N], xs[:, k, i * P:(i + 1) * P], ws,
                                             start=(k == 0 and j == 0), stop=False, skip_group_check=True)
                    nc.tensor.matmul(bank[:, 2 * EI:W1N], softT[:, i * P:(i + 1) * P],
                                     c.ma[:, ds(e * 2 * KR, 2 * KR)], start=False, stop=False,
                                     skip_group_check=True).then_inc(main_done, 1)
                if have >= 1 and tail < 2:
                    e, i, n = unit(blk, e0, i0, 1)
                    pe.wait_ge(awT_done, n + 1)
                    for s in range(2):
                        last = nc.tensor.matmul(m_ps[i % 2][:, s * EI:(s + 1) * EI], awT[:, i % 2, s, :],
                                                c.qb[:, ds(e * 2 * EI + s * EI, EI)], start=False, stop=(s == 1),
                                                skip_group_check=True)
                    last.then_inc(gate_up, 1)
                if not tail:
                    e, i, n = unit(blk, e0, i0)
                    pe.wait_ge(aw_done, n + 1)
                    pe.wait_ge(aww_done, n + 1)
                    for s in range(2):
                        last = nc.tensor.transpose(t_ps[0:KR + EK, s * P:(s + 1) * P], aw[:, i % 2, s, :],
                                                   c.ident[:, :])
                    last.then_inc(awT_ps, 1)
                if have >= 2:
                    e, i, n = unit(blk, e0, i0, 2)
                    pe.wait_ge(hT_done, n + 1)
                    if have >= 3:
                        pe.wait_ge(dw_done, n)
                    for j in range(2):
                        nc.tensor.matmul(ychunk(i), hT[:, i % 2, j, :], c.w2[:, j, ds(e * W2N, D)],
                                         start=False, stop=False, skip_group_check=True)
                    for j in range(2):
                        last = nc.tensor.matmul(d_ps[:, 0:KR], hT[:, i % 2, j, :],
                                                c.w2[:, j, ds(e * W2N + D, KR)], start=(j == 0), stop=(j == 1))
                    last.then_inc(down_done, 1)
                if have >= 1 and tail < 2:
                    e, i, n = unit(blk, e0, i0, 1)
                    pe.wait_ge(h_done, n + 1)
                    for j in range(2):
                        last = nc.tensor.transpose(h_ps[0:HJ, j * P:(j + 1) * P], h[:, i % 2, j * HJ:(j + 1) * HJ],
                                                   c.ident[:, :])
                    last.then_inc(hT_ps, 1)

            def closing(blk):
                def transpose(i):
                    if i >= 2:
                        pe.wait_ge(dwT_done, blk * BT + i - 1)
                    bank = (t_ps, h_ps)[i % 2]
                    for q in range(4):
                        last = nc.tensor.transpose(bank[:, q * P:(q + 1) * P], dw[:, i, q * P:(q + 1) * P],
                                                   c.ident[:, :])
                    last.then_inc(dwT_ps, 1)

                pe.wait_ge(dw_done, (blk + 1) * UB)
                transpose(0)
                for i in range(BT):
                    if i + 1 < BT:
                        transpose(i + 1)
                    pe.wait_ge(dwT_done, blk * BT + i + 1)
                    for q in range(4):
                        last = nc.tensor.matmul(ychunk(i), dwT[:, i % 2, q * P:(q + 1) * P], c.qbd[:, q, :],
                                                start=False, stop=(q == 3), skip_group_check=True)
                    last.then_inc(closed, 1)

            def start(blk, between=False):
                if between:
                    closing(blk - 1)
                if between or not ready:
                    ln_tensor(nc, c, pe, steps, blk, m_ps, prep)

            def body(blk):
                pe.wait_ge(steps, prep.after("xT", blk))
                for i in range(BT):
                    for k in range(KD):
                        last = nc.tensor.matmul(r_ps[:, i * NE:(i + 1) * NE], c.xT[:, k, i * P:(i + 1) * P],
                                                c.wrt[:, k, :], start=(k == 0), stop=(k == KD - 1))
                last.then_inc(steps, 1)
                shared_main(blk, 0)
                shared_main(blk, 1)
                shared_transpose(blk, 0)
                shared_main(blk, 2)
                pe.wait_ge(steps, prep.after("w_dense", blk))
                apart(pe, c)
                for i in range(BT):
                    last = nc.tensor.transpose(r_ps[0:NE, i * P:(i + 1) * P], wd[:, i, :], c.ident[:, :])
                last.then_inc(steps, 1)
                shared_transpose(blk, 1)
                shared_down(blk, 0)
                pe.wait_ge(steps, prep.after("w_denseT", blk))
                for i in range(BT):
                    last = nc.tensor.matmul(r_ps[:, i * NE:(i + 1) * NE], wdT[:, i * P:(i + 1) * P], c.onehot[:, :],
                                            start=True, stop=True)
                last.then_inc(steps, 1)
                shared_main(blk, 3)
                shared_transpose(blk, 2)
                shared_down(blk, 1)
                shared_transpose(blk, 3)
                shared_down(blk, 2)
                pe.wait_ge(steps, prep.after("soft", blk))
                apart(pe, c)
                for i in range(BT):
                    last = nc.tensor.transpose(r_ps[0:NE, i * P:(i + 1) * P], soft[:, i, :], c.ident[:, :])
                last.then_inc(steps, 1)
                shared_down(blk, 3)
                pe.wait_ge(steps, prep.after("softT", blk))
                pe.wait_ge(x_split, blk + 1)
                if isinstance(blk, int):
                    pe.wait_ge(w1_split, EARLY)
                run_units(pe, blk, step)

            blocks(pe, start, body, closing)

        @block.vector
        def _(dve):
            def at(name, blk):
                dve.wait_ge(steps, prep.after(name, blk))

            def step(blk, e0, i0, have, tail=0):
                if not tail:
                    e, i, n = unit(blk, e0, i0)
                    dve.wait_ge(main_done, n + 1)
                    a = m_ps[i % 2][:, 2 * EI:W1N].rearrange("p (s k r) -> p s k r", s=2, k=EK)
                    w = soft[:, i, ds(e * EK, EK)].unsqueeze(1).unsqueeze(3).to_broadcast([P, 2, EK, ER])
                    nc.vector.tensor_tensor(aw[:, i % 2, :, 0:KR].rearrange("p s (k r) -> p s k r", k=EK), a, w,
                                            ALU.mult).then_inc(aw_done, 1)
                if have >= 1 and tail < 2:
                    e, i, n = unit(blk, e0, i0, 1)
                    dve.wait_ge(silu_done, n + 1)
                    nc.vector.scalar_tensor_tensor(out=h[:, i % 2, :], in0=sg[:, i % 2, :],
                                                   scalar=scal[:, i, ds(e, 1)], in1=m_ps[i % 2][:, EI:2 * EI],
                                                   op0=ALU.mult, op1=ALU.mult).then_inc(h_done, 1)
                if isinstance(blk, int) and have == i0 < EX - EARLY:
                    split_w1(nc.vector, dve, EARLY + i0, i0, w1_rest_high, w1_rest_split)
                if have >= 2:
                    e, i, n = unit(blk, e0, i0, 2)
                    dve.wait_ge(down_done, n + 1)
                    a = d_ps[:, 0:KR].rearrange("p (k r) -> p k r", k=EK)
                    w = soft[:, i, ds(e * EK, EK)].unsqueeze(2).to_broadcast([P, EK, ER])
                    nc.vector.tensor_tensor(dw[:, i, ds(e * KR, KR)].rearrange("p (k r) -> p k r", k=EK), a, w,
                                            ALU.mult).then_inc(dw_done, 1)

            nc.vector.memset(pr[:, :, NE:NE + 2], -1.0).then_inc(minus_ones, 1)
            dve.wait_ge(minus_ones, 1)

            def shared_h(blk, i):
                dve.wait_ge(sh_silu, blk * BT + i + 1)
                nc.vector.tensor_tensor(shh[:, i % 2, :], ssg[:, i % 2, :], sh_ps[i % 2][1][:, 0:SH], ALU.mult)\
                    .then_inc(sh_h, 1)

            def closing(blk):
                for j in range(2):
                    dve.wait_ge(closed, blk * BT + 2 * (j + 1))
                    xs = c.x[:, ds(blk * BT + 2 * j, 2), :]
                    last = nc.vector.tensor_tensor(xs, xs, y[j][:, :].rearrange("p (a d) -> p a d", a=2), ALU.add)
                last.then_inc(added, 1)

            def start(blk, between=False):
                if between or not ready:
                    ln_vector(nc, c, dve, steps, block_of(blk), blk, prep)
                else:
                    dve.sem_inc(steps, len(LN_STEPS))
                if between:
                    closing(blk - 1)

            def body(blk):
                at("logits", blk)
                r4 = r_ps[:, 0:BT * NE].rearrange("p (t n) -> p t n", t=BT)
                nc.vector.reduce_max(rmax[:, :], r4, AX).then_inc(steps, 1)
                at("row_max", blk)
                nc.vector.tensor_tensor(lg[:, :, :], r4, rmax[:, :].unsqueeze(2).to_broadcast([P, BT, NE]),
                                        ALU.subtract).then_inc(steps, 1)
                at("exp", blk)
                nc.vector.reduce_sum(esum[:, :], ex[:, :, :], AX).then_inc(steps, 1)
                at("exp_sum", blk)
                nc.vector.reciprocal(erec[:, :], esum[:, :]).then_inc(steps, 1)
                at("exp_rec", blk)
                nc.vector.tensor_tensor(pr[:, :, 0:NE], ex[:, :, :], erec[:, :].unsqueeze(2).to_broadcast([P, BT, NE]),
                                        ALU.mult).then_inc(steps, 1)
                shared_h(blk, 0)
                at("probs", blk)
                apart(dve, c)
                for i in range(BT):
                    last = nc.vector.max(top[:, i, :], pr[:, i, 0:NE])
                last.then_inc(steps, 1)
                at("top8", blk)
                nc.vector.memset(top[:, :, TOPK:8], -1.0).then_inc(steps, 1)
                at("top6", blk)
                apart(dve, c)
                for i in range(BT):
                    last = nc.vector.match_replace(rest[:, i, :], top[:, i, :], pr[:, i, :], 0.0)
                last.then_inc(steps, 1)
                at("others", blk)
                nc.vector.tensor_tensor(wd[:, :, :], pr[:, :, 0:NE], rest[:, :, 0:NE], ALU.subtract)\
                    .then_inc(steps, 1)
                shared_h(blk, 1)
                dve.wait_ge(xh_done, blk + 1)
                nc.vector.tensor_tensor(xl[:, :, :], c.xT[:, :, :], xh[:, :, :].bitcast(F32), ALU.subtract)\
                    .then_inc(x_split, 1)
                shared_h(blk, 2)
                at("flat_psum", blk)
                nc.vector.tensor_copy(flat[:, :, :, :].rearrange("p t f k -> p (t f k)"), r_ps[:, 0:BT * NE])\
                    .then_inc(steps, 1)
                at("flat", blk)
                nc.vector.reduce_sum(scal[:, :, :], flat[:, :, :, :], AX).then_inc(steps, 1)
                at("scalar", blk)
                nc.vector.tensor_scalar(pen[:, :, :, :], flat[:, :, :, :], 0.0, -1e9, ALU.is_equal, ALU.mult)\
                    .then_inc(steps, 1)
                at("penalty", blk)
                nc.vector.tensor_tensor(fm[:, :, :, :], flat[:, :, :, :], pen[:, :, :, :], ALU.add).then_inc(steps, 1)
                at("masked", blk)
                nc.vector.reduce_max(gmax[:, :, :], fm[:, :, :, :], AX).then_inc(steps, 1)
                at("group_max", blk)
                g4 = [P, BT, EX, EK]
                nc.vector.tensor_tensor(fm[:, :, :, :], fm[:, :, :, :], gmax[:, :, :].unsqueeze(3).to_broadcast(g4),
                                        ALU.subtract).then_inc(steps, 1)
                shared_h(blk, 3)
                at("group_exp", blk)
                nc.vector.reduce_sum(gsum[:, :, :], fe[:, :, :, :], AX).then_inc(steps, 1)
                at("group_sum", blk)
                nc.vector.reciprocal(grec[:, :, :], gsum[:, :, :]).then_inc(steps, 1)
                at("group_rec", blk)
                nc.vector.tensor_tensor(soft[:, :, :].rearrange("p t (f k) -> p t f k", f=EX), fe[:, :, :, :],
                                        grec[:, :, :].unsqueeze(3).to_broadcast(g4), ALU.mult).then_inc(steps, 1)
                run_units(dve, blk, step)

            blocks(dve, start, body, closing)

        @block.gpsimd
        def _(pool):
            def step(blk, e0, i0, have, tail=0):
                if tail:
                    return
                e, i, n = unit(blk, e0, i0)
                if have >= 2:
                    pool.wait_ge(awT_ps, n - 1)
                apart(pool, c)
                w = soft[:, i, ds(e * EK, EK)].unsqueeze(1).to_broadcast([P, 2, EK])
                nc.gpsimd.tensor_copy(aw[:, i % 2, :, KR:KR + EK], w).then_inc(aww_done, 1)

            def body(blk):
                pool.wait_ge(steps, prep.after("soft", blk))
                run_units(pool, blk, step)

            for e in range(EARLY):
                split_w1(nc.gpsimd, pool, e, e, w1_high, w1_split)
            body(0)
            with pool.Fori(1, NB) as blk:
                body(blk)

        @block.scalar
        def _(act):
            def step(blk, e0, i0, have, tail=0):
                if have >= 1 and tail < 2:
                    e, i, n = unit(blk, e0, i0, 1)
                    act.wait_ge(gate_up, n + 1)
                    if have >= 3:
                        act.wait_ge(h_done, n - 1)
                    nc.scalar.activation(sg[:, i % 2, :], m_ps[i % 2][:, 0:EI], ACT.Silu).then_inc(silu_done, 1)
                if not tail:
                    e, i, n = unit(blk, e0, i0)
                    act.wait_ge(awT_ps, n + 1)
                    nc.scalar.activation(awT[:, i % 2, :, :].rearrange("p s t -> p (s t)"), t_ps[0:KR + EK, 0:2 * P],
                                         ACT.Copy).then_inc(awT_done, 1)
                if have >= 1 and tail < 2:
                    e, i, n = unit(blk, e0, i0, 1)
                    act.wait_ge(hT_ps, n + 1)
                    nc.scalar.activation(hT[:, i % 2, :, :].rearrange("p s t -> p (s t)"), h_ps[0:HJ, 0:2 * P],
                                         ACT.Copy).then_inc(hT_done, 1)

            def shared_silu(blk, i):
                act.wait_ge(sh_main, blk * BT + i + 1)
                if i >= 2:
                    act.wait_ge(sh_h, blk * BT + i - 1)
                nc.scalar.activation(ssg[:, i % 2, :], sh_ps[i % 2][0][:, 0:SH], ACT.Silu).then_inc(sh_silu, 1)

            def shared_hT(blk, i):
                act.wait_ge(sh_hT_ps, blk * BT + i + 1)
                if i >= 2:
                    act.wait_ge(sh_down, blk * BT + i - 1)
                nc.scalar.activation(shT[:, i % 2, 0:2, :].rearrange("p s t -> p (s t)"), t_ps[:, 0:2 * P], ACT.Copy)
                n = SHC[2][1]
                nc.scalar.activation(shT[0:n, i % 2, 2, :], t_ps[0:n, 2 * P:3 * P], ACT.Copy).then_inc(sh_hT, 1)

            def closing(blk, tiles):
                for i in tiles:
                    act.wait_ge(dwT_ps, blk * BT + i + 1)
                    if i >= 2:
                        act.wait_ge(closed, blk * BT + i - 1)
                    nc.scalar.activation(dwT[:, i % 2, :], (t_ps, h_ps)[i % 2][:, :], ACT.Copy).then_inc(dwT_done, 1)

            def start(blk, between=False):
                if not between:
                    if not ready:
                        ln_scalar(nc, c, act, steps, blk, m_ps, prep)
                    return
                closing(blk - 1, [0, 1])
                ln_scalar_root(nc, c, act, steps, blk, prep)
                closing(blk - 1, [2, 3])
                ln_scalar_read(nc, c, act, steps, blk, m_ps, prep)

            def body(blk):
                act.wait_ge(steps, prep.after("shifted", blk))
                nc.scalar.activation(ex[:, :, :], lg[:, :, :], ACT.Exp).then_inc(steps, 1)
                shared_silu(blk, 0)
                shared_silu(blk, 1)
                nc.scalar.activation(xh[:, :, :], c.xT[:, :, :], ACT.Copy).then_inc(xh_done, 1)
                shared_hT(blk, 0)
                shared_silu(blk, 2)
                act.wait_ge(steps, prep.after("w_denseT_psum", blk))
                nc.scalar.activation(wdT[:, :], r_ps[0:NE, :], ACT.Copy).then_inc(steps, 1)
                shared_hT(blk, 1)
                shared_silu(blk, 3)
                shared_hT(blk, 2)
                act.wait_ge(steps, prep.after("group_shifted", blk))
                nc.scalar.activation(fe[:, :, :, :], fm[:, :, :, :], ACT.Exp).then_inc(steps, 1)
                shared_hT(blk, 3)
                act.wait_ge(steps, prep.after("softT_psum", blk))
                nc.scalar.activation(softT[:, :], r_ps[0:NE, :], ACT.Copy).then_inc(steps, 1)
                run_units(act, blk, step)

            blocks(act, start, body, lambda blk: closing(blk, range(BT)))

        @block.sync
        def _(sp):
            if last_layer:
                out = c.dram["out"].rearrange("(n p) d -> p n d", p=P)
                for b in range(NB):
                    sp.wait_ge(added, b + 1)
                    sp.dma_start(out[:, b * BT:(b + 1) * BT, :], c.x[:, b * BT:(b + 1) * BT, :]).then_inc(stored, 16)
                sp.wait_ge(stored, NB * 16)



def softmax_attention(nc, c, ready=False):
    VC = 32
    UNITS = [(t, h) for t in range(BT) for h in range(HG)]
    NU = len(UNITS)
    NPB, NSB = 3, 3
    STACK_AT, SCORE_STEPS, NEG_AT, OUT_AT = [7, 12], 12, 14, 3
    STACK_FIRST = [4, 11]
    ROOT_AT, NORM_AT = 5, 9
    READ_Q_AT = [7, 8, 9, 10]
    READ_K_AT, NORMALISE_AT = 15, 6
    with ExitStack() as ctx:
        def sb(name, shape, dt=F32):
            return ctx.enter_context(nc.sbuf_tensor("b_" + name, shape, dt))

        def psum(name):
            return ctx.enter_context(nc.psum_tensor("b_ps_" + name, [P, 512], F32))

        def sem(name):
            return ctx.enter_context(nc.semaphore("b_" + name))

        w, wo = sb("w_qkv", [P, KD, 3 * D]), sb("w_out", [P, KD, D])
        bias, bias_o = sb("bias_qkv", [P, 3 * D]), sb("bias_out", [P, D])
        cos, sin = sb("cos", [P, BT, 2, BD]), sb("sin", [P, BT, 2, BD])
        maskf = sb("masks_f32", [P, 2, P])
        maskb, identb = sb("masks", [P, 2, P], BF16), sb("ident_bf16", [P, P], BF16)
        identr = sb("ident_f32r", [P, P], F32R)
        qkr = sb("qk_roped", [P, BT, 2, D])
        v = sb("v", [P, BT, D])
        stk = sb("stack_tokens", [P, 2, 2, BT, HG, 4, BD], F32R)
        vv = sb("v_ones", [P, 2, BT, HG, VC])
        ks, qn = sb("k_stack", [P, 2, S], F32R), sb("q_stack_neg", [P, 2, S], F32R)
        qz, kz = sb("q_stack_one", [P, 2, HG, S], F32R), sb("k_stack_one", [P, 2, HG, S], F32R)
        own = sb("own_rows", [P, 2, HG])
        nmax = sb("neg_max", [P, BT, HG])
        ex = sb("exp", [P, 2, HG, S])
        spare = ex[:, :, :, :].rearrange("p a h s -> p (a h s)")
        qk, t1, t2 = (spare[:, j * 4 * D:(j + 1) * 4 * D].rearrange("p (r s d) -> p r s d", r=2, s=2)
                      for j in range(3))
        oT = spare[:, 12 * D:16 * D].rearrange("p (t k n) -> p t k n", t=BT, k=KD)
        oS = sb("outT", [P, S])
        rrec, on = sb("row_rec", [P, BT, HG, 1]), sb("out_normalised", [P, BT, D])
        s_ps, p_ps = [psum(f"scores{i}") for i in range(NSB)], [psum(f"by_keys{i}") for i in range(NPB)]
        o_ps, t_ps = psum("out"), psum("transposed")

        w_loaded, out_loaded = sem("w_loaded"), sem("out_loaded")
        ln, loaded, consts, zeroed = sem("ln_steps"), sem("loaded"), sem("consts"), sem("zeroed")
        qkv_ps, biased, vread = sem("qkv_psum"), sem("biased"), sem("v_read")
        rope_a, rope_done = sem("rope_parts"), sem("rope_done")
        v_placed = sem("v_placed")
        hi_done, stacked, stack_ps, q_stacked, k_stacked = [sem(name) for name in (
            "high", "stacked", "stack_psum", "q_stacked", "k_stacked")]
        k_masked = sem("k_masked")
        scored, maxed, halved_hi, halved = sem("scored"), sem("maxed"), sem("max_high"), sem("max_halves")
        neg_psum, neg_done = sem("neg_psum"), sem("neg_done")
        by_keys, exped, weighted = sem("by_keys"), sem("exped"), sem("weighted")
        o_read, oT_ps, rec, normed = sem("out_read"), sem("outT_psum"), sem("rec"), sem("normed")
        f_ps, f_done, y_done = sem("feat_psum"), sem("feat"), sem("y_psum")
        biased_o, added = sem("y_bias"), sem("added")

        block = ctx.enter_context(nc.Block())

        def groups(engine, slot, b):
            slot(b, 0, 0)
            with engine.Fori(0, NHG // 2 - 2) as t:
                for p in range(2):
                    slot(b, 2 * t + p + 1, 1 - p)
            for g in range(NHG - 3, NHG - 1):
                slot(b, g, g % 2)
            slot(b, NHG - 1, (NHG - 1) % 2, norm=True)

        def blocks(engine, first, body, final):
            first()
            body(0, True, False)
            with engine.Fori(1, NB - 1) as b:
                body(b, False, False)
            body(NB - 1, False, True)
            final()

        def at(g, n):
            return isinstance(g, int) and g == n

        def k_bank(g):
            return p_ps[1] if at(g, 0) or at(g, 1) else t_ps

        def split(compute, engine, b, g, par):
            G = b * NHG + g
            if not (isinstance(g, int) and g < 2):
                engine.wait_ge(neg_psum, G - 1)
            if at(g, 1):
                engine.wait_ge(stacked, G)
            apart(engine, c)
            highs, low = [(0, 1), (0, 2)], [2, 1]
            srcs = [qkr[:, :, s, ds(g * HG * BD, HG * BD)].rearrange("p t (h d) -> p t h d", h=HG)
                    for s in range(2)]
            for s in range(2):
                for a in highs[s]:
                    last = compute.tensor_copy(stk[:, par, s, :, :, a, :], srcs[s])
            last.then_inc(hi_done, 1)
            engine.wait_ge(hi_done, G + 1)
            apart(engine, c)
            for s in range(2):
                last = compute.tensor_tensor(stk[:, par, s, :, :, low[s], :], srcs[s],
                                             stk[:, par, s, :, :, 0, :].bitcast(F32), ALU.subtract)
            last.then_inc(stacked, 1)

        @block.sync
        def _(sp):
            sp.dma_start(w[:, :, :], c.dram["b_w"].rearrange("(k p) n -> p k n", p=P)).then_inc(w_loaded, 16)
            sp.dma_start(bias[:, :], c.dram["b_bias"].partition_broadcast(P)).then_inc(loaded, 16)
            sp.dma_start(cos[:, :, :, :].rearrange("p t a d -> p (t a d)"), c.dram["b_cos"]).then_inc(loaded, 16)
            sp.dma_start(sin[:, :, :, :].rearrange("p t a d -> p (t a d)"), c.dram["b_sin"]).then_inc(loaded, 16)
            sp.dma_start(own[:, :, :].rearrange("p s h -> p (s h)"), c.dram["b_own"]).then_inc(loaded, 16)
            sp.dma_start(maskf[:, :, :].rearrange("p a n -> p (a n)"), c.dram["b_mask"]).then_inc(loaded, 16)
            sp.dma_start(bias_o[:, :], c.dram["b_bias_o"].partition_broadcast(P)).then_inc(out_loaded, 16)
            sp.dma_start(wo[:, :, :], c.dram["b_wo"].rearrange("(k p) n -> p k n", p=P)).then_inc(out_loaded, 16)

        @block.tensor
        def _(pe):
            def stack(b, g, par, s):
                G = b * NHG + g
                bank = k_bank(g) if s == 1 else t_ps
                if s == 0:
                    pe.wait_ge(stacked, G + 1)
                if at(g, 0) or at(g, 1):
                    if at(g, 1):
                        pe.wait_ge((q_stacked, k_stacked)[s], G)
                elif s == 0:
                    if not at(g, 2):
                        pe.wait_ge(normed, G - 2)
                else:
                    pe.wait_ge(q_stacked, G + 1)
                for i in range(BT):
                    last = nc.tensor.matmul(bank[:, i * P:(i + 1) * P].bitcast(F32R),
                                            stk[:, par, s, i, :, :, :].rearrange("p h a d -> p (h a d)"),
                                            identr[:, :], is_transpose=True, start=True, stop=True)
                last.then_inc(stack_ps, 1)

            def score(b, g, par, u):
                G = b * NHG + g
                qi, h = UNITS[u]
                N = (qi + 1) * P
                if u == 0:
                    pe.wait_ge(q_stacked, G + 1)
                    pe.wait_ge(k_stacked, G + 1)
                if not (isinstance(g, int) and g == 0 and u < NSB):
                    pe.wait_ge(maxed, G * NU + u - NSB + 1)
                nc.tensor.matmul(s_ps[u % NSB][:, 0:N], qz[:, par, h, qi * P:(qi + 1) * P],
                                 ks[:, par, 0:N], start=True, stop=False, skip_group_check=True)
                nc.tensor.matmul(s_ps[u % NSB][:, qi * P:N], identb[:, :], maskb[:, 0, :], start=False, stop=True,
                                 skip_group_check=True).then_inc(scored, 1)

            def neg(b, g, par):
                G = b * NHG + g
                pe.wait_ge(halved, G + 1)
                if at(g, 0):
                    pe.wait_ge(q_stacked, G + 2)
                elif at(g, NHG - 1):
                    pe.wait_ge(normed, G - 1)
                else:
                    pe.wait_ge(k_stacked, G + 2)
                for i in range(BT):
                    last = nc.tensor.matmul(t_ps[:, i * P:(i + 1) * P].bitcast(F32R),
                                            stk[:, par, 0, i, :, :, :].rearrange("p h a d -> p (h a d)"), identr[:, :],
                                            is_transpose=True, start=True, stop=True)
                last.then_inc(neg_psum, 1)

            def keys(b, g, par, u):
                G = b * NHG + g
                kj, h = UNITS[u]
                N = S - kj * P
                bank = p_ps[u % NPB]
                if u == 0:
                    pe.wait_ge(k_masked, G + 1)
                    pe.wait_ge(neg_done, G + 1)
                if u < NPB:
                    if not (isinstance(g, int) and g == 0):
                        pe.wait_ge(exped, G * NU)
                else:
                    pe.wait_ge(exped, G * NU + u - NPB + 1)
                nc.tensor.matmul(bank[:, 0:N], kz[:, par, h, kj * P:(kj + 1) * P], qn[:, par, kj * P:S],
                                 start=True, stop=False, skip_group_check=True)
                nc.tensor.matmul(bank[:, 0:P], identb[:, :], maskb[:, 1, :], start=False, stop=True,
                                 skip_group_check=True).then_inc(by_keys, 1)

            def weigh(b, g, par, kj):
                G = b * NHG + g
                pe.wait_ge(exped, G * NU + (kj + 1) * HG)
                if kj == 0:
                    pe.wait_ge(v_placed, G + 1)
                if kj == 0 and not (isinstance(g, int) and g == 0):
                    pe.wait_ge(o_read, G)
                for h in range(HG):
                    last = nc.tensor.matmul(o_ps[h * 32:(h + 1) * 32, kj * P:S], vv[:, par, kj, h, :],
                                            ex[:, kj % 2, h, 0:S - kj * P], start=(kj == 0), stop=(kj == BT - 1),
                                            skip_group_check=True)
                last.then_inc(weighted, 1)

            def out_tokens(b, g):
                G = b * NHG + g
                pe.wait_ge(o_read, G + 1)
                if isinstance(g, int) and g == NHG - 1:
                    pe.wait_ge(normed, G)
                else:
                    pe.wait_ge(neg_done, G + 2)
                for i in range(BT):
                    last = nc.tensor.transpose(t_ps[:, i * P:(i + 1) * P], oS[:, i * P:(i + 1) * P], c.ident[:, :])
                last.then_inc(oT_ps, 1)

            def slot(b, g, par, norm=False):
                first, last = at(g, 0), at(g, NHG - 1)
                for u in range(NU):
                    keys(b, g, par, u)
                    if u == OUT_AT and not first:
                        out_tokens(b, g - 1)
                    if not last:
                        for a in range(-(-NU * u // SCORE_STEPS), min(NU, -(-NU * (u + 1) // SCORE_STEPS))):
                            score(b, g + 1, 1 - par, a)
                    if not last and not at(g, NHG - 2) and u in STACK_AT:
                        stack(b, g + 2, par, STACK_AT.index(u))
                    if u % HG == HG - 1 and u > HG:
                        weigh(b, g, par, u // HG - 1)
                    if u == NEG_AT and not last:
                        neg(b, g + 1, 1 - par)
                    if u == NORM_AT and norm:
                        ln_tensor(nc, c, pe, ln, b + 1, s_ps)
                weigh(b, g, par, BT - 1)

            def qkv(b, i):
                if i == 0:
                    pe.wait_ge(ln, LN.after("xT", b))
                if i >= 2:
                    pe.wait_ge(biased, b * BT + i - 1)
                v_bank = (s_ps[2], p_ps[2])[i // 2]
                for k in range(KD):
                    nc.tensor.matmul(p_ps[i % 2][:, :], c.xT[:, k, i * P:(i + 1) * P], w[:, k, 0:2 * D],
                                     start=(k == 0), stop=(k == KD - 1))
                for k in range(KD):
                    last = nc.tensor.matmul(v_bank[:, (i % 2) * D:(i % 2 + 1) * D], c.xT[:, k, i * P:(i + 1) * P],
                                            w[:, k, 2 * D:3 * D], start=(k == 0), stop=(k == KD - 1))
                last.then_inc(qkv_ps, 1)

            def features(b, i):
                if i == 0:
                    pe.wait_ge(normed, (b + 1) * NHG)
                if i >= 2:
                    pe.wait_ge(f_done, b * BT + i - 1)
                for k in range(KD):
                    last = nc.tensor.transpose(s_ps[i % 2][:, k * P:(k + 1) * P], on[:, i, k * P:(k + 1) * P],
                                               c.ident[:, :])
                last.then_inc(f_ps, 1)

            def project_out(b, i):
                pe.wait_ge(f_done, b * BT + i + 1)
                if i >= 2:
                    pe.wait_ge(added, b * BT + i - 1)
                for k in range(KD):
                    last = nc.tensor.matmul((o_ps, t_ps)[i % 2][:, 0:D], oT[:, i, k, :], wo[:, k, :],
                                            start=(k == 0), stop=(k == KD - 1))
                last.then_inc(y_done, 1)

            def first():
                if not ready:
                    ln_tensor(nc, c, pe, ln, 0, s_ps)
                pe.wait_ge(w_loaded, 16)

            def body(b, first, last):
                qkv(b, 0)
                qkv(b, 1)
                if not first:
                    features(b - 1, 0)
                    features(b - 1, 1)
                qkv(b, 2)
                if not first:
                    project_out(b - 1, 0)
                    features(b - 1, 2)
                    project_out(b - 1, 1)
                    features(b - 1, 3)
                qkv(b, 3)
                if not first:
                    project_out(b - 1, 2)
                    project_out(b - 1, 3)
                if first:
                    pe.wait_ge(consts, 3)
                    pe.wait_ge(out_loaded, 32)
                if not first:
                    pe.wait_ge(added, b * BT)
                stack(b, 0, 0, 0)
                stack(b, 0, 0, 1)
                pe.wait_ge(vread, 2 * b + 2)
                for u in range(NU):
                    score(b, 0, 0, u)
                    if u in STACK_FIRST:
                        stack(b, 1, 1, STACK_FIRST.index(u))
                neg(b, 0, 0)
                pe.wait_ge(k_stacked, b * NHG + 2)
                groups(pe, slot, b)
                out_tokens(b, NHG - 1)

            def final():
                b = NB - 1
                features(b, 0)
                features(b, 1)
                for i in range(BT):
                    project_out(b, i)
                    if i + 2 < BT:
                        features(b, i + 2)

            blocks(pe, first, body, final)

        @block.gpsimd
        def _(pool):
            def own_k(b, g, par):
                G = b * NHG + g
                pool.wait_ge(k_stacked, G + 1)
                if not (isinstance(g, int) and g < 2):
                    pool.wait_ge(by_keys, NU * (G - 1))
                apart(pool, c)
                for h in range(HG):
                    last = nc.gpsimd.tensor_scalar(kz[:, par, h, :], ks[:, par, :].bitcast(F32), own[:, 1, h:h + 1],
                                                   None, ALU.mult)
                last.then_inc(k_masked, 1)

            def place_v(b, g, par):
                G = b * NHG + g
                if not (isinstance(g, int) and g < 2):
                    pool.wait_ge(weighted, BT * (G - 1))
                apart(pool, c)
                nc.gpsimd.tensor_copy(vv[:, par, :, :, 0:BD],
                                      v[:, :, ds(g * HG * BD, HG * BD)].rearrange("p t (h d) -> p t h d", h=HG))\
                    .then_inc(v_placed, 1)

            for par in range(2):
                nc.gpsimd.memset(stk[:, par, 0, :, :, 3, :].bitcast(F32), 0.0)
                nc.gpsimd.memset(stk[:, par, 1, :, :, 3, 2:BD].bitcast(F32), 0.0)
                nc.gpsimd.memset(stk[:, par, 1, :, :, 3, 0:2].bitcast(F32), 1.0)
            nc.gpsimd.memset(vv[:, :, :, :, BD + 1:VC], 0.0)
            nc.gpsimd.memset(vv[:, :, :, :, BD:BD + 1], 1.0).then_inc(zeroed, 1)
            def body(b, first, last):
                if first:
                    pool.wait_ge(loaded, 16 * 5)
                    pool.wait_ge(out_loaded, 32)
                pool.wait_ge(ln, LN.after("normalised", b))
                apart(pool, c)
                xs = c.x[:, ds(b * BT, BT), :]
                nc.gpsimd.tensor_tensor(xs, xs, bias_o[:, :].unsqueeze(1).to_broadcast([P, BT, D]), ALU.add)\
                    .then_inc(biased_o, 1)
                for i in range(BT):
                    pool.wait_ge(rope_a, b * BT + i + 1)
                    apart(pool, c)
                    nc.gpsimd.tensor_tensor(qkr[:, i, :, :], t1[:, i % 2, :, :], t2[:, i % 2, :, :], ALU.add)\
                        .then_inc(rope_done, 1)
                split(nc.gpsimd, pool, b, 1, 1)
                own_k(b, 0, 0)
                pool.wait_ge(vread, 2 * b + 2)
                place_v(b, 0, 0)
                place_v(b, 1, 1)
                with pool.Fori(0, NHG // 2 - 1) as t:
                    for p in range(2):
                        split(nc.gpsimd, pool, b, 2 * t + p + 2, p)
                        own_k(b, 2 * t + p + 1, 1 - p)
                        place_v(b, 2 * t + p + 2, p)
                own_k(b, NHG - 1, 1)

            blocks(pool, lambda: None, body, lambda: None)

        @block.vector
        def _(dve):
            def read_k(b, g, par):
                G = b * NHG + g
                dve.wait_ge(stack_ps, 2 * G + 2)
                nc.vector.tensor_copy(ks[:, par, :], k_bank(g)[:, :]).then_inc(k_stacked, 1)

            def maxima(b, g, par):
                G = b * NHG + g
                for u in range(NU):
                    qi, h = UNITS[u]
                    n = G * NU + u
                    if u == 0 and not (isinstance(g, int) and g == 0):
                        dve.wait_ge(halved, G)
                    dve.wait_ge(scored, n + 1)
                    nc.vector.reduce_max(nmax[:, qi, h:h + 1], s_ps[u % NSB][:, 0:(qi + 1) * P], AX, negate=True)\
                        .then_inc(maxed, 1)
                    if at(g, 0) and u == STACK_FIRST[1]:
                        read_k(b, 1, 1)
                    if u == READ_K_AT and not at(g, 0) and not at(g, NHG - 1):
                        read_k(b, g + 1, 1 - par)
                    if u == NORMALISE_AT and not at(g, 0) and not at(g, 1):
                        normalise(b, g - 2)
                dve.wait_ge(maxed, (G + 1) * NU)
                top = stk[:, par, 0, :, :, 3, 0]
                nc.vector.tensor_copy(top, nmax[:, :, :]).then_inc(halved_hi, 1)
                dve.wait_ge(halved_hi, G + 1)
                nc.vector.tensor_tensor(stk[:, par, 0, :, :, 3, 1], nmax[:, :, :], top.bitcast(F32), ALU.subtract)\
                    .then_inc(halved, 1)

            def normalise(b, g):
                G = b * NHG + g
                dve.wait_ge(oT_ps, G + 1)
                o4 = t_ps[:, :].rearrange("p (t h d) -> p t h d", t=BT, h=HG)
                nc.vector.reciprocal(rrec[:, :, :, :], o4[:, :, :, BD:BD + 1]).then_inc(rec, 1)
                dve.wait_ge(rec, G + 1)
                dst = on[:, :, ds(g * HG * BD, HG * BD)].rearrange("p t (h d) -> p t h d", h=HG)
                nc.vector.tensor_tensor(dst, o4[:, :, :, 0:BD], rrec[:, :, :, :].to_broadcast([P, BT, HG, BD]),
                                        ALU.mult).then_inc(normed, 1)

            def slot(b, g, par, norm=False):
                if at(g, NHG - 1):
                    normalise(b, g - 1)
                    if norm:
                        if isinstance(b, int) and b == NB - 1:
                            dve.wait_ge(added, BT)
                        ln_vector(nc, c, dve, ln, block_of(b + 1), b + 1)
                else:
                    maxima(b, g + 1, 1 - par)

            H2 = BD // 2
            full, half = [P, BH, BD], [P, BH, H2]

            def rope(b, i):
                n = b * BT + i
                r = i % 2
                if i >= 2:
                    dve.wait_ge(rope_done, n - 1)
                dve.wait_ge(qkv_ps, n + 1)
                nc.vector.tensor_tensor(qk[:, r, :, :].rearrange("p a d -> p (a d)"), p_ps[r][:, :],
                                        bias[:, 0:2 * D], ALU.add).then_inc(biased, 1)
                dve.wait_ge(biased, n + 1)
                for s in range(2):
                    q4 = qk[:, r, s, :].rearrange("p (h d) -> p h d", d=BD)
                    a4, b4 = (t[:, r, s, :].rearrange("p (h d) -> p h d", d=BD) for t in (t1, t2))
                    nc.vector.tensor_tensor(a4, q4, cos[:, i, s, :].unsqueeze(1).to_broadcast(full), ALU.mult)
                    nc.vector.tensor_tensor(b4[:, :, 0:H2], q4[:, :, H2:BD],
                                            sin[:, i, s, 0:H2].unsqueeze(1).to_broadcast(half), ALU.mult)
                    last = nc.vector.tensor_tensor(b4[:, :, H2:BD], q4[:, :, 0:H2],
                                                   sin[:, i, s, H2:BD].unsqueeze(1).to_broadcast(half), ALU.mult)
                last.then_inc(rope_a, 1)

            def bias_v(b, j):
                dve.wait_ge(qkv_ps, b * BT + 2 * j + 2)
                nc.vector.tensor_tensor(v[:, 2 * j:2 * j + 2, :], (s_ps[2], p_ps[2])[j][:, :].rearrange(
                    "p (t d) -> p t d", t=2), bias[:, 2 * D:].unsqueeze(1).to_broadcast([P, 2, D]), ALU.add)\
                    .then_inc(vread, 1)

            def residual(b, i):
                n = b * BT + i
                if i == 0:
                    dve.wait_ge(biased_o, b + 1)
                dve.wait_ge(y_done, n + 1)
                xs = c.x[:, ds(n, 1), :].rearrange("p a d -> p (a d)")
                nc.vector.tensor_tensor(xs, xs, (o_ps, t_ps)[i % 2][:, 0:D], ALU.add).then_inc(added, 1)

            def first():
                if not ready:
                    ln_vector(nc, c, dve, ln, 0, 0)
                else:
                    dve.sem_inc(ln, len(LN_STEPS))
                dve.wait_ge(loaded, 16 * 5)
                nc.vector.tensor_copy(maskb[:, :, :], maskf[:, :, :]).then_inc(consts, 1)
                nc.vector.tensor_copy(identb[:, :], c.ident[:, :]).then_inc(consts, 1)
                nc.vector.tensor_copy(identr[:, :], c.ident[:, :]).then_inc(consts, 1)
                dve.wait_ge(zeroed, 1)

            def body(b, first, last):
                rope(b, 0)
                rope(b, 1)
                bias_v(b, 0)
                if not first:
                    residual(b - 1, 0)
                rope(b, 2)
                if not first:
                    residual(b - 1, 1)
                rope(b, 3)
                if not first:
                    residual(b - 1, 2)
                    residual(b - 1, 3)
                bias_v(b, 1)
                dve.wait_ge(rope_done, (b + 1) * BT)
                split(nc.vector, dve, b, 0, 0)
                read_k(b, 0, 0)
                maxima(b, 0, 0)
                groups(dve, slot, b)
                normalise(b, NHG - 1)

            def final():
                for i in range(BT):
                    residual(NB - 1, i)
                dve.wait_ge(added, NB * BT)

            blocks(dve, first, body, final)

        @block.scalar
        def _(act):
            def read_q(b, g, par, h):
                if h == 0:
                    act.wait_ge(stack_ps, 2 * (b * NHG + g) + 1)
                last = nc.scalar.activation(qz[:, par, h, :], t_ps[:, :], ACT.Copy, scale=own[:, 0, h:h + 1])
                if h == HG - 1:
                    last.then_inc(q_stacked, 1)

            def read_neg(b, g, par):
                act.wait_ge(neg_psum, b * NHG + g + 1)
                nc.scalar.activation(qn[:, par, :], t_ps[:, :], ACT.Copy).then_inc(neg_done, 1)

            def read_out(b, g):
                G = b * NHG + g
                act.wait_ge(weighted, BT * (G + 1))
                if not (isinstance(g, int) and g == 0):
                    act.wait_ge(oT_ps, G)
                nc.scalar.activation(oS[:, :], o_ps[:, :], ACT.Copy).then_inc(o_read, 1)

            def slot(b, g, par, norm=False):
                G = b * NHG + g
                last = at(g, NHG - 1)
                for u in range(NU):
                    kj, h = UNITS[u]
                    act.wait_ge(by_keys, G * NU + u + 1)
                    if kj >= 2 and h == 0:
                        act.wait_ge(weighted, BT * G + kj - 1)
                    nc.scalar.activation(ex[:, kj % 2, h, 0:S - kj * P], p_ps[u % NPB][:, 0:S - kj * P], ACT.Exp)\
                        .then_inc(exped, 1)
                    if u in READ_Q_AT and not last and not at(g, NHG - 2):
                        read_q(b, g + 2, par, READ_Q_AT.index(u))
                    if u == NEG_AT and not last:
                        read_neg(b, g + 1, 1 - par)
                    if u == ROOT_AT and norm:
                        ln_scalar_root(nc, c, act, ln, b + 1)
                    if u == NORM_AT + 1 and norm:
                        ln_scalar_read(nc, c, act, ln, b + 1, s_ps)
                read_out(b, g)

            def features(b):
                for i in range(BT):
                    act.wait_ge(f_ps, b * BT + i + 1)
                    nc.scalar.activation(oT[:, i, :, :].rearrange("p k t -> p (k t)"), s_ps[i % 2][:, 0:D], ACT.Copy)\
                        .then_inc(f_done, 1)

            def first():
                if not ready:
                    ln_scalar(nc, c, act, ln, 0, s_ps)
                act.wait_ge(loaded, 16 * 5)

            def body(b, first, last):
                if not first:
                    features(b - 1)
                for g in range(2):
                    for h in range(HG):
                        read_q(b, g, g, h)
                read_neg(b, 0, 0)
                groups(act, slot, b)

            blocks(act, first, body, lambda: features(NB - 1))


def build(nc, dram):
    with ExitStack() as ctx:
        c = Chip()
        resident(nc, ctx, c, dram)
        linear_attention(nc, c)
        expert_weights(nc, c)
        experts(nc, c, "f0_", False, ready=True)
        softmax_attention(nc, c, ready=True)
        experts(nc, c, "f1_", True, ready=True)


def _layouts(np, a):
    f4 = np.float32

    def t(x):
        return np.ascontiguousarray(np.asarray(x).T)

    get = {k: np.asarray(v) for k, v in a.items()}
    d = {"x": get["L0_attn_a_x"].reshape(NB * S, D)}
    wq, wk, wv = (t(get["L0_attn_a_W" + n]).reshape(D, AG, -1) for n in "qkv")
    d["a_w"] = np.concatenate([wv, wk, wq], axis=2).reshape(D, -1)
    d["a_wo"] = t(get["L0_attn_a_Wo"])
    d["b_w"] = np.concatenate([t(get["L0_attn_b_W" + n]) for n in "qkv"], axis=1)
    d["b_wo"] = t(get["L0_attn_b_Wo"])
    d["b_bias"] = np.concatenate([get["L0_attn_b_b" + n] for n in "qkv"])
    d["b_bias_o"] = get["L0_attn_b_bo"]
    f = {k[7:]: v for k, v in get.items() if k.startswith("L0_ffn_")}
    d["wrt"] = t(f["gate_weight"])
    d["mapping"] = f["inv_mapping"].reshape(NE)
    w1 = np.concatenate([f["gate_W"], f["up_W"], f["gate_qa"].reshape(EX, KR, D), f["up_qa"].reshape(EX, KR, D)],
                        axis=1)
    d["w1"] = np.ascontiguousarray(w1.transpose(2, 0, 1).reshape(D, EX * W1N))
    w2 = np.concatenate([f["down_W"].transpose(0, 2, 1), f["down_qa"].reshape(EX, KR, EI).transpose(0, 2, 1)], axis=2)
    d["w2"] = np.ascontiguousarray(w2.transpose(1, 0, 2).reshape(EI, EX * W2N))
    qb = [f[n].transpose(0, 1, 3, 2).reshape(EX, KR, EI) for n in ("gate_qb", "up_qb")]
    d["qb"] = np.ascontiguousarray(np.concatenate(qb, axis=2).transpose(1, 0, 2).reshape(KR, EX * 2 * EI))
    d["scale_gu"] = np.concatenate([f["gate_scale"], f["up_scale"]], axis=1).reshape(EX * 2 * EI)
    d["qbd"] = np.ascontiguousarray(f["down_qb"].transpose(0, 1, 3, 2).reshape(EX * KR, D))
    d["scale_d"] = f["down_scale"]
    d["mu"] = np.ascontiguousarray(f["mask_up_W"].transpose(1, 0, 2).reshape(D, NE))
    mup = np.zeros((D, EX, NE), f["mask_up_W"].dtype)
    for e in range(EX):
        mup[:, e, e * EK:(e + 1) * EK] = f["mask_up_W"][e]
    d["mup"] = mup.reshape(D, EX * NE)
    d["shgu"] = np.concatenate([t(f["sh_gate_W"]), t(f["sh_up_W"])], axis=1)
    d["shd"] = t(f["sh_down_W"])
    d["ident"] = np.eye(P, dtype=f4)
    d["row"] = np.arange(NE, dtype=f4).reshape(NE, 1)
    pos = np.arange(P)
    d["a_mask"] = (pos[:, None] <= pos[None, :]).astype(f4)
    by_query = np.where(pos[:, None] >= pos[None, :], 0.0, NEG).astype(f4)
    d["b_mask"] = np.concatenate([by_query, by_query.T], axis=1)
    head = pos[:, None] // 32 == np.arange(HG)[None, :]
    d["b_own"] = np.concatenate([head & (pos[:, None] % 32 < 3 * BD), head], axis=1).astype(f4)
    inv = (f4(1.0) / f4(10000.0) ** (np.arange(0, HD, 2, dtype=f4) / f4(HD))).astype(f4)
    ang = np.outer(np.arange(S, dtype=f4), inv).astype(f4).T
    d["a_cos"] = np.concatenate([np.cos(ang), np.cos(ang)]).astype(f4)
    d["a_sin"] = np.concatenate([np.sin(ang), -np.sin(ang)]).astype(f4)
    theta = (f4(10000.0) ** (-np.arange(0, BD, 2, dtype=f4) / f4(BD))).astype(f4)
    frame = np.floor((np.arange(S) // 72).astype(f4) * 0.5)
    ang = (np.arange(S, dtype=f4)[:, None] * theta).astype(np.float64) + (frame.astype(f4)[:, None] * theta)
    co, si = np.cos(ang), np.sin(ang)
    for name, tab in (("b_cos", np.concatenate([co, co], 1)), ("b_sin", np.concatenate([-si, si], 1))):
        both = np.stack([tab / np.sqrt(BD), tab], axis=1).astype(f4)
        d[name] = np.ascontiguousarray(both.reshape(BT, P, 2 * BD).transpose(1, 0, 2).reshape(P, BT * 2 * BD))
    return d


def kernel(**inputs):
    import numpy as np
    import concourse.bacc as bacc
    from concourse.bass_utils import run_bass_kernel_spmd

    nc = bacc.Bacc("TRN2", target_bir_lowering=False, num_devices=1)
    arrays, dram = {}, {}
    for name, a in _layouts(np, inputs).items():
        arrays[f"in_{name}"] = np.ascontiguousarray(a)
        dram[name] = nc.dram_tensor(f"in_{name}", a.shape, mybir.dt.from_np(a.dtype), kind="ExternalInput").ap()
    dram["out"] = nc.dram_tensor("out_0", (NB * S, D), F32, kind="ExternalOutput").ap()
    build(nc, dram)
    r = run_bass_kernel_spmd(nc, [arrays], core_ids=[0])
    return r.results[0]["out_0"].reshape(NB, S, D)
```
